# Optimizing a Trainium2 kernel written in Bass

```python
import numpy as np
import jax
import jax.numpy as jnp

def _softmax(x, axis=-1):
    return jax.nn.softmax(x, axis=axis)

def _gelu(x):
    return jax.nn.gelu(x, approximate=True)

def _silu(x):
    return jax.nn.silu(x)

def _sigmoid(x):
    return jax.nn.sigmoid(x)

def _layernorm(x, axis=-1, eps=1e-05):
    m = jnp.mean(x, axis=axis, keepdims=True)
    v = jnp.var(x, axis=axis, keepdims=True)
    return (x - m) / jnp.sqrt(v + eps)

def _scatter_add(tgt, idx, src, axis=0):
    return tgt.at[idx].add(src)

def _segment_sum(src, seg, n):
    return jax.ops.segment_sum(src, seg, n)
kernel_name = 'mk_seq_preln_d1_jaxref_r4_4bebd8'

def setup_inputs(seed: int=0):
    np.random.seed(seed)
    _w = jnp.asarray

    def _L0_attn_setup():
        import jax, jax.numpy as jnp
        import numpy as np
        B, T, D, C = (8, 512, 256, 128)
        key = jax.random.key(seed)
        ks = jax.random.split(key, 16)
        s = 1.0 / np.sqrt(D)
        so = 1.0 / np.sqrt(C)
        return {'x': jax.random.normal(ks[0], (B, T, D), jnp.float32), 'Wq': jax.random.normal(ks[1], (D, C), jnp.float32) * s, 'bq': jax.random.normal(ks[2], (C,), jnp.float32) * 0.01, 'Wk': jax.random.normal(ks[3], (D, C), jnp.float32) * s, 'bk': jax.random.normal(ks[4], (C,), jnp.float32) * 0.01, 'Wv': jax.random.normal(ks[5], (D, C), jnp.float32) * s, 'bv': jax.random.normal(ks[6], (C,), jnp.float32) * 0.01, 'Wa': jax.random.normal(ks[7], (D, 1), jnp.float32) * s, 'ba': jax.random.normal(ks[8], (1,), jnp.float32) * 0.01, 'Wb': jax.random.normal(ks[9], (D, 1), jnp.float32) * s, 'bb': jax.random.normal(ks[10], (1,), jnp.float32) * 0.01, 'Wg': jax.random.normal(ks[11], (D, C), jnp.float32) * s, 'bg': jax.random.normal(ks[12], (C,), jnp.float32) * 0.01, 'Wo': jax.random.normal(ks[13], (C, D), jnp.float32) * so, 'bo': jax.random.normal(ks[14], (D,), jnp.float32) * 0.01}
    _L0_attn_in = _L0_attn_setup()

    def _L0_ffn_setup():
        import jax, jax.numpy as jnp
        import numpy as np
        EPS = 1e-12

        def rms_norm(t, gamma):
            n = jnp.maximum(jnp.linalg.norm(t, axis=-1, keepdims=True), EPS)
            scale = jnp.sqrt(jnp.asarray(t.shape[-1], t.dtype))
            return t / n * scale * gamma
        key = jax.random.key(seed)
        ks = jax.random.split(key, 4)
        b, s, d = (4, 1024, 256)
        e, t = (8, 128)
        hidden = 4 * d
        return {'x': jax.random.normal(ks[0], (b, s, d), dtype=jnp.float32), 'gamma_x': jnp.ones((d,), dtype=jnp.float32), 'gamma_slot': jnp.ones((d,), dtype=jnp.float32), 'slot_embeds': jax.random.normal(ks[1], (e, t, d), dtype=jnp.float32), 'w1': jax.random.normal(ks[2], (d, hidden), dtype=jnp.float32) * (1.0 / np.sqrt(d)), 'w2': jax.random.normal(ks[3], (hidden, d), dtype=jnp.float32) * (1.0 / np.sqrt(hidden))}
    _L0_ffn_in = _L0_ffn_setup()
    _d = {'L0_attn_x': _L0_attn_in['x'], 'L0_attn_Wq': _L0_attn_in['Wq'], 'L0_attn_bq': _L0_attn_in['bq'], 'L0_attn_Wk': _L0_attn_in['Wk'], 'L0_attn_bk': _L0_attn_in['bk'], 'L0_attn_Wv': _L0_attn_in['Wv'], 'L0_attn_bv': _L0_attn_in['bv'], 'L0_attn_Wa': _L0_attn_in['Wa'], 'L0_attn_ba': _L0_attn_in['ba'], 'L0_attn_Wb': _L0_attn_in['Wb'], 'L0_attn_bb': _L0_attn_in['bb'], 'L0_attn_Wg': _L0_attn_in['Wg'], 'L0_attn_bg': _L0_attn_in['bg'], 'L0_attn_Wo': _L0_attn_in['Wo'], 'L0_attn_bo': _L0_attn_in['bo'], 'L0_ffn_gamma_x': _L0_ffn_in['gamma_x'], 'L0_ffn_gamma_slot': _L0_ffn_in['gamma_slot'], 'L0_ffn_slot_embeds': _L0_ffn_in['slot_embeds'], 'L0_ffn_w1': _L0_ffn_in['w1'], 'L0_ffn_w2': _L0_ffn_in['w2']}
    _x0 = _d['L0_attn_x']
    _d['L0_attn_x'] = jax.random.normal(jax.random.fold_in(jax.random.key(seed), 1), (4, 2048, 256), dtype=_x0.dtype)
    del _x0
    return _d

def reference(L0_attn_x, L0_attn_Wq, L0_attn_bq, L0_attn_Wk, L0_attn_bk, L0_attn_Wv, L0_attn_bv, L0_attn_Wa, L0_attn_ba, L0_attn_Wb, L0_attn_bb, L0_attn_Wg, L0_attn_bg, L0_attn_Wo, L0_attn_bo, L0_ffn_gamma_x, L0_ffn_gamma_slot, L0_ffn_slot_embeds, L0_ffn_w1, L0_ffn_w2):

    def _L0_attn_ref(x, Wq, bq, Wk, bk, Wv, bv, Wa, ba, Wb, bb, Wg, bg, Wo, bo):
        import jax, jax.numpy as jnp
        import numpy as np
        B, T, D, C = (8, 512, 256, 128)
        Bn = x.shape[0]
        Cn = Wq.shape[1]
        q = x @ Wq + bq
        k = x @ Wk + bk
        v = x @ Wv + bv
        k = k / jnp.maximum(jnp.linalg.norm(k, axis=-1, keepdims=True), 1e-12)
        alpha = jax.nn.sigmoid(x @ Wa + ba)
        beta = jax.nn.sigmoid(x @ Wb + bb)
        gate = jax.nn.sigmoid(x @ Wg + bg)
        I = jnp.eye(Cn, dtype=x.dtype)

        def step(S, ins):
            q_t, k_t, v_t, a_t, b_t, g_t = ins
            kkT = k_t[:, :, None] * k_t[:, None, :]
            trans = a_t[:, :, None] * (I - b_t[:, :, None] * kkT)
            vkT = v_t[:, :, None] * k_t[:, None, :]
            S = jnp.einsum('bij,bjk->bik', S, trans) + b_t[:, :, None] * vkT
            o = jnp.einsum('bc,bcd->bd', q_t, S) * g_t
            return (S, o)
        tfirst = lambda a: jnp.swapaxes(a, 0, 1)
        S0 = jnp.zeros((Bn, Cn, Cn), x.dtype)
        _, o = jax.lax.scan(step, S0, (tfirst(q), tfirst(k), tfirst(v), tfirst(alpha), tfirst(beta), tfirst(gate)))
        y = jnp.swapaxes(o, 0, 1) @ Wo + bo
        return y

    def _L0_ffn_ref(x, gamma_x, gamma_slot, slot_embeds, w1, w2):
        import jax, jax.numpy as jnp
        import numpy as np
        EPS = 1e-12

        def rms_norm(t, gamma):
            n = jnp.maximum(jnp.linalg.norm(t, axis=-1, keepdims=True), EPS)
            scale = jnp.sqrt(jnp.asarray(t.shape[-1], t.dtype))
            return t / n * scale * gamma
        b, s, d = x.shape
        e, t, _ = slot_embeds.shape
        xn = rms_norm(x, gamma_x)
        se = rms_norm(slot_embeds, gamma_slot)
        logits = jnp.einsum('bsd,etd->bset', xn, se)
        dispatch = jax.nn.softmax(logits, axis=1)
        slots = jnp.einsum('bsd,bset->betd', xn, dispatch)
        h = jax.nn.gelu(slots @ w1, approximate=False)
        processed = h @ w2
        combine = jax.nn.softmax(logits.reshape(b, s, e * t), axis=-1)
        out = jnp.einsum('bnd,bsn->bsd', processed.reshape(b, e * t, d), combine)
        return out
    x = L0_attn_x
    x = x + _L0_attn_ref(_layernorm(x, axis=-1), L0_attn_Wq, L0_attn_bq, L0_attn_Wk, L0_attn_bk, L0_attn_Wv, L0_attn_bv, L0_attn_Wa, L0_attn_ba, L0_attn_Wb, L0_attn_bb, L0_attn_Wg, L0_attn_bg, L0_attn_Wo, L0_attn_bo)
    x = x + _L0_ffn_ref(_layernorm(x, axis=-1), L0_ffn_gamma_x, L0_ffn_gamma_slot, L0_ffn_slot_embeds, L0_ffn_w1, L0_ffn_w2)
    return x

_drawn_inputs = setup_inputs


def setup_inputs(seed=0):
    import zlib

    import numpy as np

    out = dict(_drawn_inputs(seed))
    spreads = {'L0_ffn_gamma_x': (1.0, 0.2), 'L0_ffn_gamma_slot': (1.0, 0.2)}
    factors = {'L0_attn_bq': 6.989,
     'L0_attn_bk': 6.917,
     'L0_attn_bv': 6.536,
     'L0_attn_bg': 8.0,
     'L0_attn_bo': 3.215}
    for name, (base, spread) in spreads.items():
        noise = np.random.default_rng([zlib.crc32(name.encode()), seed]).standard_normal(out[name].shape)
        drawn = base * np.exp(spread * noise) if base else spread * noise
        out[name] = jnp.asarray(drawn.astype(out[name].dtype))
    for name, factor in factors.items():
        out[name] = (out[name] * factor).astype(out[name].dtype)
    return out
```

```python
import math
from contextlib import ExitStack

import concourse.bass as bass
import numpy as np
from concourse import mybir

F32 = mybir.dt.float32
F16 = mybir.dt.float16
ALU = mybir.AluOpType
ACT = mybir.ActivationFunctionType
AX = mybir.AxisListType

P = 128
B = 4
T = 2048
D = 256
C = 128
KD = D // P
NCH = T // P
NG = 2
GB = B // NG
NL = 7
KVW = 2 * C + 2
LN_EPS = 1e-5
RMS_GUARD = 1e-24 / D
NORM_EPS2 = 1e-24

C_ID, C_MASK = 0, P
CONSTW = P * (1 + NL)


def constants():
    s, t = np.arange(P)[:, None], np.arange(P)[None, :]
    parts = [np.eye(P)]
    for l in range(NL):
        h = 1 << l
        m = (s // (2 * h) == t // (2 * h)) & (s // h % 2 == 0) & (t // h % 2 == 1)
        parts.append(m * (-1.0 if l == 0 else 1.0))
    return np.concatenate([np.asarray(p, np.float32) for p in parts], axis=1)


def attention(nc, io, x1_dram, X_dram, XT_dram):
    held = []
    with ExitStack() as ctx:
        def sb(name, shape, dt=F32):
            return ctx.enter_context(nc.sbuf_tensor(name, shape, dt))

        def per_group(name, shape, dt=F32):
            return [sb(f"{name}{g}", shape, dt) for g in range(NG)]

        def sem(name):
            held.append(ctx.enter_context(nc.semaphore("a_" + name)))
            return held[-1]

        def sems(name):
            return [sem(f"{name}{g}") for g in range(NG)]

        const = sb("a_const", [P, CONSTW])
        ident = const[:, C_ID:C_ID + P]
        ident16 = sb("a_ident16", [P, P], F16)
        wkv = sb("wkv", [P, KD, KVW])
        wqg = sb("wqg", [P, KD, 2 * C])
        wo = sb("wo", [P, D])
        bkv = sb("bkv", [P, KVW])
        bq = sb("bq", [P, 1])
        bg = sb("bg", [P, 1])
        bo = sb("bo", [P, D])
        neg_half = sb("a_neg_half", [P, GB])
        ln_eps = sb("a_ln_eps", [P, GB])
        zeros = sb("a_zeros", [P, P])

        x = per_group("x", [P, GB, D])
        xres = per_group("xres", [P, GB, D])
        stats = per_group("stats", [P, GB, 6])
        mv = per_group("mv", [P, GB, 2])
        rstd = per_group("rstd", [P, GB])
        xn = per_group("xn", [P, GB, D])
        xnT = per_group("xnT", [P, KD, GB, P])
        kvab = per_group("kvab", [P, GB, KVW])
        qT = per_group("qT", [P, GB, P])
        qTg = per_group("qTg", [P, GB, P])
        gateT = per_group("gateT", [P, GB, P])
        ab = per_group("ab", [P, GB, 2])
        junk = per_group("junk", [P, GB, C])
        kn2 = per_group("kn2", [P, GB])
        krn = per_group("krn", [P, GB])
        kh = per_group("kh", [P, GB, C])
        khd = per_group("khd", [P, GB, C])
        kT = per_group("kT", [P, GB, P])
        kTg = per_group("kTg", [P, GB, P])
        gam = per_group("gam", [P, GB, P])
        gbc = per_group("gbc", [P, GB, P])
        M = per_group("M", [P, GB, P])
        moff = per_group("moff", [P, NL, GB, P])
        Z = per_group("Z", [P, GB, P])
        ZT = per_group("ZT", [P, GB, P])
        P1T = per_group("P1T", [P, GB, P])
        X0 = per_group("X0", [P, GB, C])
        S = per_group("S", [P, GB, C])
        R = per_group("R", [P, GB, C])
        U = per_group("U", [P, GB, C])
        UT = per_group("UT", [P, GB, P])
        PT = per_group("PT", [P, GB, P])
        OT = per_group("OT", [P, GB, P])
        x1 = per_group("x1", [P, GB, D])
        stats2 = per_group("stats2", [P, GB, 6])
        mv2 = per_group("mv2", [P, GB, 2])
        guard = per_group("guard", [P, GB])
        var2 = per_group("var2", [P, GB])
        rvar = per_group("rvar", [P, GB])
        xf = per_group("xf", [P, GB, D])
        Xh = per_group("Xh", [P, GB, D], F16)
        Xl = per_group("Xl", [P, GB, D], F16)
        XT = per_group("XT", [P, 2, KD, GB, P], F16)
        bank = [[ctx.enter_context(nc.psum_tensor(f"a_bank{g}{n}", [P, 512], F32)) for n in range(4)]
                for g in range(NG)]

        def half(g, n, h=0):
            return bank[g][n][:, h * GB * P:(h + 1) * GB * P].rearrange("p (b t) -> p b t", b=GB)

        consts_in, cols_in, pool_consts, dve_consts = (
            sem("consts_in"), sem("cols_in"), sem("pool_consts"), sem("dve_consts"))
        (x_in, x_read, xres_ok, stats_ok, mv_ok, rstd_a, rstd_ok, xn_ok, xnT_ps, xnT_ok, kv_ps, kv_ok, qg_ps,
         qg_ok, ab_ok, kn_ok, krn_a, krn_ok, kh_ok, abc_ps, kT_ps, kT_ok, gam_ok, gbc_ok, scaled_ok, khd_ok,
         kk_ps, M_ok, z_half, moff_ok, ZT_ps, ZT_ok, P1T_ps, P1T_ok, Z_ps, Z_ok, kr_ps, X0_ok, S_ok,
         U_ps, U_ok, R_ps, R_ok, UT_ps, UT_ok, sc_ps, PT_ok, OT_ps, OT_ok, y_ps, x1_ok, x1_out, stats2_ok, mv2_ok, guard_ok, var2_ok, rvar_ok, xf_ok, Xh_ok, Xl_ok, XT_ps, XT_ok,
         X_out) = [
            sems(n) for n in (
                "x_in x_read xres_ok stats_ok mv_ok rstd_a rstd_ok xn_ok xnT_ps xnT_ok kv_ps kv_ok qg_ps "
                "qg_ok ab_ok kn_ok krn_a krn_ok kh_ok abc_ps kT_ps kT_ok gam_ok gbc_ok scaled_ok khd_ok "
                "kk_ps M_ok z_half moff_ok ZT_ps ZT_ok P1T_ps P1T_ok Z_ps Z_ok kr_ps X0_ok S_ok "
                "U_ps U_ok R_ps R_ok UT_ps UT_ok sc_ps PT_ok OT_ps OT_ok y_ps x1_ok x1_out "
                "stats2_ok mv2_ok guard_ok var2_ok rvar_ok xf_ok Xh_ok Xl_ok XT_ps XT_ok X_out").split()]
        N_CONSTS = 13 * 16
        work = ExitStack()
        block = work.enter_context(nc.Block())

        @block.sync
        def _(sp):
            def bcast(v, n):
                return v.rearrange("(a n) -> a n", a=1).broadcast_to([P, n])

            for dst, src in (
                (const[:, :], io["const"]),
                (wkv[:, :, 0:C], io["L0_attn_Wk"].rearrange("(k p) n -> p k n", p=P)),
                (wkv[:, :, C:2 * C], io["L0_attn_Wv"].rearrange("(k p) n -> p k n", p=P)),
                (wkv[:, :, 2 * C:2 * C + 1], io["L0_attn_Wa"].rearrange("(k p) n -> p k n", p=P)),
                (wkv[:, :, 2 * C + 1:], io["L0_attn_Wb"].rearrange("(k p) n -> p k n", p=P)),
                (wqg[:, :, 0:C], io["L0_attn_Wq"].rearrange("(k p) n -> p k n", p=P)),
                (wqg[:, :, C:], io["L0_attn_Wg"].rearrange("(k p) n -> p k n", p=P)),
                (wo[:, :], io["L0_attn_Wo"]),
                (bkv[:, 0:C], bcast(io["L0_attn_bk"], C)),
                (bkv[:, C:2 * C], bcast(io["L0_attn_bv"], C)),
                (bkv[:, 2 * C:2 * C + 1], bcast(io["L0_attn_ba"], 1)),
                (bkv[:, 2 * C + 1:], bcast(io["L0_attn_bb"], 1)),
                (bo[:, :], bcast(io["L0_attn_bo"], D)),
            ):
                sp.dma_start(dst, src, allow_slow_non_contiguous=True).then_inc(consts_in, 16)

            def load(i, n):
                for g in range(NG):
                    sp.wait_ge(xn_ok[g], n)
                    sp.wait_ge(xres_ok[g], n)
                    sp.dma_start(x[g][:, :, :], io["L0_attn_x"][g * GB:(g + 1) * GB, bass.ds(i * P, P), :]
                                 .rearrange("b p d -> p b d")).then_inc(x_in[g], 16)

            def store_parts(i, n):
                for g in range(NG):
                    gb = slice(g * GB, (g + 1) * GB)
                    sp.wait_ge(Xh_ok[g], n)
                    sp.dma_start(X_dram[0, gb, bass.ds(i * P, P), :].rearrange("b p d -> p b d"),
                                 Xh[g][:, :, :]).then_inc(X_out[g], 16)
                    sp.wait_ge(Xl_ok[g], n)
                    sp.dma_start(X_dram[1, gb, bass.ds(i * P, P), :].rearrange("b p d -> p b d"),
                                 Xl[g][:, :, :]).then_inc(X_out[g], 16)
                    sp.wait_ge(consts_in, N_CONSTS)
                    sp.wait_ge(XT_ok[g], n)
                    sp.dma_start(XT_dram[:, :, gb, bass.ds(i * P, P)],
                                 XT[g][:, :, :, :, :].rearrange("p s k b t -> p (s k) b t")).then_inc(X_out[g], 16)

            load(0, 1)
            with sp.Fori(0, NCH - 1) as i:
                n = sp.snap(i + 1)
                load(n, i + 2)
                store_parts(i, n)
            store_parts(NCH - 1, NCH)

        @block.gpsimd
        def _(pool):
            pool.dma_start(bq[:, :], io["L0_attn_bq"].rearrange("(p n) -> p n", n=1),
                           allow_slow_non_contiguous=True).then_inc(cols_in, 16)
            pool.dma_start(bg[:, :], io["L0_attn_bg"].rearrange("(p n) -> p n", n=1),
                           allow_slow_non_contiguous=True).then_inc(cols_in, 16)
            pool.memset(ln_eps[:, :], LN_EPS)
            pool.memset(neg_half[:, :], -0.5).then_inc(pool_consts, 1)
            pool.wait_ge(pool_consts, 1)
            pool.wait_ge(consts_in, N_CONSTS)
            for g in range(NG):
                pool.sem_inc(xres_ok[g], 1)
            with pool.Fori(0, NCH) as i:
                n = pool.snap(i + 1)
                for g in range(NG):
                    pool.wait_ge(mv_ok[g], n)
                    pool.tensor_tensor(rstd[g][:, :], mv[g][:, :, 1], ln_eps[:, :], ALU.add).then_inc(rstd_a[g], 1)
                    pool.wait_ge(rstd_a[g], n)
                    pool.tensor_tensor(rstd[g][:, :], rstd[g][:, :], neg_half[:, :], ALU.pow).then_inc(rstd_ok[g], 1)
                for g in range(NG):
                    pool.wait_ge(x_in[g], 16 * n)
                    pool.wait_ge(x1_ok[g], n)
                    pool.tensor_tensor(xres[g][:, :, :], x[g][:, :, :],
                                       bo[:, :].rearrange("p (a d) -> p a d", a=1).broadcast_to([P, GB, D]),
                                       ALU.add).then_inc(xres_ok[g], 1)
                for g in range(NG):
                    pool.wait_ge(pool_consts, 1)
                    pool.wait_ge(kn_ok[g], n)
                    pool.tensor_scalar(krn[g][:, :], kn2[g][:, :], NORM_EPS2, None, ALU.max).then_inc(krn_a[g], 1)
                    pool.wait_ge(krn_a[g], n)
                    pool.tensor_tensor(krn[g][:, :], krn[g][:, :], neg_half[:, :], ALU.pow).then_inc(krn_ok[g], 1)
                for g in range(NG):
                    pool.wait_ge(gbc_ok[g], n)
                    pool.wait_ge(kT_ok[g], n)
                    pool.tensor_tensor(kTg[g][:, :, :], kT[g][:, :, :], gbc[g][:, :, :], ALU.mult)
                    pool.wait_ge(qg_ok[g], n)
                    pool.tensor_tensor(qTg[g][:, :, :], qT[g][:, :, :], gbc[g][:, :, :], ALU.mult)\
                        .then_inc(scaled_ok[g], 1)
                for g in range(NG):
                    pool.wait_ge(M_ok[g], n)
                    m0 = const[:, C_MASK:C_MASK + P].rearrange("p (a t) -> p a t", a=1).broadcast_to([P, GB, P])
                    pool.tensor_tensor(moff[g][:, 0], M[g][:, :, :], m0, ALU.mult).then_inc(z_half[g], 1)
                    pool.wait_ge(z_half[g], n)
                    pool.tensor_tensor(Z[g][:, :, :], moff[g][:, 0],
                                       ident.rearrange("p (a t) -> p a t", a=1).broadcast_to([P, GB, P]),
                                       ALU.add).then_inc(moff_ok[g], 1)
                for l in range(1, NL):
                    for g in range(NG):
                        ml = const[:, C_MASK + l * P:C_MASK + (l + 1) * P]
                        pool.tensor_tensor(moff[g][:, l], M[g][:, :, :],
                                           ml.rearrange("p (a t) -> p a t", a=1).broadcast_to([P, GB, P]),
                                           ALU.mult).then_inc(moff_ok[g], 1)
                for g in range(NG):
                    pool.wait_ge(var2_ok[g], n)
                    pool.tensor_tensor(rvar[g][:, :], var2[g][:, :], neg_half[:, :], ALU.pow).then_inc(rvar_ok[g], 1)

        @block.vector
        def _(dve):
            dve.wait_ge(consts_in, N_CONSTS)
            dve.tensor_copy(ident16[:, :], ident)
            dve.memset(zeros[:, :], 0.0).then_inc(dve_consts, 1)
            for g in range(NG):
                dve.memset(R[g][:, :, :], 0.0).then_inc(R_ok[g], 1)
            for g in range(NG):
                dve.sem_inc(xn_ok[g], 1)
                dve.sem_inc(x1_ok[g], 1)
            dve.wait_ge(dve_consts, 1)
            dve.wait_ge(consts_in, N_CONSTS)
            with dve.Fori(0, NCH) as i:
                n = dve.snap(i + 1)
                for g in range(NG):
                    dve.wait_ge(x_in[g], 16 * n)
                    for b in range(GB):
                        last = dve.bn_stats(stats[g][:, b, :], x[g][:, b, :])
                    last.then_inc(stats_ok[g], 1)
                    dve.wait_ge(dve_consts, 1)
                    dve.wait_ge(stats_ok[g], n)
                    for b in range(GB):
                        last = dve.bn_aggr(mv[g][:, b, :], stats[g][:, b, :])
                    last.then_inc(mv_ok[g], 1)
                for g in range(NG):
                    dve.wait_ge(rstd_ok[g], n)
                    for b in range(GB):
                        last = dve.tensor_scalar(xn[g][:, b, :], x[g][:, b, :], mv[g][:, b, 0:1],
                                                 rstd[g][:, b:b + 1], ALU.subtract, ALU.mult)
                    last.then_inc(xn_ok[g], 1)
                for g in range(NG):
                    dve.wait_ge(kv_ps[g], n)
                    for b in range(GB):
                        last = dve.tensor_tensor(kvab[g][:, b, :], bank[g][1 + b][:, 0:KVW], bkv[:, :], ALU.add)
                    last.then_inc(kv_ok[g], 1)
                for g in range(NG):
                    dve.wait_ge(krn_ok[g], n)
                    for b in range(GB):
                        last = dve.tensor_scalar(kh[g][:, b, :], kvab[g][:, b, 0:C], krn[g][:, b:b + 1], None,
                                                 ALU.mult)
                    last.then_inc(kh_ok[g], 1)
                for g in range(NG):
                    dve.wait_ge(abc_ps[g], n)
                    for b in range(GB):
                        last = dve.tensor_tensor_scan(gam[g][:, b, :], half(g, 0)[:, b, :], ident, 0.0,
                                                      ALU.mult, ALU.add)
                    last.then_inc(gam_ok[g], 1)
                    for b in range(GB):
                        last = dve.tensor_tensor_scan(gbc[g][:, b, :], half(g, 0)[:, b, :], zeros[:, :], 1.0,
                                                      ALU.mult, ALU.add)
                    last.then_inc(gbc_ok[g], 1)
                    dve.wait_ge(gam_ok[g], n)
                    for b in range(GB):
                        last = dve.tensor_scalar(khd[g][:, b, :], kh[g][:, b, :], gam[g][:, b, P - 1:P], None,
                                                 ALU.mult)
                    last.then_inc(khd_ok[g], 1)
                for g in range(NG):
                    dve.wait_ge(kk_ps[g], n)
                    for b in range(GB):
                        last = dve.scalar_tensor_tensor(M[g][:, b, :], half(g, 2)[:, b, :], ab[g][:, b, 1:2],
                                                        gam[g][:, b, :], ALU.mult, ALU.mult)
                    last.then_inc(M_ok[g], 1)
                for g in range(NG):
                    dve.wait_ge(kr_ps[g], n)
                    dve.tensor_tensor(X0[g][:, :, :], kvab[g][:, :, C:2 * C], half(g, 2, 0), ALU.subtract)\
                        .then_inc(X0_ok[g], 1)
                    dve.tensor_copy(S[g][:, :, :], half(g, 2, 1)).then_inc(S_ok[g], 1)
                for l in range(1, NL):
                    for g in range(NG):
                        dve.wait_ge(Z_ps[g], (NL - 1) * i + l)
                        dve.tensor_tensor(Z[g][:, :, :], Z[g][:, :, :], half(g, 1), ALU.subtract)\
                            .then_inc(Z_ok[g], 1)
                for g in range(NG):
                    dve.wait_ge(R_ps[g], n)
                    dve.wait_ge(gbc_ok[g], n)
                    for b in range(GB):
                        last = dve.scalar_tensor_tensor(R[g][:, b, :], R[g][:, b, :], gbc[g][:, b, P - 1:P],
                                                        half(g, 0)[:, b, :], ALU.mult, ALU.add)
                    last.then_inc(R_ok[g], 1)
                for g in range(NG):
                    dve.wait_ge(sc_ps[g], n)
                    dve.tensor_tensor(PT[g][:, :, :], half(g, 2), gam[g][:, :, :], ALU.mult).then_inc(PT_ok[g], 1)
                for g in range(NG):
                    dve.wait_ge(OT_ps[g], n)
                    dve.tensor_tensor(OT[g][:, :, :], half(g, 3), gateT[g][:, :, :], ALU.mult)\
                        .then_inc(OT_ok[g], 1)
                for g in range(NG):
                    dve.wait_ge(y_ps[g], n)
                    dve.wait_ge(xres_ok[g], n + 1)
                    dve.wait_ge(x1_out[g], 16 * n)
                    dve.tensor_tensor(x1[g][:, :, :], xres[g][:, :, :],
                                      bank[g][1][:, :].rearrange("p (b d) -> p b d", b=GB), ALU.add)\
                        .then_inc(x1_ok[g], 1)
                for g in range(NG):
                    dve.wait_ge(x1_ok[g], n + 1)
                    for b in range(GB):
                        last = dve.bn_stats(stats2[g][:, b, :], x1[g][:, b, :])
                    last.then_inc(stats2_ok[g], 1)
                    dve.wait_ge(dve_consts, 1)
                    dve.wait_ge(stats2_ok[g], n)
                    for b in range(GB):
                        last = dve.bn_aggr(mv2[g][:, b, :], stats2[g][:, b, :])
                    last.then_inc(mv2_ok[g], 1)
                    dve.wait_ge(mv2_ok[g], n)
                    dve.tensor_scalar(guard[g][:, :], mv2[g][:, :, 1], RMS_GUARD, RMS_GUARD * LN_EPS,
                                      ALU.mult, ALU.add).then_inc(guard_ok[g], 1)
                    dve.wait_ge(guard_ok[g], n)
                    dve.tensor_tensor(var2[g][:, :], mv2[g][:, :, 1], guard[g][:, :], ALU.max).then_inc(var2_ok[g], 1)
                for g in range(NG):
                    dve.wait_ge(rvar_ok[g], n)
                    for b in range(GB):
                        last = dve.tensor_scalar(xf[g][:, b, :], x1[g][:, b, :], mv2[g][:, b, 0:1],
                                                 rvar[g][:, b:b + 1], ALU.subtract, ALU.mult)
                    last.then_inc(xf_ok[g], 1)
                for g in range(NG):
                    dve.wait_ge(Xh_ok[g], n)
                    dve.wait_ge(X_out[g], 48 * n)
                    dve.tensor_tensor(Xl[g][:, :, :], xf[g][:, :, :], Xh[g][:, :, :], ALU.subtract)\
                        .then_inc(Xl_ok[g], 1)

        @block.scalar
        def _(act):
            act.wait_ge(cols_in, 32)
            for g in range(NG):
                act.sem_inc(x1_out[g], 16)
                act.sem_inc(X_out[g], 48)
            with act.Fori(0, NCH) as i:
                n = act.snap(i + 1)
                for g in range(NG):
                    act.wait_ge(xnT_ps[g], n)
                    act.copy(xnT[g][:, :, :, :].rearrange("p k b t -> p (k b t)"), bank[g][0][:, :])\
                        .then_inc(xnT_ok[g], 1)
                for g in range(NG):
                    act.wait_ge(kv_ok[g], n)
                    for b in range(GB):
                        last = act.activation(junk[g][:, b, :], kvab[g][:, b, 0:C], ACT.Square,
                                              accum_out=kn2[g][:, b:b + 1])
                    last.then_inc(kn_ok[g], 1)
                    act.activation(ab[g][:, :, :], kvab[g][:, :, 2 * C:], ACT.Sigmoid).then_inc(ab_ok[g], 1)
                for g in range(NG):
                    act.wait_ge(qg_ps[g], n)
                    act.activation(qT[g][:, :, :], half(g, 3, 0), ACT.Identity, bias=bq[:, 0:1])
                    act.activation(gateT[g][:, :, :], half(g, 3, 1), ACT.Sigmoid, bias=bg[:, 0:1])\
                        .then_inc(qg_ok[g], 1)
                for g in range(NG):
                    act.wait_ge(kT_ps[g], n)
                    act.copy(kT[g][:, :, :], half(g, 1)).then_inc(kT_ok[g], 1)
                for l in range(1, NL):
                    for g in range(NG):
                        act.wait_ge(ZT_ps[g], (NL - 1) * i + l)
                        act.copy(ZT[g][:, :, :], half(g, 3)).then_inc(ZT_ok[g], 1)
                    for g in range(NG):
                        act.wait_ge(P1T_ps[g], (NL - 1) * i + l)
                        act.copy(P1T[g][:, :, :], half(g, 0)).then_inc(P1T_ok[g], 1)
                for g in range(NG):
                    act.wait_ge(U_ps[g], n)
                    for b in range(GB):
                        last = act.activation(U[g][:, b, :], half(g, 3)[:, b, :], ACT.Identity,
                                              scale=ab[g][:, b, 1:2])
                    last.then_inc(U_ok[g], 1)
                for g in range(NG):
                    act.wait_ge(UT_ps[g], n)
                    act.copy(UT[g][:, :, :], half(g, 1)).then_inc(UT_ok[g], 1)
                for g in range(NG):
                    act.wait_ge(x1_ok[g], n + 1)
                    act.dma_start(x1_dram[g * GB:(g + 1) * GB, bass.ds(i * P, P), :].rearrange("b p d -> p b d"),
                                  x1[g][:, :, :]).then_inc(x1_out[g], 16)
                for g in range(NG):
                    act.wait_ge(xf_ok[g], n)
                    act.wait_ge(X_out[g], 48 * n)
                    act.copy(Xh[g][:, :, :], xf[g][:, :, :]).then_inc(Xh_ok[g], 1)
                for g in range(NG):
                    act.wait_ge(XT_ps[g], n)
                    act.copy(XT[g][:, :, :, :, :].rearrange("p s k b t -> p (s k b t)"),
                             bank[g][2][:, :].bitcast(F16)).then_inc(XT_ok[g], 1)
            for g in range(NG):
                act.wait_ge(x1_out[g], 16 * NCH + 16)
                act.wait_ge(X_out[g], 16 * 3 * NCH + 48)

        @block.tensor
        def _(pe):
            pe.wait_ge(consts_in, N_CONSTS)
            pe.wait_ge(dve_consts, 1)
            with pe.Fori(0, NCH) as i:
                n = pe.snap(i + 1)
                for g in range(NG):
                    pe.wait_ge(xn_ok[g], n + 1)
                    pe.wait_ge(R_ok[g], n)
                    for k in range(KD):
                        for b in range(GB):
                            at = (k * GB + b) * P
                            last = pe.transpose(bank[g][0][:, at:at + P], xn[g][:, b, k * P:(k + 1) * P], ident)
                    last.then_inc(xnT_ps[g], 1)
                for g in range(NG):
                    pe.wait_ge(xnT_ok[g], n)
                    pe.wait_ge(x1_ok[g], n)
                    for b in range(GB):
                        for k in range(KD):
                            last = pe.matmul(bank[g][1 + b][:, 0:KVW], xnT[g][:, k, b, :], wkv[:, k, :],
                                             start=(k == 0), stop=(k == KD - 1))
                    last.then_inc(kv_ps[g], 1)
                    for h in range(2):
                        for k in range(KD):
                            last = pe.matmul(half(g, 3, h).rearrange("p b t -> p (b t)"),
                                             wqg[:, k, h * C:(h + 1) * C],
                                             xnT[g][:, k].rearrange("p b t -> p (b t)"),
                                             start=(k == 0), stop=(k == KD - 1))
                    last.then_inc(qg_ps[g], 1)
                for g in range(NG):
                    pe.wait_ge(ab_ok[g], n)
                    for b in range(GB):
                        last = pe.transpose(half(g, 0)[:, b, :], ab[g][:, b, 0:1].broadcast_to([P, P]), ident)
                    last.then_inc(abc_ps[g], 1)
                    pe.wait_ge(kh_ok[g], n)
                    for b in range(GB):
                        last = pe.transpose(half(g, 1)[:, b, :], kh[g][:, b, :], ident)
                    last.then_inc(kT_ps[g], 1)
                for g in range(NG):
                    pe.wait_ge(kT_ok[g], n)
                    for b in range(GB):
                        last = pe.matmul(half(g, 2)[:, b, :], kT[g][:, b, :], kT[g][:, b, :], start=True, stop=True)
                    last.then_inc(kk_ps[g], 1)
                for g in range(NG):
                    pe.wait_ge(scaled_ok[g], n)
                    pe.wait_ge(M_ok[g], n)
                    pe.wait_ge(R_ok[g], n)
                    for b in range(GB):
                        pe.matmul(half(g, 2, 0)[:, b, :], kTg[g][:, b, :], R[g][:, b, :], start=True, stop=True)
                    for b in range(GB):
                        last = pe.transpose(half(g, 2, 1)[:, b, :], R[g][:, b, :], ident)
                    last.then_inc(kr_ps[g], 1)
                for l in range(1, NL):
                    for g in range(NG):
                        if l == 1:
                            pe.wait_ge(moff_ok[g], NL * i + 1)
                            pe.wait_ge(qg_ok[g], n)
                        else:
                            pe.wait_ge(Z_ok[g], (NL - 1) * i + l - 1)
                        for b in range(GB):
                            last = pe.transpose(half(g, 3)[:, b, :], Z[g][:, b, :], ident)
                        last.then_inc(ZT_ps[g], 1)
                    for g in range(NG):
                        pe.wait_ge(ZT_ok[g], (NL - 1) * i + l)
                        pe.wait_ge(moff_ok[g], NL * i + l + 1)
                        if l == 1:
                            pe.wait_ge(gbc_ok[g], n)
                        for b in range(GB):
                            last = pe.matmul(half(g, 0)[:, b, :], moff[g][:, l, b, :], ZT[g][:, b, :],
                                             start=True, stop=True)
                        last.then_inc(P1T_ps[g], 1)
                    for g in range(NG):
                        pe.wait_ge(P1T_ok[g], (NL - 1) * i + l)
                        for b in range(GB):
                            last = pe.matmul(half(g, 1)[:, b, :], P1T[g][:, b, :], Z[g][:, b, :],
                                             start=True, stop=True)
                        last.then_inc(Z_ps[g], 1)
                for g in range(NG):
                    pe.wait_ge(Z_ok[g], (NL - 1) * i + NL - 1)
                    pe.wait_ge(X0_ok[g], n)
                    for b in range(GB):
                        last = pe.matmul(half(g, 3)[:, b, :], Z[g][:, b, :], X0[g][:, b, :], start=True, stop=True)
                    last.then_inc(U_ps[g], 1)
                for g in range(NG):
                    pe.wait_ge(U_ok[g], n)
                    pe.wait_ge(khd_ok[g], n)
                    for b in range(GB):
                        last = pe.matmul(half(g, 0)[:, b, :], khd[g][:, b, :], U[g][:, b, :], start=True, stop=True)
                    last.then_inc(R_ps[g], 1)
                    for b in range(GB):
                        last = pe.transpose(half(g, 1)[:, b, :], U[g][:, b, :], ident)
                    last.then_inc(UT_ps[g], 1)
                for g in range(NG):
                    pe.wait_ge(UT_ok[g], n)
                    pe.wait_ge(S_ok[g], n)
                    for b in range(GB):
                        last = pe.matmul(half(g, 2)[:, b, :], UT[g][:, b, :], qT[g][:, b, :], start=True, stop=True)
                    last.then_inc(sc_ps[g], 1)
                for g in range(NG):
                    pe.wait_ge(PT_ok[g], n)
                    for b in range(GB):
                        pe.matmul(half(g, 3)[:, b, :], S[g][:, b, :], qTg[g][:, b, :], start=True, stop=False)
                        last = pe.matmul(half(g, 3)[:, b, :], kh[g][:, b, :], PT[g][:, b, :], start=False, stop=True)
                    last.then_inc(OT_ps[g], 1)
                for g in range(NG):
                    pe.wait_ge(OT_ok[g], n)
                    for b in range(GB):
                        last = pe.matmul(bank[g][1][:, b * D:(b + 1) * D], OT[g][:, b, :], wo[:, :],
                                         start=True, stop=True)
                    last.then_inc(y_ps[g], 1)
                for g in range(NG):
                    pe.wait_ge(Xh_ok[g], n)
                    pe.wait_ge(Xl_ok[g], n)
                    bank16 = bank[g][2][:, :].bitcast(F16)
                    for s, part in enumerate((Xh, Xl)):
                        for k in range(KD):
                            for b in range(GB):
                                at = ((s * KD + k) * GB + b) * P
                                last = pe.transpose(bank16[:, at:at + P], part[g][:, b, k * P:(k + 1) * P],
                                                    ident16[:, :])
                    last.then_inc(XT_ps[g], 1)

        work.close()
        with nc.Block() as clearing:
            @clearing.gpsimd
            def _(pool):
                for s in held:
                    pool.sem_clear(s)


E_SLOTS = 1024
HID = 4 * D
NS = E_SLOTS // P
NT = T // P
HS = E_SLOTS // 2
QS = HS // P
NF = HID // P
XW = D + 1
XS = D + 2
WSCALE = 64.0
ESHIFT = 12 * math.log(2)


def moe(nc, io, x1_dram, X_dram, XT_dram, out):
    with ExitStack() as ctx:
        def sb(name, shape, dt=F32):
            return ctx.enter_context(nc.sbuf_tensor("m_" + name, shape, dt))

        def two(name, shape, dt=F32):
            return [sb(f"{name}{p}", shape, dt) for p in range(2)]

        def sem(name):
            return ctx.enter_context(nc.semaphore("m_" + name))

        def sems(name):
            return [sem(f"{name}{p}") for p in range(2)]

        ident = sb("ident", [P, P])
        ident16 = sb("ident16", [P, P], F16)
        zero16 = sb("zero16", [P, XW], F16)
        L = sb("L", [P, NT, E_SLOTS])
        X = sb("X", [P, 2, NT, XS], F16)
        XT = sb("XT", [P, 2 * KD, T], F16)
        seT = sb("seT", [P, 2, KD, E_SLOTS], F16)
        w1s = sb("w1s", [P, 2, KD, HID], F16)
        w2s = sb("w2s", [P, 2, NF, D], F16)
        gx = sb("gx", [P, D])
        gs = sb("gs", [P, D])
        gx_col = sb("gx_col", [P, KD])
        neg_half = sb("neg_half", [P, NS])
        slots_in = L[:, 0:2, :].rearrange("p a n -> p (a n)").rearrange("p (e d) -> p e d", d=D)
        w1_in = L[:, 2:4, :].rearrange("p a n -> p (a n)").rearrange("p (k n) -> p k n", k=KD)
        w2_in = L[:, 4:6, :].rearrange("p a n -> p (a n)").rearrange("p (f n) -> p f n", f=NF)
        slots_n = L[:, 6:8, :].rearrange("p a n -> p (a n)").rearrange("p (e d) -> p e d", d=D)
        slots_g = L[:, 8:10, :].rearrange("p a n -> p (a n)").rearrange("p (e d) -> p e d", d=D)
        w1_g = L[:, 10:12, :].rearrange("p a n -> p (a n)").rearrange("p (k n) -> p k n", k=KD)
        junk = L[:, 12:14, :].rearrange("p a n -> p (a n)").rearrange("p (e d) -> p e d", d=D)
        gxs = sb("gxs", [P, D])
        sp_h = L[:, 14, :].bitcast(F16).rearrange("p (e d) -> p e d", d=D)
        sp_l = L[:, 15, :].bitcast(F16).rearrange("p (e d) -> p e d", d=D)
        sn2 = sb("sn2", [P, NS])
        sn2g = sb("sn2g", [P, NS])
        srn = sb("srn", [P, NS])

        rmax = sb("rmax", [P, NT])
        nrm = sb("nrm", [P, NT])
        cmax = sb("cmax", [P, E_SLOTS])
        mcol = sb("mcol", [P, NS])
        mcs = sb("mcs", [P, NS])
        Mb = sb("Mb", [P, E_SLOTS])
        Dm = two("Dm", [P, HS])
        E = two("E", [P, HS])
        Eh = two("Eh", [P, HS], F16)
        El = two("El", [P, HS], F16)
        rden = sb("rden", [P, QS])
        sl = sb("sl", [P, QS, D])
        sTh = sb("sTh", [P, KD, HS], F16)
        sTl = sb("sTl", [P, KD, HS], F16)
        hf = two("hf", [P, HS])
        hh = sb("hh", [P, NF, HS], F16)
        hl = sb("hl", [P, NF, HS], F16)
        Ph = sb("Ph", [P, NS, XS], F16)
        Pl = sb("Pl", [P, NS, XS], F16)
        Ec = two("Ec", [P, E_SLOTS])
        Th = two("Th", [P, E_SLOTS], F16)
        Tl = two("Tl", [P, E_SLOTS], F16)
        cden = two("cden", [P, 1])
        x1t = two("x1t", [P, D])
        o = two("o", [P, D])

        wide = [ctx.enter_context(nc.psum_tensor(f"m_wide{n}", [P, 1024], F32)) for n in range(4)]
        lg = tp = wide[0:2]
        acc = [wide[q // 2][:, 512 * (q % 2):512 * (q % 2) + XW] for q in range(QS)]
        up = [wide[3][:, 512 * p:512 * p + HS] for p in range(2)]
        down = [wide[2][:, 512 * p:512 * p + D] for p in range(2)]
        co = [wide[2][:, 512 * p:512 * p + XW] for p in range(2)]

        in_ok, pc, sq_ok, sn_g, srn_ok, sln_ok, slg_ok, slh_ok, sll_ok = map(sem, (
            "in_ok pool_consts sq_ok sn_g srn_ok sln_ok slg_ok slh_ok sll_ok").split())
        gxs_ok, w1g_ok, w1h_ok, w2h_ok, seT_ps, seT_ok, set_up = map(sem, (
            "gxs_ok w1g_ok w1h_ok w2h_ok seT_ps seT_ok set_up").split())
        X_in, XT_in, A_dve, rm_ok, cT_ps, mc_ok, mcs_ok, Mb_ps, Mb_ok = map(sem, (
            "X_in XT_in A_dve rm_ok cT_ps mc_ok mcs_ok Mb_ps Mb_ok").split())
        cm_ok = sem("cm_ok")
        acc_ps, rd_ok, sl_ok, sT_ps, sTh_ok, sTl_ok = map(sem, "acc_ps rd_ok sl_ok sT_ps sTh_ok sTl_ok".split())
        (lg_ps, L_ok, D_ok, E_ok, Eh_ok, El_ok, B_ps, up_ps, hf_ok, hh_ok, hl_ok, dn_ps, Ph_ok, Pl_ok,
         Ec_ok, tp_ps, Th_ok, Tl_ok, co_ps, cd_ok, o_ok, o_out, x1_in) = [sems(x) for x in (
             "lg_ps L_ok D_ok E_ok Eh_ok El_ok B_ps up_ps hf_ok hh_ok hl_ok dn_ps Ph_ok Pl_ok "
             "Ec_ok tp_ps Th_ok Tl_ok co_ps cd_ok o_ok o_out x1_in").split()]
        N_IN = 7 * 16
        HB = NT // 2
        parts3 = ((0, 0), (0, 1), (1, 0))
        block = ctx.enter_context(nc.Block())

        @block.sync
        def _(sp):
            def bcast(v, n):
                return v.rearrange("(a n) -> a n", a=1).broadcast_to([P, n])

            for dst, src in (
                (ident[:, :], io["const"][:, C_ID:C_ID + P]),
                (slots_in, io["L0_ffn_slot_embeds"].rearrange("e p d -> p e d")),
                (w1_in, io["L0_ffn_w1"].rearrange("(k p) n -> p k n", p=P)),
                (w2_in, io["L0_ffn_w2"].rearrange("(f p) n -> p f n", p=P)),
                (gx[:, :], bcast(io["L0_ffn_gamma_x"], D)),
                (gs[:, :], bcast(io["L0_ffn_gamma_slot"], D)),
                (gx_col[:, :], io["L0_ffn_gamma_x"].rearrange("(k p) -> p k", p=P)),
            ):
                sp.dma_start(dst, src, allow_slow_non_contiguous=True).then_inc(in_ok, 16)
            for p in range(2):
                sp.sem_inc(o_out[p], 16)
            with sp.Fori(0, B) as b:
                nb = sp.snap(b + 1)
                sp.wait_ge(cT_ps, nb)
                sp.dma_start(XT[:, :, :], XT_dram[:, :, b, :]).then_inc(XT_in, 16)
                done = sp.snap(sp.to_reg(2 * b + 1))
                sp.wait_ge(in_ok, N_IN)
                sp.wait_ge(acc_ps, done)
                with sp.Fori(0, NT) as j:
                    for s in range(2):
                        sp.dma_start(X[:, s, bass.ds(j, 1), 0:D].rearrange("q a d -> q (a d)"),
                                     X_dram[s, b, bass.ds(j * P, P), :]).then_inc(X_in, 16)
                with sp.Fori(0, HB) as h:
                    n = sp.snap(b * HB + h + 1)
                    for p in range(2):
                        sp.wait_ge(o_ok[p], n)
                        sp.dma_start(x1t[p][:, :], x1_dram[b, bass.ds(h * 2 * P + p * P, P), :])\
                            .then_inc(x1_in[p], 16)
                    for p in range(2):
                        sp.wait_ge(o_ok[p], n + 1)
                        sp.dma_start(out[b, bass.ds(h * 2 * P + p * P, P), :], o[p][:, :]).then_inc(o_out[p], 16)
            for p in range(2):
                sp.wait_ge(o_out[p], 16 * B * HB + 16)

        @block.gpsimd
        def _(pool):
            pool.memset(neg_half[:, :], -0.5)
            pool.memset(zero16[:, :], 0.0)
            for s in range(2):
                pool.memset(X[:, s, :, D:], 1.0 - s)
            pool.memset(Ph[:, :, D:], WSCALE)
            pool.memset(Pl[:, :, D:], 0.0).then_inc(pc, 1)
            pool.wait_ge(pc, 1)
            pool.wait_ge(sq_ok, 1)
            pool.tensor_scalar(sn2g[:, :], sn2[:, :], NORM_EPS2, None, ALU.max).then_inc(sn_g, 1)
            pool.wait_ge(sn_g, 1)
            pool.tensor_tensor(srn[:, :], sn2g[:, :], neg_half[:, :], ALU.pow).then_inc(srn_ok, 1)
            with pool.Fori(0, 2 * B) as s:
                with pool.Fori(0, HB) as h:
                    for p in range(2):
                        n = pool.snap(pool.to_reg(s * HB + h + 1))
                        pool.wait_ge(pc, 1)
                        pool.wait_ge(E_ok[p], n)
                        pool.wait_ge(B_ps[p], n)
                        pool.tensor_copy(Eh[p][:, :], E[p][:, :]).then_inc(Eh_ok[p], 1)
                for f in range(NF):
                    n = pool.snap(pool.to_reg(s * (NF // 2) + f // 2 + 1))
                    pool.wait_ge(pc, 1)
                    pool.wait_ge(hf_ok[f % 2], n)
                    pool.tensor_copy(hh[:, f, :], hf[f % 2][:, :]).then_inc(hh_ok[f % 2], 1)

        @block.vector
        def _(dve):
            dve.wait_ge(in_ok, N_IN)
            dve.tensor_copy(ident16[:, :], ident[:, :])
            dve.tensor_tensor(gxs[:, :], gx[:, :], gs[:, :], ALU.mult).then_inc(gxs_ok, 1)
            dve.wait_ge(srn_ok, 1)
            for e in range(NS):
                last = dve.tensor_scalar(slots_n[:, e, :], slots_in[:, e, :], srn[:, e:e + 1], math.sqrt(D),
                                         ALU.mult, ALU.mult)
            last.then_inc(sln_ok, 1)
            dve.wait_ge(sln_ok, 1)
            dve.wait_ge(gxs_ok, 1)
            dve.tensor_tensor(slots_g, slots_n, gxs[:, :].rearrange("p (a d) -> p a d", a=1).broadcast_to([P, NS, D]),
                              ALU.mult).then_inc(slg_ok, 1)
            dve.wait_ge(slg_ok, 1)
            dve.tensor_copy(sp_h, slots_g).then_inc(slh_ok, 1)
            dve.wait_ge(slh_ok, 1)
            dve.tensor_tensor(sp_l, slots_g, sp_h, ALU.subtract).then_inc(sll_ok, 1)
            for k in range(KD):
                last = dve.tensor_scalar(w1_g[:, k, :], w1_in[:, k, :], gx_col[:, k:k + 1], WSCALE,
                                         ALU.mult, ALU.mult)
            last.then_inc(w1g_ok, 1)
            dve.tensor_scalar(w2s[:, 0, :, :], w2_in, WSCALE, None, ALU.mult).then_inc(w2h_ok, 1)
            dve.wait_ge(w1g_ok, 1)
            dve.tensor_copy(w1s[:, 0, :, :], w1_g).then_inc(w1h_ok, 1)
            dve.wait_ge(w2h_ok, 1)
            dve.scalar_tensor_tensor(w2s[:, 1, :, :], w2_in, WSCALE, w2s[:, 0, :, :], ALU.mult, ALU.subtract)
            dve.wait_ge(w1h_ok, 1)
            dve.tensor_tensor(w1s[:, 1, :, :], w1_g, w1s[:, 0, :, :], ALU.subtract).then_inc(set_up, 1)
            for p in range(2):
                dve.sem_inc(El_ok[p], 1)
                dve.sem_inc(hl_ok[p], 1)
                dve.sem_inc(Pl_ok[p], 1)
                dve.sem_inc(Tl_ok[p], 1)
                dve.sem_inc(o_ok[p], 1)
            dve.sem_inc(sl_ok, 1)

            with dve.Fori(0, B) as b:
                nb = dve.snap(b + 1)
                dve.memset(cmax[:, :], -3.0e38).then_inc(cm_ok, 1)
                with dve.Fori(0, HB) as h:
                    m = dve.snap(b * HB + h)
                    for p in range(2):
                        dve.wait_ge(L_ok[p], m + 2)
                        dve.wait_ge(cm_ok, 2 * m + nb + p)
                        dve.tensor_tensor(cmax[:, :], cmax[:, :], L[:, bass.ds(2 * h + p, 1), :]
                                          .rearrange("q a n -> q (a n)"), ALU.max).then_inc(cm_ok, 1)
                        dve.tensor_reduce(rmax[:, bass.ds(2 * h + p, 1)], L[:, bass.ds(2 * h + p, 1), :]
                                          .rearrange("q a n -> q (a n)"), AX.X, ALU.max, negate=True)\
                            .then_inc(rm_ok, 1)
                dve.wait_ge(rm_ok, NT * nb)
                dve.tensor_scalar(nrm[:, :], rmax[:, :], ESHIFT, None, ALU.add).then_inc(A_dve, 1)
                dve.wait_ge(cT_ps, nb + 1)
                dve.tensor_reduce(mcol[:, :], wide[2][:, :].rearrange("q (e t) -> q e t", t=P), AX.X, ALU.max)\
                    .then_inc(mc_ok, 1)
                dve.wait_ge(mc_ok, nb)
                dve.tensor_scalar(mcs[:, :], mcol[:, :], ESHIFT, None, ALU.subtract).then_inc(mcs_ok, 1)

                with dve.Fori(0, 2) as v:
                    s = dve.snap(2 * b + v)

                    def shifted(h, p):
                        dve.wait_ge(El_ok[p], s * HB + h + 1)
                        dve.tensor_tensor(Dm[p][:, :],
                                          L[:, bass.ds(2 * h + p, 1), bass.ds(v * HS, HS)]
                                          .rearrange("q a n -> q (a n)"),
                                          Mb[:, bass.ds(v * HS, HS)], ALU.subtract).then_inc(D_ok[p], 1)

                    def low(h, p):
                        n = s * HB + h + 1
                        dve.wait_ge(Eh_ok[p], n)
                        dve.tensor_tensor(El[p][:, :], E[p][:, :], Eh[p][:, :], ALU.subtract).then_inc(El_ok[p], 1)

                    dve.wait_ge(Mb_ok, nb)
                    shifted(0, 0)
                    with dve.Fori(0, HB - 1) as h:
                        shifted(h, 1)
                        low(h, 0)
                        shifted(h + 1, 0)
                        low(h, 1)
                    shifted(HB - 1, 1)
                    low(HB - 1, 0)
                    low(HB - 1, 1)
                    dve.wait_ge(acc_ps, s + 2)
                    for q in range(QS):
                        last = dve.reciprocal(rden[:, q:q + 1], acc[q][:, D:D + 1])
                    last.then_inc(rd_ok, 1)
                    dve.wait_ge(rd_ok, s + 1)
                    for q in range(QS):
                        last = dve.tensor_scalar(sl[:, q, :], acc[q][:, 0:D], rden[:, q:q + 1], None, ALU.mult)
                    last.then_inc(sl_ok, 1)
                    dve.wait_ge(sTh_ok, s + 1)
                    dve.tensor_tensor(sTl[:, :, :].rearrange("q k n -> q (k n)"), wide[2][:, :],
                                      sTh[:, :, :].rearrange("q k n -> q (k n)"), ALU.subtract).then_inc(sTl_ok, 1)
                    for f in range(NF):
                        dve.wait_ge(hh_ok[f % 2], s * (NF // 2) + f // 2 + 1)
                        dve.tensor_tensor(hl[:, f, :], hf[f % 2][:, :], hh[:, f, :], ALU.subtract)\
                            .then_inc(hl_ok[f % 2], 1)
                    for q in range(QS):
                        dve.wait_ge(Ph_ok[q % 2], s * (QS // 2) + q // 2 + 1)
                        at = bass.ds(v * QS + q, 1)
                        dve.tensor_tensor(Pl[:, at, 0:D].rearrange("q a n -> q (a n)"), down[q % 2],
                                          Ph[:, at, 0:D].rearrange("q a n -> q (a n)"), ALU.subtract)\
                            .then_inc(Pl_ok[q % 2], 1)

                def low_weights(h, p):
                    n = b * HB + h + 1
                    dve.wait_ge(Th_ok[p], n)
                    dve.tensor_tensor(Tl[p][:, :], tp[p][:, :], Th[p][:, :], ALU.subtract).then_inc(Tl_ok[p], 1)

                def finish(h, p):
                    n = b * HB + h + 1
                    dve.wait_ge(co_ps[p], n)
                    dve.reciprocal(cden[p][:, :], co[p][:, D:D + 1]).then_inc(cd_ok[p], 1)
                    dve.wait_ge(cd_ok[p], n)
                    dve.wait_ge(x1_in[p], 16 * n)
                    dve.wait_ge(o_out[p], 16 * n)
                    dve.scalar_tensor_tensor(o[p][:, :], co[p][:, 0:D], cden[p][:, 0:1], x1t[p][:, :],
                                             ALU.mult, ALU.add).then_inc(o_ok[p], 1)

                low_weights(0, 0)
                with dve.Fori(0, HB - 1) as h:
                    low_weights(h, 1)
                    finish(h, 0)
                    low_weights(h + 1, 0)
                    finish(h, 1)
                low_weights(HB - 1, 1)
                finish(HB - 1, 0)
                finish(HB - 1, 1)

        @block.scalar
        def _(act):
            act.wait_ge(in_ok, N_IN)
            for e in range(NS):
                last = act.activation(junk[:, e, :], slots_in[:, e, :], ACT.Square, accum_out=sn2[:, e:e + 1])
            last.then_inc(sq_ok, 1)
            for e in range(NS):
                act.wait_ge(seT_ps, e + 1)
                act.copy(seT[:, :, :, e * P:(e + 1) * P].rearrange("q s k n -> q (s k) n"),
                         lg[e % 2][:, 0:256].bitcast(F16).rearrange("q (s n) -> q s n", n=P)).then_inc(seT_ok, 1)
            act.wait_ge(set_up, 1)
            act.wait_ge(seT_ok, NS)
            for p in range(2):
                act.sem_inc(L_ok[p], 1)
            with act.Fori(0, B) as b:
                nb = act.snap(b + 1)
                with act.Fori(0, HB) as h:
                    m = act.snap(b * HB + h + 1)
                    for p in range(2):
                        act.wait_ge(pc, 1)
                        act.wait_ge(lg_ps[p], m)
                        act.copy(L[:, bass.ds(2 * h + p, 1), :].rearrange("q a n -> q (a n)"), lg[p][:, :])\
                            .then_inc(L_ok[p], 1)
                act.wait_ge(Mb_ps, nb)
                act.copy(Mb[:, :], wide[3][:, :]).then_inc(Mb_ok, 1)
                with act.Fori(0, 2) as v:
                    s = act.snap(2 * b + v)
                    with act.Fori(0, HB) as h:
                        for p in range(2):
                            act.wait_ge(D_ok[p], s * HB + h + 1)
                            act.activation(E[p][:, :], Dm[p][:, :], ACT.Exp).then_inc(E_ok[p], 1)
                    act.wait_ge(sT_ps, s + 1)
                    act.copy(sTh[:, :, :].rearrange("q k n -> q (k n)"), wide[2][:, :]).then_inc(sTh_ok, 1)
                    for f in range(NF):
                        n = s * (NF // 2) + f // 2 + 1
                        act.wait_ge(up_ps[f % 2], n)
                        act.wait_ge(hl_ok[f % 2], n)
                        act.activation(hf[f % 2][:, :], up[f % 2], ACT.Gelu, scale=1.0 / WSCALE)\
                            .then_inc(hf_ok[f % 2], 1)
                    for q in range(QS):
                        act.wait_ge(pc, 1)
                        act.wait_ge(dn_ps[q % 2], s * (QS // 2) + q // 2 + 1)
                        act.copy(Ph[:, bass.ds(v * QS + q, 1), 0:D].rearrange("q a n -> q (a n)"), down[q % 2])\
                            .then_inc(Ph_ok[q % 2], 1)

                def weights(h, p):
                    n = act.snap(b * HB + h + 1)
                    act.wait_ge(pc, 1)
                    act.wait_ge(tp_ps[p], n)
                    act.activation(Ec[p][:, :], L[:, bass.ds(2 * h + p, 1), :].rearrange("q a n -> q (a n)"),
                                   ACT.Exp, bias=nrm[:, bass.ds(2 * h + p, 1)]).then_inc(Ec_ok[p], 1)

                def high(h, p):
                    n = b * HB + h + 1
                    act.wait_ge(tp_ps[p], n + 1)
                    act.copy(Th[p][:, :], tp[p][:, :]).then_inc(Th_ok[p], 1)

                act.wait_ge(A_dve, nb)
                weights(0, 0)
                with act.Fori(0, HB - 1) as h:
                    weights(h, 1)
                    high(h, 0)
                    weights(h + 1, 0)
                    high(h, 1)
                weights(HB - 1, 1)
                high(HB - 1, 0)
                high(HB - 1, 1)

        @block.tensor
        def _(pe):
            pe.wait_ge(pc, 1)
            pe.wait_ge(sll_ok, 1)
            for e in range(NS):
                if e >= 2:
                    pe.wait_ge(seT_ok, e - 1)
                half16 = lg[e % 2][:, 0:256].bitcast(F16)
                for s, part in enumerate((sp_h, sp_l)):
                    for k in range(KD):
                        at = (s * KD + k) * P
                        last = pe.transpose(half16[:, at:at + P], part[:, e, k * P:(k + 1) * P], ident16[:, :])
                last.then_inc(seT_ps, 1)
            pe.wait_ge(seT_ok, NS)
            pe.wait_ge(set_up, 1)
            for p in range(2):
                pe.sem_inc(B_ps[p], 1)
                pe.sem_inc(tp_ps[p], 1)
            pe.sem_inc(cT_ps, 1)
            pe.sem_inc(acc_ps, 1)
            with pe.Fori(0, B) as b:
                nb = pe.snap(b + 1)
                pe.wait_ge(XT_in, 16 * nb)
                turned = pe.snap(pe.to_reg(HB * b + 1))
                pe.wait_ge(pc, 1)
                for p in range(2):
                    pe.wait_ge(Tl_ok[p], turned)
                with pe.Fori(0, HB) as h:
                    m = pe.snap(b * HB + h + 1)
                    for p in range(2):
                        pe.wait_ge(L_ok[p], m)
                        for j in range(2):
                            c = 0
                            for k in range(KD):
                                for sx, ss in parts3:
                                    last = pe.matmul(lg[p][:, j * 512:(j + 1) * 512],
                                                     XT[:, sx * KD + k, bass.ds(h * 2 * P + p * P, P)],
                                                     seT[:, ss, k, j * 512:(j + 1) * 512],
                                                     start=(c == 0), stop=(c == 3 * KD - 1))
                                    c += 1
                        last.then_inc(lg_ps[p], 1)
                pe.wait_ge(cm_ok, (NT + 1) * nb)
                for p in range(2):
                    pe.wait_ge(o_ok[p], HB * b + 1)
                for e in range(NS):
                    last = pe.transpose(wide[2][:, e * P:(e + 1) * P], cmax[:, e * P:(e + 1) * P], ident[:, :])
                last.then_inc(cT_ps, 1)
                pe.wait_ge(mcs_ok, nb)
                for e in range(NS):
                    last = pe.transpose(wide[3][:, e * P:(e + 1) * P], mcs[:, e:e + 1].broadcast_to([P, P]),
                                        ident[:, :])
                last.then_inc(Mb_ps, 1)
                arrived = pe.snap(pe.to_reg(32 * NT * nb))
                pe.wait_ge(pc, 1)
                pe.wait_ge(X_in, arrived)
                with pe.Fori(0, 2) as v:
                    s = pe.snap(2 * b + v)
                    pe.wait_ge(sl_ok, s + 1)
                    for p in range(2):
                        pe.wait_ge(L_ok[p], HB * nb + 1)
                    for q in range(QS):
                        pe.matmul(acc[q], zero16[:, 0:P], zero16[:, :], start=True, stop=False)
                    with pe.Fori(0, HB) as h:
                        for p in range(2):
                            n = s * HB + h + 1
                            pe.wait_ge(El_ok[p], n + 1)
                            j = 2 * h + p
                            for q in range(QS):
                                qs = slice(q * P, (q + 1) * P)
                                for e, sx in ((Eh, 0), (Eh, 1), (El, 0)):
                                    last = pe.matmul(acc[q], e[p][:, qs],
                                                     X[:, sx, bass.ds(j, 1), 0:XW].rearrange("q a n -> q (a n)"),
                                                     start=False, stop=False)
                            last.then_inc(B_ps[p], 1)
                    for q in range(QS):
                        last = pe.matmul(acc[q], zero16[:, 0:P], zero16[:, :], start=False, stop=True)
                    last.then_inc(acc_ps, 1)
                    pe.wait_ge(sl_ok, s + 2)
                    pe.wait_ge(Pl_ok[1], s * (QS // 2) + 1)
                    for k in range(KD):
                        for q in range(QS):
                            last = pe.transpose(wide[2][:, (k * QS + q) * P:(k * QS + q + 1) * P],
                                                sl[:, q, k * P:(k + 1) * P], ident[:, :])
                    last.then_inc(sT_ps, 1)
                    pe.wait_ge(sTl_ok, s + 1)
                    sT = (sTh, sTl)
                    for f in range(NF):
                        if f >= 2:
                            pe.wait_ge(hf_ok[f % 2], s * (NF // 2) + f // 2)
                        c = 0
                        for k in range(KD):
                            for sw, ss in parts3:
                                last = pe.matmul(up[f % 2], w1s[:, sw, k, f * P:(f + 1) * P], sT[ss][:, k, :],
                                                 start=(c == 0), stop=(c == 3 * KD - 1))
                                c += 1
                        last.then_inc(up_ps[f % 2], 1)
                    for p in range(2):
                        pe.wait_ge(hl_ok[p], (s + 1) * (NF // 2) + 1)
                    hT = (hh, hl)
                    for q in range(QS):
                        if q >= 2:
                            pe.wait_ge(Pl_ok[q % 2], s * (QS // 2) + q // 2 + 1)
                        c = 0
                        for f in range(NF):
                            for sh, sw in parts3:
                                last = pe.matmul(down[q % 2], hT[sh][:, f, q * P:(q + 1) * P], w2s[:, sw, f, :],
                                                 start=(c == 0), stop=(c == 3 * NF - 1))
                                c += 1
                        last.then_inc(dn_ps[q % 2], 1)

                def turn(h, p):
                    n = b * HB + h + 1
                    pe.wait_ge(Ec_ok[p], n)
                    pe.wait_ge(Tl_ok[p], n)
                    for e in range(NS):
                        last = pe.transpose(tp[p][:, e * P:(e + 1) * P], Ec[p][:, e * P:(e + 1) * P], ident[:, :])
                    last.then_inc(tp_ps[p], 1)

                def combine(h, p):
                    n = b * HB + h + 1
                    pe.wait_ge(Tl_ok[p], n + 1)
                    pe.wait_ge(o_ok[p], n)
                    c = 0
                    for e in range(NS):
                        es = slice(e * P, (e + 1) * P)
                        for a, pp in ((Th, Ph), (Th, Pl), (Tl, Ph)):
                            last = pe.matmul(co[p], a[p][:, es], pp[:, e, 0:XW], start=(c == 0),
                                             stop=(c == 3 * NS - 1))
                            c += 1
                    last.then_inc(co_ps[p], 1)

                pe.wait_ge(Pl_ok[0], (nb * QS) + 1)
                pe.wait_ge(Pl_ok[1], (nb * QS) + 1)
                turn(0, 0)
                with pe.Fori(0, HB - 1) as h:
                    turn(h, 1)
                    combine(h, 0)
                    turn(h + 1, 0)
                    combine(h, 1)
                turn(HB - 1, 1)
                combine(HB - 1, 0)
                combine(HB - 1, 1)



def build(nc, io, out):
    with ExitStack() as ctx:
        x1_dram = nc.dram_tensor("x1_dram", (B, T, D), F32, kind="Internal").ap()
        X_dram = nc.dram_tensor("X_dram", (2, B, T, D), F16, kind="Internal").ap()
        XT_dram = nc.dram_tensor("XT_dram", (P, 2 * KD, B, T), F16, kind="Internal").ap()
        attention(nc, io, x1_dram, X_dram, XT_dram)
        moe(nc, io, x1_dram, X_dram, XT_dram, out)


_INS = ["L0_attn_x", "L0_attn_Wq", "L0_attn_bq", "L0_attn_Wk", "L0_attn_bk", "L0_attn_Wv", "L0_attn_bv",
        "L0_attn_Wa", "L0_attn_ba", "L0_attn_Wb", "L0_attn_bb", "L0_attn_Wg", "L0_attn_bg", "L0_attn_Wo",
        "L0_attn_bo", "L0_ffn_gamma_x", "L0_ffn_gamma_slot", "L0_ffn_slot_embeds", "L0_ffn_w1", "L0_ffn_w2"]


def kernel(**inputs):
    import numpy as _np
    import concourse.bacc as _bacc
    from concourse import mybir as _mybir
    from concourse.bass_utils import run_bass_kernel_spmd as _run

    nc = _bacc.Bacc("TRN2", target_bir_lowering=False, num_devices=1)
    arrays, io = {}, {}
    for name in _INS + ["const"]:
        a = _np.ascontiguousarray(constants() if name == "const" else inputs[name])
        arrays[f"in_{name}_dram"] = a
        io[name] = nc.dram_tensor(f"in_{name}_dram", a.shape, _mybir.dt.from_np(a.dtype), kind="ExternalInput").ap()
    out = nc.dram_tensor("out_0_dram", (B, T, D), F32, kind="ExternalOutput").ap()
    build(nc, io, out)
    r = _run(nc, [arrays], core_ids=[0])
    return r.results[0]["out_0_dram"]
```

```python
import math
from contextlib import ExitStack

import concourse.bass as bass
import numpy as np
from concourse import mybir

F32 = mybir.dt.float32
F16 = mybir.dt.float16
ALU = mybir.AluOpType
ACT = mybir.ActivationFunctionType
AX = mybir.AxisListType

P = 128
B = 4
T = 2048
D = 256
C = 128
KD = D // P
NCH = T // P
NG = 2
GB = B // NG
NL = 7
KVW = 2 * C + 2
LN_EPS = 1e-5
RMS_GUARD = 1e-24 / D
NORM_EPS2 = 1e-24

C_ID, C_MASK = 0, P
CONSTW = P * (1 + NL)


def constants():
    s, t = np.arange(P)[:, None], np.arange(P)[None, :]
    parts = [np.eye(P)]
    for l in range(NL):
        h = 1 << l
        m = (s // (2 * h) == t // (2 * h)) & (s // h % 2 == 0) & (t // h % 2 == 1)
        parts.append(m * (-1.0 if l == 0 else 1.0))
    return np.concatenate([np.asarray(p, np.float32) for p in parts], axis=1)


def attention(nc, io, x1_dram, X_dram, XT_dram):
    held = []
    with ExitStack() as ctx:
        def sb(name, shape, dt=F32):
            return ctx.enter_context(nc.sbuf_tensor(name, shape, dt))

        def per_group(name, shape, dt=F32):
            return [sb(f"{name}{g}", shape, dt) for g in range(NG)]

        def by_parity(name, shape, dt=F32):
            return [per_group(f"{name}_{q}_", shape, dt) for q in range(2)]

        def sem(name):
            held.append(ctx.enter_context(nc.semaphore("a_" + name)))
            return held[-1]

        def sems(name):
            return [sem(f"{name}{g}") for g in range(NG)]

        const = sb("a_const", [P, CONSTW])
        ident = const[:, C_ID:C_ID + P]
        ident16 = sb("a_ident16", [P, P], F16)
        wkv = sb("wkv", [P, KD, KVW])
        wqg = sb("wqg", [P, KD, 2 * C])
        wo = sb("wo", [P, D])
        bkv = sb("bkv", [P, KVW])
        bq = sb("bq", [P, 1])
        bg = sb("bg", [P, 1])
        bo = sb("bo", [P, D])
        neg_half = sb("a_neg_half", [P, GB])
        ln_eps = sb("a_ln_eps", [P, GB])
        zeros = sb("a_zeros", [P, P])
        table = sb("a_table", [P, 1])

        x = per_group("x", [P, GB, D])
        xres = by_parity("xres", [P, GB, D])
        stats = per_group("stats", [P, GB, 6])
        mv = per_group("mv", [P, GB, 2])
        rstd = per_group("rstd", [P, GB])
        xn = per_group("xn", [P, GB, D])
        xnT = per_group("xnT", [P, KD, GB, P])
        kvab = by_parity("kvab", [P, GB, KVW])
        qT = by_parity("qT", [P, GB, P])
        qTg = by_parity("qTg", [P, GB, P])
        gateT = by_parity("gateT", [P, GB, P])
        ab = by_parity("ab", [P, GB, 2])
        junk = per_group("junk", [P, GB, C])
        kn2 = per_group("kn2", [P, GB])
        krn = per_group("krn", [P, GB])
        kh = by_parity("kh", [P, GB, C])
        khd = by_parity("khd", [P, GB, C])
        kT = per_group("kT", [P, GB, P])
        kTg = by_parity("kTg", [P, GB, P])
        gam = by_parity("gam", [P, GB, P])
        gbc = by_parity("gbc", [P, GB, P])
        M = per_group("M", [P, GB, P])
        moff = per_group("moff", [P, NL, GB, P])
        Z = by_parity("Z", [P, GB, P])
        ZT = per_group("ZT", [P, GB, P])
        P1T = per_group("P1T", [P, GB, P])
        X0 = per_group("X0", [P, GB, C])
        S = per_group("S", [P, GB, C])
        R = per_group("R", [P, GB, C])
        U = per_group("U", [P, GB, C])
        UT = per_group("UT", [P, GB, P])
        PT = per_group("PT", [P, GB, P])
        OT = per_group("OT", [P, GB, P])
        x1 = per_group("x1", [P, GB, D])
        stats2 = per_group("stats2", [P, GB, 6])
        mv2 = per_group("mv2", [P, GB, 2])
        guard = per_group("guard", [P, GB])
        var2 = per_group("var2", [P, GB])
        rvar = per_group("rvar", [P, GB])
        xf = per_group("xf", [P, GB, D])
        Xh = per_group("Xh", [P, GB, D], F16)
        Xl = per_group("Xl", [P, GB, D], F16)
        XT = per_group("XT", [P, 2, KD, GB, P], F16)
        bank = [[ctx.enter_context(nc.psum_tensor(f"a_bank{g}{n}", [P, 512], F32)) for n in range(4)]
                for g in range(NG)]

        def half(g, n, h=0):
            return bank[g][n][:, h * GB * P:(h + 1) * GB * P].rearrange("p (b t) -> p b t", b=GB)

        consts_in, cols_in, pool_consts, dve_consts = (
            sem("consts_in"), sem("cols_in"), sem("pool_consts"), sem("dve_consts"))
        (x_in, xres_ok, stats_ok, mv_ok, rstd_a, rstd_ok, xn_ok, xnT_ps, xnT_ok, kv_ps, kv_ok, qg_ps,
         qg_ok, ab_ok, kn_ok, krn_a, krn_ok, kh_ok, abc_ps, kT_ps, kT_ok, gam_ok, gbc_ok, scaled_ok, khd_ok,
         kk_ps, M_ok, z_half, moff_ok, ZT_ps, ZT_ok, P1T_ps, P1T_ok, Z_ps, Z_ok, kr_ps, X0_ok, S_ok,
         U_ps, U_ok, R_ps, R_ok, UT_ps, UT_ok, sc_ps, PT_ok, OT_ps, OT_ok, y_ps, x1_ok, x1_out,
         stats2_ok, mv2_ok, guard_ok, var2_ok, rvar_ok, xf_ok, Xh_ok, Xl_ok, XT_ps, XT_ok, X_out) = [
            sems(n) for n in (
                "x_in xres_ok stats_ok mv_ok rstd_a rstd_ok xn_ok xnT_ps xnT_ok kv_ps kv_ok qg_ps "
                "qg_ok ab_ok kn_ok krn_a krn_ok kh_ok abc_ps kT_ps kT_ok gam_ok gbc_ok scaled_ok khd_ok "
                "kk_ps M_ok z_half moff_ok ZT_ps ZT_ok P1T_ps P1T_ok Z_ps Z_ok kr_ps X0_ok S_ok "
                "U_ps U_ok R_ps R_ok UT_ps UT_ok sc_ps PT_ok OT_ps OT_ok y_ps x1_ok x1_out "
                "stats2_ok mv2_ok guard_ok var2_ok rvar_ok xf_ok Xh_ok Xl_ok XT_ps XT_ok X_out").split()]
        N_CONSTS = 13 * 16
        work = ExitStack()
        block = work.enter_context(nc.Block())

        def rounds(eng, body):
            with eng.Fori(0, NCH // 2 - 1) as j:
                for q in range(2):
                    body(eng.snap(2 * j + q), q)

        @block.sync
        def _(sp):
            def bcast(v, n):
                return v.rearrange("(a n) -> a n", a=1).broadcast_to([P, n])

            for dst, src in (
                (const[:, :], io["const"]),
                (wkv[:, :, 0:C], io["L0_attn_Wk"].rearrange("(k p) n -> p k n", p=P)),
                (wkv[:, :, C:2 * C], io["L0_attn_Wv"].rearrange("(k p) n -> p k n", p=P)),
                (wkv[:, :, 2 * C:2 * C + 1], io["L0_attn_Wa"].rearrange("(k p) n -> p k n", p=P)),
                (wkv[:, :, 2 * C + 1:], io["L0_attn_Wb"].rearrange("(k p) n -> p k n", p=P)),
                (wqg[:, :, 0:C], io["L0_attn_Wq"].rearrange("(k p) n -> p k n", p=P)),
                (wqg[:, :, C:], io["L0_attn_Wg"].rearrange("(k p) n -> p k n", p=P)),
                (wo[:, :], io["L0_attn_Wo"]),
                (bkv[:, 0:C], bcast(io["L0_attn_bk"], C)),
                (bkv[:, C:2 * C], bcast(io["L0_attn_bv"], C)),
                (bkv[:, 2 * C:2 * C + 1], bcast(io["L0_attn_ba"], 1)),
                (bkv[:, 2 * C + 1:], bcast(io["L0_attn_bb"], 1)),
                (bo[:, :], bcast(io["L0_attn_bo"], D)),
            ):
                sp.dma_start(dst, src, allow_slow_non_contiguous=True).then_inc(consts_in, 16)

            def load(c):
                for g in range(NG):
                    if not isinstance(c, int) or c > 0:
                        sp.wait_ge(xn_ok[g], c)
                        sp.wait_ge(xres_ok[g], c)
                    sp.dma_start(x[g][:, :, :], io["L0_attn_x"][g * GB:(g + 1) * GB, bass.ds(c * P, P), :]
                                 .rearrange("b p d -> p b d")).then_inc(x_in[g], 16)

            def store_parts(c):
                n = c + 1
                for g in range(NG):
                    gb = slice(g * GB, (g + 1) * GB)
                    sp.wait_ge(Xh_ok[g], n)
                    sp.dma_start(X_dram[0, gb, bass.ds(c * P, P), :].rearrange("b p d -> p b d"),
                                 Xh[g][:, :, :]).then_inc(X_out[g], 16)
                    sp.wait_ge(Xl_ok[g], n)
                    sp.dma_start(X_dram[1, gb, bass.ds(c * P, P), :].rearrange("b p d -> p b d"),
                                 Xl[g][:, :, :]).then_inc(X_out[g], 16)
                    sp.wait_ge(consts_in, N_CONSTS)
                    sp.wait_ge(XT_ok[g], c + 2)
                    sp.dma_start(XT_dram[:, :, gb, bass.ds(c * P, P)],
                                 XT[g][:, :, :, :, :].rearrange("p s k b t -> p (s k) b t")).then_inc(X_out[g], 16)

            load(0)
            load(1)

            def body(c, q):
                load(c + 2)
                store_parts(c)

            rounds(sp, body)
            store_parts(NCH - 2)
            store_parts(NCH - 1)

        @block.gpsimd
        def _(pool):
            pool.dma_start(bq[:, :], io["L0_attn_bq"].rearrange("(p n) -> p n", n=1),
                           allow_slow_non_contiguous=True).then_inc(cols_in, 16)
            pool.dma_start(bg[:, :], io["L0_attn_bg"].rearrange("(p n) -> p n", n=1),
                           allow_slow_non_contiguous=True).then_inc(cols_in, 16)
            pool.memset(ln_eps[:, :], LN_EPS)
            pool.memset(neg_half[:, :], -0.5).then_inc(pool_consts, 1)
            pool.wait_ge(pool_consts, 1)
            pool.wait_ge(consts_in, N_CONSTS)

            def norm(c, q):
                n = c + 1
                for g in range(NG):
                    pool.wait_ge(mv_ok[g], n)
                    pool.tensor_tensor(rstd[g][:, :], mv[g][:, :, 1], ln_eps[:, :], ALU.add).then_inc(rstd_a[g], 1)
                    pool.wait_ge(rstd_a[g], n)
                    pool.tensor_tensor(rstd[g][:, :], rstd[g][:, :], neg_half[:, :], ALU.pow).then_inc(rstd_ok[g], 1)
                for g in range(NG):
                    pool.wait_ge(x_in[g], 16 * n)
                    if not isinstance(c, int):
                        pool.wait_ge(x1_ok[g], c)
                    pool.tensor_tensor(xres[q][g][:, :, :], x[g][:, :, :],
                                       bo[:, :].rearrange("p (a d) -> p a d", a=1).broadcast_to([P, GB, D]),
                                       ALU.add).then_inc(xres_ok[g], 1)

            def keys(c, q):
                n = c + 1 if isinstance(c, int) else pool.snap(pool.to_reg(c + 1))
                for g in range(NG):
                    pool.wait_ge(pool_consts, 1)
                    pool.wait_ge(kn_ok[g], n)
                    pool.tensor_scalar(krn[g][:, :], kn2[g][:, :], NORM_EPS2, None, ALU.max).then_inc(krn_a[g], 1)
                    pool.wait_ge(krn_a[g], n)
                    pool.tensor_tensor(krn[g][:, :], krn[g][:, :], neg_half[:, :], ALU.pow).then_inc(krn_ok[g], 1)

            def first_doubling(c, q):
                n = c + 1
                for g in range(NG):
                    pool.wait_ge(M_ok[g], n)
                    m0 = const[:, C_MASK:C_MASK + P].rearrange("p (a t) -> p a t", a=1).broadcast_to([P, GB, P])
                    pool.tensor_tensor(moff[g][:, 0], M[g][:, :, :], m0, ALU.mult).then_inc(z_half[g], 1)
                    pool.wait_ge(z_half[g], n)
                    pool.tensor_tensor(Z[q][g][:, :, :], moff[g][:, 0],
                                       ident.rearrange("p (a t) -> p a t", a=1).broadcast_to([P, GB, P]),
                                       ALU.add).then_inc(moff_ok[g], 1)

            def cut(l):
                for g in range(NG):
                    ml = const[:, C_MASK + l * P:C_MASK + (l + 1) * P]
                    pool.tensor_tensor(moff[g][:, l], M[g][:, :, :],
                                       ml.rearrange("p (a t) -> p a t", a=1).broadcast_to([P, GB, P]),
                                       ALU.mult).then_inc(moff_ok[g], 1)

            def decayed(c, q):
                n = c + 1
                for g in range(NG):
                    pool.wait_ge(gbc_ok[g], n)
                    pool.wait_ge(kT_ok[g], n)
                    pool.tensor_tensor(kTg[q][g][:, :, :], kT[g][:, :, :], gbc[q][g][:, :, :], ALU.mult)
                    pool.wait_ge(qg_ok[g], n)
                    pool.tensor_tensor(qTg[q][g][:, :, :], qT[q][g][:, :, :], gbc[q][g][:, :, :], ALU.mult)\
                        .then_inc(scaled_ok[g], 1)

            def local(c, q):
                keys(c, q)
                first_doubling(c, q)
                for l in range(1, NL):
                    cut(l)
                decayed(c, q)

            def outputs(c, q):
                for g in range(NG):
                    pool.wait_ge(var2_ok[g], c + 1)
                    pool.tensor_tensor(rvar[g][:, :], var2[g][:, :], neg_half[:, :], ALU.pow).then_inc(rvar_ok[g], 1)

            def body(c, q):
                d, r = c + 1, 1 - q
                keys(d, r)
                first_doubling(d, r)
                for l in range(1, 5):
                    cut(l)
                norm(c + 2, q)
                for l in range(5, NL):
                    cut(l)
                outputs(c, q)
                decayed(d, r)

            norm(0, 0)
            local(0, 0)
            norm(1, 1)
            rounds(pool, body)
            local(NCH - 1, 1)
            outputs(NCH - 2, 0)
            outputs(NCH - 1, 1)

        @block.vector
        def _(dve):
            dve.wait_ge(consts_in, N_CONSTS)
            dve.tensor_copy(ident16[:, :], ident)
            dve.memset(zeros[:, :], 0.0).then_inc(dve_consts, 1)
            for g in range(NG):
                dve.memset(R[g][:, :, :], 0.0).then_inc(R_ok[g], 1)
                dve.sem_inc(x1_ok[g], 1)
            dve.wait_ge(dve_consts, 1)

            def norm(c, q):
                n = dve.snap(dve.to_reg(c + 1)) if not isinstance(c, int) else c + 1
                for g in range(NG):
                    dve.wait_ge(x_in[g], 16 * n)
                    for b in range(GB):
                        last = dve.bn_stats(stats[g][:, b, :], x[g][:, b, :])
                    last.then_inc(stats_ok[g], 1)
                    dve.wait_ge(dve_consts, 1)
                    dve.wait_ge(stats_ok[g], n)
                    for b in range(GB):
                        last = dve.bn_aggr(mv[g][:, b, :], stats[g][:, b, :])
                    last.then_inc(mv_ok[g], 1)

            def norm_end(c, q):
                for g in range(NG):
                    dve.wait_ge(rstd_ok[g], c + 1)
                    for b in range(GB):
                        last = dve.tensor_scalar(xn[g][:, b, :], x[g][:, b, :], mv[g][:, b, 0:1],
                                                 rstd[g][:, b:b + 1], ALU.subtract, ALU.mult)
                    last.then_inc(xn_ok[g], 1)

            def biases(c, q):
                for g in range(NG):
                    dve.wait_ge(kv_ps[g], c + 1)
                    for b in range(GB):
                        last = dve.tensor_tensor(kvab[q][g][:, b, :], bank[g][1 - b][:, 0:KVW], bkv[:, :], ALU.add)
                    last.then_inc(kv_ok[g], 1)

            def keys(c, q):
                for g in range(NG):
                    dve.wait_ge(krn_ok[g], c + 1)
                    for b in range(GB):
                        last = dve.tensor_scalar(kh[q][g][:, b, :], kvab[q][g][:, b, 0:C], krn[g][:, b:b + 1], None,
                                                 ALU.mult)
                    last.then_inc(kh_ok[g], 1)

            def decays(c, q):
                for g in range(NG):
                    dve.wait_ge(abc_ps[g], c + 1)
                    for b in range(GB):
                        last = dve.tensor_tensor_scan(gam[q][g][:, b, :], half(g, 0)[:, b, :], ident, 0.0,
                                                      ALU.mult, ALU.add)
                    last.then_inc(gam_ok[g], 1)
                    for b in range(GB):
                        last = dve.tensor_tensor_scan(gbc[q][g][:, b, :], half(g, 0)[:, b, :], zeros[:, :], 1.0,
                                                      ALU.mult, ALU.add)
                    last.then_inc(gbc_ok[g], 1)

            def decayed(c, q):
                for g in range(NG):
                    dve.wait_ge(gam_ok[g], c + 1)
                    for b in range(GB):
                        last = dve.tensor_scalar(khd[q][g][:, b, :], kh[q][g][:, b, :], gam[q][g][:, b, P - 1:P], None,
                                                 ALU.mult)
                    last.then_inc(khd_ok[g], 1)

            def system(c, q):
                for g in range(NG):
                    dve.wait_ge(kk_ps[g], c + 1)
                    for b in range(GB):
                        last = dve.scalar_tensor_tensor(M[g][:, b, :], half(g, 0)[:, b, :], ab[q][g][:, b, 1:2],
                                                        gam[q][g][:, b, :], ALU.mult, ALU.mult)
                    last.then_inc(M_ok[g], 1)

            def doubling(c, q, l):
                for g in range(NG):
                    dve.wait_ge(Z_ps[g], (NL - 1) * c + l)
                    dve.tensor_tensor(Z[q][g][:, :, :], Z[q][g][:, :, :], half(g, 1), ALU.subtract)\
                        .then_inc(Z_ok[g], 1)

            def right_side(c, q):
                for g in range(NG):
                    dve.wait_ge(kr_ps[g], c + 1)
                    dve.tensor_tensor(X0[g][:, :, :], kvab[q][g][:, :, C:2 * C], half(g, 2, 0), ALU.subtract)\
                        .then_inc(X0_ok[g], 1)
                    dve.tensor_copy(S[g][:, :, :], half(g, 2, 1)).then_inc(S_ok[g], 1)

            def next_state(c, q):
                for g in range(NG):
                    dve.wait_ge(R_ps[g], c + 1)
                    for b in range(GB):
                        last = dve.scalar_tensor_tensor(R[g][:, b, :], R[g][:, b, :], gbc[q][g][:, b, P - 1:P],
                                                        half(g, 2)[:, b, :], ALU.mult, ALU.add)
                    last.then_inc(R_ok[g], 1)

            def weights(c, q):
                for g in range(NG):
                    dve.wait_ge(sc_ps[g], c + 1)
                    dve.tensor_tensor(PT[g][:, :, :], half(g, 2), gam[q][g][:, :, :], ALU.mult).then_inc(PT_ok[g], 1)

            def gated(c, q):
                for g in range(NG):
                    dve.wait_ge(OT_ps[g], c + 1)
                    dve.tensor_tensor(OT[g][:, :, :], half(g, 3), gateT[q][g][:, :, :], ALU.mult)\
                        .then_inc(OT_ok[g], 1)

            def residual(c, q):
                for g in range(NG):
                    dve.wait_ge(y_ps[g], c + 1)
                    dve.wait_ge(xres_ok[g], c + 1)
                    dve.wait_ge(x1_out[g], 16 * c + 16)
                    dve.tensor_tensor(x1[g][:, :, :], xres[q][g][:, :, :],
                                      bank[g][2][:, :].rearrange("p (b d) -> p b d", b=GB), ALU.add)\
                        .then_inc(x1_ok[g], 1)

            def statistics(c, q):
                n = dve.snap(dve.to_reg(c + 1)) if not isinstance(c, int) else c + 1
                for g in range(NG):
                    dve.wait_ge(x1_ok[g], n + 1)
                    for b in range(GB):
                        last = dve.bn_stats(stats2[g][:, b, :], x1[g][:, b, :])
                    last.then_inc(stats2_ok[g], 1)
                for g in range(NG):
                    dve.wait_ge(dve_consts, 1)
                    dve.wait_ge(stats2_ok[g], n)
                    for b in range(GB):
                        last = dve.bn_aggr(mv2[g][:, b, :], stats2[g][:, b, :])
                    last.then_inc(mv2_ok[g], 1)
                for g in range(NG):
                    dve.wait_ge(mv2_ok[g], n)
                    dve.tensor_scalar(guard[g][:, :], mv2[g][:, :, 1], RMS_GUARD, RMS_GUARD * LN_EPS,
                                      ALU.mult, ALU.add).then_inc(guard_ok[g], 1)
                for g in range(NG):
                    dve.wait_ge(guard_ok[g], n)
                    dve.tensor_tensor(var2[g][:, :], mv2[g][:, :, 1], guard[g][:, :], ALU.max).then_inc(var2_ok[g], 1)

            def normalised(c, q):
                for g in range(NG):
                    dve.wait_ge(rvar_ok[g], c + 1)
                    for b in range(GB):
                        last = dve.tensor_scalar(xf[g][:, b, :], x1[g][:, b, :], mv2[g][:, b, 0:1],
                                                 rvar[g][:, b:b + 1], ALU.subtract, ALU.mult)
                    last.then_inc(xf_ok[g], 1)

            def low_part(c, q):
                for g in range(NG):
                    dve.wait_ge(Xh_ok[g], c + 1)
                    dve.wait_ge(X_out[g], 48 * c + 48)
                    dve.tensor_tensor(Xl[g][:, :, :], xf[g][:, :, :], Xh[g][:, :, :], ALU.subtract)\
                        .then_inc(Xl_ok[g], 1)

            def local(c, q):
                biases(c, q)
                keys(c, q)
                decays(c, q)
                system(c, q)
                decayed(c, q)
                for l in range(1, NL):
                    doubling(c, q, l)

            def state(c, q):
                right_side(c, q)
                next_state(c, q)
                weights(c, q)
                gated(c, q)
                residual(c, q)
                statistics(c, q)
                normalised(c, q)
                low_part(c, q)

            def both(c, q, norm_too):
                d, r = c + 1, 1 - q
                right_side(c, q)
                biases(d, r)
                keys(d, r)
                decays(d, r)
                system(d, r)
                decayed(d, r)
                next_state(c, q)
                doubling(d, r, 1)
                weights(c, q)
                doubling(d, r, 2)
                gated(c, q)
                doubling(d, r, 3)
                if norm_too:
                    norm(c + 2, q)
                residual(c, q)
                doubling(d, r, 4)
                statistics(c, q)
                doubling(d, r, 5)
                if norm_too:
                    norm_end(c + 2, q)
                normalised(c, q)
                doubling(d, r, 6)
                low_part(c, q)

            norm(0, 0)
            norm_end(0, 0)
            local(0, 0)
            norm(1, 1)
            norm_end(1, 1)
            rounds(dve, lambda c, q: both(c, q, True))
            both(NCH - 2, 0, False)
            state(NCH - 1, 1)

        @block.scalar
        def _(act):
            act.wait_ge(cols_in, 32)
            for g in range(NG):
                act.sem_inc(x1_out[g], 16)
                act.sem_inc(X_out[g], 48)
                act.sem_inc(XT_ok[g], 1)
            act.wait_ge(dve_consts, 1)
            act.activation(table[:, :], zeros[:, 0:1], ACT.Sigmoid)

            def turned_x(c, q):
                for g in range(NG):
                    act.wait_ge(xnT_ps[g], c + 1)
                    act.copy(xnT[g][:, :, :, :].rearrange("p k b t -> p (k b t)"), bank[g][0][:, :])\
                        .then_inc(xnT_ok[g], 1)

            def key_norms(c, q):
                for g in range(NG):
                    act.wait_ge(kv_ok[g], c + 1)
                    for b in range(GB):
                        last = act.activation(junk[g][:, b, :], kvab[q][g][:, b, 0:C], ACT.Square,
                                              accum_out=kn2[g][:, b:b + 1])
                    last.then_inc(kn_ok[g], 1)
                    act.activation(ab[q][g][:, :, :], kvab[q][g][:, :, 2 * C:], ACT.Sigmoid).then_inc(ab_ok[g], 1)

            def queries(c, q):
                for g in range(NG):
                    act.wait_ge(qg_ps[g], c + 1)
                    act.activation(qT[q][g][:, :, :], half(g, 1, 0), ACT.Identity, bias=bq[:, 0:1])
                    act.activation(gateT[q][g][:, :, :], half(g, 1, 1), ACT.Sigmoid, bias=bg[:, 0:1])\
                        .then_inc(qg_ok[g], 1)

            def turned_keys(c, q):
                for g in range(NG):
                    act.wait_ge(kT_ps[g], c + 1)
                    act.copy(kT[g][:, :, :], half(g, 1)).then_inc(kT_ok[g], 1)

            def doubling(c, q, l):
                for g in range(NG):
                    act.wait_ge(ZT_ps[g], (NL - 1) * c + l)
                    act.copy(ZT[g][:, :, :], half(g, 1)).then_inc(ZT_ok[g], 1)
                for g in range(NG):
                    act.wait_ge(P1T_ps[g], (NL - 1) * c + l)
                    act.copy(P1T[g][:, :, :], half(g, 0)).then_inc(P1T_ok[g], 1)

            def updates(c, q):
                for g in range(NG):
                    act.wait_ge(U_ps[g], c + 1)
                    for b in range(GB):
                        last = act.activation(U[g][:, b, :], half(g, 3)[:, b, :], ACT.Identity,
                                              scale=ab[q][g][:, b, 1:2])
                    last.then_inc(U_ok[g], 1)

            def turned_updates(c, q):
                for g in range(NG):
                    act.wait_ge(UT_ps[g], c + 1)
                    act.copy(UT[g][:, :, :], half(g, 3)).then_inc(UT_ok[g], 1)

            def store(c, q):
                for g in range(NG):
                    act.wait_ge(x1_ok[g], c + 2)
                    act.dma_start(x1_dram[g * GB:(g + 1) * GB, bass.ds(c * P, P), :].rearrange("b p d -> p b d"),
                                  x1[g][:, :, :]).then_inc(x1_out[g], 16)

            def high_part(c, q):
                for g in range(NG):
                    act.wait_ge(xf_ok[g], c + 1)
                    act.wait_ge(X_out[g], 48 * c + 48)
                    act.copy(Xh[g][:, :, :], xf[g][:, :, :]).then_inc(Xh_ok[g], 1)

            def turned_parts(c, q):
                for g in range(NG):
                    act.wait_ge(XT_ps[g], c + 1)
                    act.copy(XT[g][:, :, :, :, :].rearrange("p s k b t -> p (s k b t)"),
                             bank[g][3][:, :].bitcast(F16)).then_inc(XT_ok[g], 1)

            def both(c, q):
                d, r = c + 1, 1 - q
                turned_x(d, r)
                updates(c, q)
                key_norms(d, r)
                queries(d, r)
                turned_keys(d, r)
                doubling(d, r, 1)
                turned_updates(c, q)
                for l in range(2, 5):
                    doubling(d, r, l)
                store(c, q)
                doubling(d, r, 5)
                doubling(d, r, 6)
                high_part(c, q)
                turned_parts(c, q)

            turned_x(0, 0)
            key_norms(0, 0)
            queries(0, 0)
            turned_keys(0, 0)
            for l in range(1, NL):
                doubling(0, 0, l)
            rounds(act, both)
            both(NCH - 2, 0)
            updates(NCH - 1, 1)
            turned_updates(NCH - 1, 1)
            store(NCH - 1, 1)
            high_part(NCH - 1, 1)
            turned_parts(NCH - 1, 1)
            for g in range(NG):
                act.wait_ge(x1_out[g], 16 * NCH + 16)
                act.wait_ge(X_out[g], 48 * NCH + 48)

        @block.tensor
        def _(pe):
            pe.wait_ge(consts_in, N_CONSTS)
            pe.wait_ge(dve_consts, 1)

            def turn_x(c, q):
                for g in range(NG):
                    pe.wait_ge(xn_ok[g], c + 1)
                    for k in range(KD):
                        for b in range(GB):
                            at = (k * GB + b) * P
                            last = pe.transpose(bank[g][0][:, at:at + P], xn[g][:, b, k * P:(k + 1) * P], ident)
                    last.then_inc(xnT_ps[g], 1)

            def keys_values(c, q):
                for g in range(NG):
                    pe.wait_ge(xnT_ok[g], c + 1)
                    if not isinstance(c, int) or c > 0:
                        pe.wait_ge(Z_ok[g], (NL - 1) * c)
                    for b in range(GB):
                        for k in range(KD):
                            last = pe.matmul(bank[g][1 - b][:, 0:KVW], xnT[g][:, k, b, :], wkv[:, k, :],
                                             start=(k == 0), stop=(k == KD - 1))
                    last.then_inc(kv_ps[g], 1)

            def queries_gates(c, q):
                for g in range(NG):
                    pe.wait_ge(kv_ok[g], c + 1)
                    for h in range(2):
                        for k in range(KD):
                            last = pe.matmul(half(g, 1, h).rearrange("p b t -> p (b t)"),
                                             wqg[:, k, h * C:(h + 1) * C],
                                             xnT[g][:, k].rearrange("p b t -> p (b t)"),
                                             start=(k == 0), stop=(k == KD - 1))
                    last.then_inc(qg_ps[g], 1)

            def spread_alpha(c, q):
                for g in range(NG):
                    pe.wait_ge(ab_ok[g], c + 1)
                    for b in range(GB):
                        last = pe.transpose(half(g, 0)[:, b, :], ab[q][g][:, b, 0:1].broadcast_to([P, P]), ident)
                    last.then_inc(abc_ps[g], 1)

            def turn_keys(c, q):
                for g in range(NG):
                    pe.wait_ge(kh_ok[g], c + 1)
                    pe.wait_ge(qg_ok[g], c + 1)
                    for b in range(GB):
                        last = pe.transpose(half(g, 1)[:, b, :], kh[q][g][:, b, :], ident)
                    last.then_inc(kT_ps[g], 1)

            def system(c, q):
                for g in range(NG):
                    pe.wait_ge(kT_ok[g], c + 1)
                    pe.wait_ge(gbc_ok[g], c + 1)
                    for b in range(GB):
                        last = pe.matmul(half(g, 0)[:, b, :], kT[g][:, b, :], kT[g][:, b, :], start=True, stop=True)
                    last.then_inc(kk_ps[g], 1)

            def doubling(c, q, l, beside=None):
                for g in range(NG):
                    if l == 1:
                        pe.wait_ge(moff_ok[g], NL * c + 1)
                    else:
                        pe.wait_ge(Z_ok[g], (NL - 1) * c + l - 1)
                    for b in range(GB):
                        last = pe.transpose(half(g, 1)[:, b, :], Z[q][g][:, b, :], ident)
                    last.then_inc(ZT_ps[g], 1)
                if beside:
                    beside(0)
                for g in range(NG):
                    pe.wait_ge(ZT_ok[g], (NL - 1) * c + l)
                    pe.wait_ge(moff_ok[g], NL * c + l + 1)
                    for b in range(GB):
                        last = pe.matmul(half(g, 0)[:, b, :], moff[g][:, l, b, :], ZT[g][:, b, :],
                                         start=True, stop=True)
                    last.then_inc(P1T_ps[g], 1)
                if beside:
                    beside(1)
                for g in range(NG):
                    pe.wait_ge(P1T_ok[g], (NL - 1) * c + l)
                    for b in range(GB):
                        last = pe.matmul(half(g, 1)[:, b, :], P1T[g][:, b, :], Z[q][g][:, b, :],
                                         start=True, stop=True)
                    last.then_inc(Z_ps[g], 1)

            def recall(c, q):
                for g in range(NG):
                    pe.wait_ge(scaled_ok[g], c + 1)
                    pe.wait_ge(x1_ok[g], c + 1)
                    pe.wait_ge(R_ok[g], c + 1)
                    for b in range(GB):
                        pe.matmul(half(g, 2, 0)[:, b, :], kTg[q][g][:, b, :], R[g][:, b, :], start=True, stop=True)
                    for b in range(GB):
                        last = pe.transpose(half(g, 2, 1)[:, b, :], R[g][:, b, :], ident)
                    last.then_inc(kr_ps[g], 1)

            def updates(c, q):
                for g in range(NG):
                    pe.wait_ge(Z_ok[g], (NL - 1) * c + NL - 1)
                    pe.wait_ge(X0_ok[g], c + 1)
                    pe.wait_ge(XT_ok[g], c + 1)
                    for b in range(GB):
                        last = pe.matmul(half(g, 3)[:, b, :], Z[q][g][:, b, :], X0[g][:, b, :], start=True, stop=True)
                    last.then_inc(U_ps[g], 1)

            def next_state(c, q, groups=range(NG)):
                for g in groups:
                    pe.wait_ge(U_ok[g], c + 1)
                    pe.wait_ge(khd_ok[g], c + 1)
                    pe.wait_ge(S_ok[g], c + 1)
                    for b in range(GB):
                        last = pe.matmul(half(g, 2)[:, b, :], khd[q][g][:, b, :], U[g][:, b, :], start=True, stop=True)
                    last.then_inc(R_ps[g], 1)
                    for b in range(GB):
                        last = pe.transpose(half(g, 3)[:, b, :], U[g][:, b, :], ident)
                    last.then_inc(UT_ps[g], 1)

            def scores(c, q, groups=range(NG)):
                for g in groups:
                    pe.wait_ge(UT_ok[g], c + 1)
                    pe.wait_ge(R_ok[g], c + 2)
                    for b in range(GB):
                        last = pe.matmul(half(g, 2)[:, b, :], UT[g][:, b, :], qT[q][g][:, b, :], start=True, stop=True)
                    last.then_inc(sc_ps[g], 1)

            def heads(c, q, groups=range(NG)):
                for g in groups:
                    pe.wait_ge(PT_ok[g], c + 1)
                    for b in range(GB):
                        pe.matmul(half(g, 3)[:, b, :], S[g][:, b, :], qTg[q][g][:, b, :], start=True, stop=False)
                        last = pe.matmul(half(g, 3)[:, b, :], kh[q][g][:, b, :], PT[g][:, b, :], start=False, stop=True)
                    last.then_inc(OT_ps[g], 1)

            def outputs(c, q, groups=range(NG)):
                for g in groups:
                    pe.wait_ge(OT_ok[g], c + 1)
                    for b in range(GB):
                        last = pe.matmul(bank[g][2][:, b * D:(b + 1) * D], OT[g][:, b, :], wo[:, :],
                                         start=True, stop=True)
                    last.then_inc(y_ps[g], 1)

            def turn_parts(c, q):
                for g in range(NG):
                    pe.wait_ge(Xh_ok[g], c + 1)
                    pe.wait_ge(Xl_ok[g], c + 1)
                    bank16 = bank[g][3][:, :].bitcast(F16)
                    for s, part in enumerate((Xh, Xl)):
                        for k in range(KD):
                            for b in range(GB):
                                at = ((s * KD + k) * GB + b) * P
                                last = pe.transpose(bank16[:, at:at + P], part[g][:, b, k * P:(k + 1) * P],
                                                    ident16[:, :])
                    last.then_inc(XT_ps[g], 1)

            def both(c, q):
                d, r = c + 1, 1 - q
                recall(c, q)
                turn_x(d, r)
                updates(c, q)
                keys_values(d, r)
                queries_gates(d, r)
                spread_alpha(d, r)
                turn_keys(d, r)
                system(d, r)
                doubling(d, r, 1, lambda g: next_state(c, q, [g]))
                doubling(d, r, 2, lambda g: scores(c, q, [g]))
                doubling(d, r, 3, lambda g: heads(c, q, [g]))
                doubling(d, r, 4, lambda g: outputs(c, q, [g]))
                doubling(d, r, 5)
                doubling(d, r, 6)
                turn_parts(c, q)

            turn_x(0, 0)
            keys_values(0, 0)
            queries_gates(0, 0)
            spread_alpha(0, 0)
            turn_keys(0, 0)
            system(0, 0)
            for l in range(1, NL):
                doubling(0, 0, l)
            rounds(pe, both)
            both(NCH - 2, 0)
            recall(NCH - 1, 1)
            updates(NCH - 1, 1)
            next_state(NCH - 1, 1)
            scores(NCH - 1, 1)
            heads(NCH - 1, 1)
            outputs(NCH - 1, 1)
            turn_parts(NCH - 1, 1)

        work.close()
        with nc.Block() as clearing:
            @clearing.gpsimd
            def _(pool):
                for s in held:
                    pool.sem_clear(s)


E_SLOTS = 1024
HID = 4 * D
NS = E_SLOTS // P
NT = T // P
HS = E_SLOTS // 2
QS = HS // P
NF = HID // P
XW = D + 1
XS = D + 2
WSCALE = 64.0
ESHIFT = 12 * math.log(2)


def moe(nc, io, x1_dram, X_dram, XT_dram, out):
    with ExitStack() as ctx:
        def sb(name, shape, dt=F32):
            return ctx.enter_context(nc.sbuf_tensor("m_" + name, shape, dt))

        def two(name, shape, dt=F32):
            return [sb(f"{name}{p}", shape, dt) for p in range(2)]

        def sem(name):
            return ctx.enter_context(nc.semaphore("m_" + name))

        def sems(name):
            return [sem(f"{name}{p}") for p in range(2)]

        ident = sb("ident", [P, P])
        ident16 = sb("ident16", [P, P], F16)
        zero16 = sb("zero16", [P, XW], F16)
        L = sb("L", [P, NT, E_SLOTS])
        X = sb("X", [P, 2, NT, XS], F16)
        XT = sb("XT", [P, 2 * KD, T], F16)
        seT = sb("seT", [P, 2, KD, E_SLOTS], F16)
        w1s = sb("w1s", [P, 2, KD, HID], F16)
        w2s = sb("w2s", [P, 2, NF, D], F16)
        gx_col = sb("gx_col", [P, KD])
        neg_half = sb("neg_half", [P, NS])
        table = sb("table", [P, 2])
        slots_in = L[:, 0:2, :].rearrange("p a n -> p (a n)").rearrange("p (e d) -> p e d", d=D)
        w1_in = L[:, 2:4, :].rearrange("p a n -> p (a n)").rearrange("p (k n) -> p k n", k=KD)
        w2_in = L[:, 4:6, :].rearrange("p a n -> p (a n)").rearrange("p (f n) -> p f n", f=NF)
        slots_n = L[:, 6:8, :].rearrange("p a n -> p (a n)").rearrange("p (e d) -> p e d", d=D)
        slots_g = L[:, 8:10, :].rearrange("p a n -> p (a n)").rearrange("p (e d) -> p e d", d=D)
        w1_g = L[:, 10:12, :].rearrange("p a n -> p (a n)").rearrange("p (k n) -> p k n", k=KD)
        junk = L[:, 12:14, :].rearrange("p a n -> p (a n)").rearrange("p (e d) -> p e d", d=D)
        sp_h = L[:, 14, :].bitcast(F16).rearrange("p (e d) -> p e d", d=D)
        sp_l = L[:, 15, :].bitcast(F16).rearrange("p (e d) -> p e d", d=D)
        sn2 = sb("sn2", [P, NS])
        sn2g = sb("sn2g", [P, NS])
        srn = sb("srn", [P, NS])

        rmax = sb("rmax", [P, NT])
        nrm = sb("nrm", [P, NT])
        cmax = sb("cmax", [P, E_SLOTS])
        mcol = sb("mcol", [P, NS])
        eshift = sb("eshift", [P, 1])
        Mb = sb("Mb", [P, E_SLOTS])
        gx, gs, gxs = (Mb[:, n * D:(n + 1) * D] for n in range(3))
        Dm = two("Dm", [P, HS])
        E = [sb(f"E{u}", [P, HS]) for u in range(4)]
        Eh = [sb(f"Eh{u}", [P, HS], F16) for u in range(4)]
        El = [sb(f"El{u}", [P, HS], F16) for u in range(4)]
        rden = sb("rden", [P, QS])
        sl = sb("sl", [P, QS, D])
        sTh = sb("sTh", [P, KD, HS], F16)
        sTl = sb("sTl", [P, KD, HS], F16)
        hf = E
        hh = sb("hh", [P, NF, HS], F16)
        hl = sb("hl", [P, NF, HS], F16)
        Ph = sb("Ph", [P, NS, XS], F16)
        Pl = sb("Pl", [P, NS, XS], F16)
        Ec = two("Ec", [P, E_SLOTS])
        Th = two("Th", [P, E_SLOTS], F16)
        Tl = two("Tl", [P, E_SLOTS], F16)
        cden = two("cden", [P, 1])
        x1t = two("x1t", [P, D])
        o = two("o", [P, D])

        wide = [ctx.enter_context(nc.psum_tensor(f"m_wide{n}", [P, 1024], F32)) for n in range(4)]
        lg = tp = wide[0:2]
        acc = [[wide[2 * v + q // 2][:, 512 * (q % 2):512 * (q % 2) + XW] for q in range(QS)] for v in range(2)]
        sT_bank = wide[0]
        up = [wide[1][:, 512 * p:512 * p + HS] for p in range(2)]
        down = [wide[2][:, 512 * p:512 * p + D] for p in range(2)]
        co = [wide[3][:, 512 * p:512 * p + XW] for p in range(2)]

        in_ok, pc, sq_ok, sn_g, srn_ok, sln_ok, slg_ok, slh_ok, sll_ok = map(sem, (
            "in_ok pool_consts sq_ok sn_g srn_ok sln_ok slg_ok slh_ok sll_ok").split())
        gxs_ok, w1g_ok, w1h_ok, w2h_ok, seT_ps, seT_ok, set_up = map(sem, (
            "gxs_ok w1g_ok w1h_ok w2h_ok seT_ps seT_ok set_up").split())
        X_in, XT_in, A_dve, rm_ok, cT_ps, mc_ok, Mb_ps, Mb_ok = map(sem, (
            "X_in XT_in A_dve rm_ok cT_ps mc_ok Mb_ps Mb_ok").split())
        cm_ok = sem("cm_ok")
        acc_ps, rd_ok, sl_ok, sT_ps, sTh_ok, sTl_ok = map(sem, "acc_ps rd_ok sl_ok sT_ps sTh_ok sTl_ok".split())
        (lg_ps, L_ok, D_ok, E_ok, Eh_ok, El_ok, B_ps, up_ps, hf_ok, hh_ok, hl_ok, dn_ps, Ph_ok, Pl_ok,
         Ec_ok, tp_ps, Th_ok, Tl_ok, co_ps, cd_ok, o_ok, o_out, x1_in) = [sems(x) for x in (
             "lg_ps L_ok D_ok E_ok Eh_ok El_ok B_ps up_ps hf_ok hh_ok hl_ok dn_ps Ph_ok Pl_ok "
             "Ec_ok tp_ps Th_ok Tl_ok co_ps cd_ok o_ok o_out x1_in").split()]
        N_IN = 7 * 16
        HB = NT // 2
        parts3 = ((0, 0), (0, 1), (1, 0))
        block = ctx.enter_context(nc.Block())

        @block.sync
        def _(sp):
            def bcast(v, n):
                return v.rearrange("(a n) -> a n", a=1).broadcast_to([P, n])

            for dst, src in (
                (ident[:, :], io["const"][:, C_ID:C_ID + P]),
                (slots_in, io["L0_ffn_slot_embeds"].rearrange("e p d -> p e d")),
                (w1_in, io["L0_ffn_w1"].rearrange("(k p) n -> p k n", p=P)),
                (w2_in, io["L0_ffn_w2"].rearrange("(f p) n -> p f n", p=P)),
                (gx, bcast(io["L0_ffn_gamma_x"], D)),
                (gs, bcast(io["L0_ffn_gamma_slot"], D)),
                (gx_col[:, :], io["L0_ffn_gamma_x"].rearrange("(k p) -> p k", p=P)),
            ):
                sp.dma_start(dst, src, allow_slow_non_contiguous=True).then_inc(in_ok, 16)
            for p in range(2):
                sp.sem_inc(o_out[p], 16)

            def load_XT(b):
                sp.dma_start(XT[:, :, :], XT_dram[:, :, bass.ds(b, 1), :].rearrange("q k b t -> q k (b t)"))\
                    .then_inc(XT_in, 16)

            def load_X(b):
                sp.wait_ge(in_ok, N_IN)
                with sp.Fori(0, NT) as j:
                    for s in range(2):
                        sp.dma_start(X[:, s, bass.ds(j, 1), 0:D].rearrange("q a d -> q (a d)"),
                                     X_dram[s, bass.ds(b, 1), bass.ds(j * P, P), :]
                                     .rearrange("b q d -> (b q) d")).then_inc(X_in, 16)

            def results(b):
                with sp.Fori(0, HB) as h:
                    n = sp.snap(b * HB + h + 1)
                    for p in range(2):
                        sp.wait_ge(o_ok[p], n)
                        sp.dma_start(x1t[p][:, :], x1_dram[bass.ds(b, 1), bass.ds(h * 2 * P + p * P, P), :]
                                     .rearrange("b q d -> (b q) d")).then_inc(x1_in[p], 16)
                    for p in range(2):
                        sp.wait_ge(o_ok[p], n + 1)
                        sp.dma_start(out[bass.ds(b, 1), bass.ds(h * 2 * P + p * P, P), :]
                                     .rearrange("b q d -> (b q) d"), o[p][:, :]).then_inc(o_out[p], 16)

            load_XT(0)
            load_X(0)
            with sp.Fori(0, B - 1) as b:
                sp.wait_ge(cT_ps, 2 * b + 2)
                load_XT(b + 1)
                done = sp.snap(sp.to_reg(2 * b + 2))
                sp.wait_ge(in_ok, N_IN)
                sp.wait_ge(acc_ps, done)
                load_X(b + 1)
                results(b)
            results(B - 1)
            for p in range(2):
                sp.wait_ge(o_out[p], 16 * B * HB + 16)

        @block.gpsimd
        def _(pool):
            pool.memset(neg_half[:, :], -0.5)
            pool.memset(zero16[:, :], 0.0)
            pool.memset(eshift[:, :], ESHIFT)
            for s in range(2):
                pool.memset(X[:, s, :, D:], 1.0 - s)
            pool.memset(Ph[:, :, D:], WSCALE)
            pool.memset(Pl[:, :, D:], 0.0).then_inc(pc, 1)
            pool.wait_ge(pc, 1)
            pool.wait_ge(sq_ok, 1)
            pool.tensor_scalar(sn2g[:, :], sn2[:, :], NORM_EPS2, None, ALU.max).then_inc(sn_g, 1)
            pool.wait_ge(sn_g, 1)
            pool.tensor_tensor(srn[:, :], sn2g[:, :], neg_half[:, :], ALU.pow).then_inc(srn_ok, 1)

        @block.vector
        def _(dve):
            dve.wait_ge(in_ok, N_IN)
            dve.tensor_copy(ident16[:, :], ident[:, :])
            dve.tensor_tensor(gxs, gx, gs, ALU.mult).then_inc(gxs_ok, 1)
            dve.wait_ge(srn_ok, 1)
            for e in range(NS):
                last = dve.tensor_scalar(slots_n[:, e, :], slots_in[:, e, :], srn[:, e:e + 1], math.sqrt(D),
                                         ALU.mult, ALU.mult)
            last.then_inc(sln_ok, 1)
            dve.wait_ge(sln_ok, 1)
            dve.wait_ge(gxs_ok, 1)
            dve.tensor_tensor(slots_g, slots_n, gxs.rearrange("p (a d) -> p a d", a=1).broadcast_to([P, NS, D]),
                              ALU.mult).then_inc(slg_ok, 1)
            dve.wait_ge(slg_ok, 1)
            dve.tensor_copy(sp_h, slots_g).then_inc(slh_ok, 1)
            dve.wait_ge(slh_ok, 1)
            dve.tensor_tensor(sp_l, slots_g, sp_h, ALU.subtract).then_inc(sll_ok, 1)
            for k in range(KD):
                last = dve.tensor_scalar(w1_g[:, k, :], w1_in[:, k, :], gx_col[:, k:k + 1], WSCALE,
                                         ALU.mult, ALU.mult)
            last.then_inc(w1g_ok, 1)
            dve.tensor_scalar(w2s[:, 0, :, :], w2_in, WSCALE, None, ALU.mult).then_inc(w2h_ok, 1)
            dve.wait_ge(w1g_ok, 1)
            dve.tensor_copy(w1s[:, 0, :, :], w1_g).then_inc(w1h_ok, 1)
            dve.wait_ge(w2h_ok, 1)
            dve.scalar_tensor_tensor(w2s[:, 1, :, :], w2_in, WSCALE, w2s[:, 0, :, :], ALU.mult, ALU.subtract)
            dve.wait_ge(w1h_ok, 1)
            dve.tensor_tensor(w1s[:, 1, :, :], w1_g, w1s[:, 0, :, :], ALU.subtract).then_inc(set_up, 1)
            for p in range(2):
                dve.sem_inc(El_ok[p], 2)
                dve.sem_inc(hl_ok[p], 2)
                dve.sem_inc(Pl_ok[p], 1)
                dve.sem_inc(Tl_ok[p], 1)
                dve.sem_inc(o_ok[p], 1)

            with dve.Fori(0, B) as b:
                nb = dve.snap(b + 1)
                dve.memset(cmax[:, :], -3.0e38).then_inc(cm_ok, 1)
                with dve.Fori(0, HB) as h:
                    m = dve.snap(b * HB + h)
                    for p in range(2):
                        dve.wait_ge(L_ok[p], m + 2)
                        dve.wait_ge(cm_ok, 2 * m + nb + p)
                        dve.tensor_tensor(cmax[:, :], cmax[:, :], L[:, bass.ds(2 * h + p, 1), :]
                                          .rearrange("q a n -> q (a n)"), ALU.max).then_inc(cm_ok, 1)
                        dve.tensor_reduce(rmax[:, bass.ds(2 * h + p, 1)], L[:, bass.ds(2 * h + p, 1), :]
                                          .rearrange("q a n -> q (a n)"), AX.X, ALU.max, negate=True)\
                            .then_inc(rm_ok, 1)
                dve.wait_ge(rm_ok, NT * nb)
                dve.tensor_scalar(nrm[:, :], rmax[:, :], ESHIFT, None, ALU.add).then_inc(A_dve, 1)
                for z in range(2):
                    dve.wait_ge(cT_ps, 2 * b + z + 1)
                    dve.tensor_reduce(mcol[:, z * QS:(z + 1) * QS], wide[2][:, z * HS:(z + 1) * HS]
                                      .rearrange("q (e t) -> q e t", t=P), AX.X, ALU.max).then_inc(mc_ok, 1)

                def shifted(v, g, t):
                    p, s = t % 2, 2 * b + v
                    dve.wait_ge(E_ok[p], s * HB + 2 * g + t // 2 + 1)
                    dve.tensor_tensor(Dm[p][:, :],
                                      L[:, bass.ds(4 * g + t, 1), v * HS:(v + 1) * HS]
                                      .rearrange("q a n -> q (a n)"),
                                      Mb[:, v * HS:(v + 1) * HS], ALU.subtract).then_inc(D_ok[p], 1)

                def low(v, g, t):
                    p, s = t % 2, 2 * b + v
                    dve.wait_ge(Eh_ok[p], s * HB + 2 * g + t // 2 + 1)
                    dve.tensor_tensor(El[t % 4][:, :], E[t % 4][:, :], Eh[t % 4][:, :], ALU.subtract)\
                        .then_inc(El_ok[p], 1)

                def slots_out(v, qs):
                    s = 2 * b + v
                    dve.wait_ge(acc_ps, s + 1)
                    for q in qs:
                        last = dve.reciprocal(rden[:, q:q + 1], acc[v][q][:, D:D + 1])
                    last.then_inc(rd_ok, len(qs))
                    dve.wait_ge(rd_ok, s * QS + qs[-1] + 1)
                    if v == 1:
                        dve.wait_ge(sT_ps, s)
                    for q in qs:
                        last = dve.tensor_scalar(sl[:, q, :], acc[v][q][:, 0:D], rden[:, q:q + 1], None, ALU.mult)
                    last.then_inc(sl_ok, len(qs))

                def slots_low(v):
                    dve.wait_ge(sTh_ok, 2 * b + v + 1)
                    dve.tensor_tensor(sTl[:, :, :].rearrange("q k n -> q (k n)"), sT_bank[:, :],
                                      sTh[:, :, :].rearrange("q k n -> q (k n)"), ALU.subtract).then_inc(sTl_ok, 1)

                def hidden_low(v):
                    for f in range(NF):
                        dve.wait_ge(hh_ok[f % 2], (2 * b + v) * (NF // 2) + f // 2 + 1)
                        dve.tensor_tensor(hl[:, f, :], hf[f % 4][:, :], hh[:, f, :], ALU.subtract)\
                            .then_inc(hl_ok[f % 2], 1)

                def processed_low(v):
                    for q in range(QS):
                        dve.wait_ge(Ph_ok[q % 2], (2 * b + v) * (QS // 2) + q // 2 + 1)
                        dve.tensor_tensor(Pl[:, v * QS + q, 0:D], down[q % 2], Ph[:, v * QS + q, 0:D],
                                          ALU.subtract).then_inc(Pl_ok[q % 2], 1)

                for v in range(2):
                    loops = NT // 4 - 1 - v
                    dve.wait_ge(Mb_ok, 2 * b + v + 1)
                    shifted(v, 0, 0)
                    shifted(v, 0, 1)
                    with dve.Fori(0, loops) as g:
                        for t in range(4):
                            shifted(v, g, t + 2)
                            low(v, g, t)
                    for t in range(4 * loops, NT):
                        if t + 2 < NT:
                            shifted(v, 0, t + 2)
                        low(v, 0, t)
                        if v == 1 and t < 4 * loops + QS:
                            slots_out(0, [t - 4 * loops])
                slots_low(0)
                slots_out(1, range(QS))
                hidden_low(0)
                slots_low(1)
                processed_low(0)
                hidden_low(1)

                def low_weights(h, p):
                    n = b * HB + h + 1
                    dve.wait_ge(Th_ok[p], n)
                    dve.tensor_tensor(Tl[p][:, :], tp[p][:, :], Th[p][:, :], ALU.subtract).then_inc(Tl_ok[p], 1)

                def finish(h, p):
                    n = b * HB + h + 1
                    dve.wait_ge(co_ps[p], n)
                    dve.reciprocal(cden[p][:, :], co[p][:, D:D + 1]).then_inc(cd_ok[p], 1)
                    dve.wait_ge(cd_ok[p], n)
                    dve.wait_ge(x1_in[p], 16 * n)
                    dve.wait_ge(o_out[p], 16 * n)
                    dve.scalar_tensor_tensor(o[p][:, :], co[p][:, 0:D], cden[p][:, 0:1], x1t[p][:, :],
                                             ALU.mult, ALU.add).then_inc(o_ok[p], 1)

                low_weights(0, 0)
                processed_low(1)
                low_weights(0, 1)
                with dve.Fori(0, HB - 1) as h:
                    for p in range(2):
                        finish(h, p)
                        low_weights(h + 1, p)
                for p in range(2):
                    finish(HB - 1, p)

        @block.scalar
        def _(act):
            act.wait_ge(in_ok, N_IN)
            for e in range(NS):
                last = act.activation(junk[:, e, :], slots_in[:, e, :], ACT.Square, accum_out=sn2[:, e:e + 1])
            last.then_inc(sq_ok, 1)
            for e in range(NS):
                act.wait_ge(seT_ps, e + 1)
                act.copy(seT[:, :, :, e * P:(e + 1) * P].rearrange("q s k n -> q (s k) n"),
                         lg[e % 2][:, 0:256].bitcast(F16).rearrange("q (s n) -> q s n", n=P)).then_inc(seT_ok, 1)
            act.wait_ge(set_up, 1)
            act.wait_ge(seT_ok, NS)
            for p in range(2):
                act.sem_inc(L_ok[p], 1)
                act.sem_inc(E_ok[p], 1)
            with act.Fori(0, B) as b:
                nb = act.snap(b + 1)
                with act.Fori(0, HB) as h:
                    m = act.snap(b * HB + h + 1)
                    for p in range(2):
                        act.wait_ge(pc, 1)
                        act.wait_ge(lg_ps[p], m)
                        act.copy(L[:, bass.ds(2 * h + p, 1), :].rearrange("q a n -> q (a n)"), lg[p][:, :])\
                            .then_inc(L_ok[p], 1)
                act.activation(table[:, 0:1], zero16[:, 0:1], ACT.Exp)
                for z in range(2):
                    act.wait_ge(Mb_ps, 2 * b + z + 1)
                    act.copy(Mb[:, z * HS:(z + 1) * HS], wide[3][:, z * HS:(z + 1) * HS]).then_inc(Mb_ok, 1)

                def exps(v, g, t):
                    p, s = t % 2, 2 * b + v
                    n = s * HB + 2 * g + t // 2 + 1
                    act.wait_ge(D_ok[p], n)
                    act.wait_ge(El_ok[p], n)
                    act.activation(E[t % 4][:, :], Dm[p][:, :], ACT.Exp, bias=eshift[:, 0:1]).then_inc(E_ok[p], 1)

                def high_exps(v, g, t):
                    p, s = t % 2, 2 * b + v
                    n = s * HB + 2 * g + t // 2 + 1
                    act.wait_ge(E_ok[p], n + 1)
                    act.wait_ge(B_ps[p], n)
                    act.copy(Eh[t % 4][:, :], E[t % 4][:, :]).then_inc(Eh_ok[p], 1)

                def slots_high(v):
                    act.wait_ge(sT_ps, 2 * b + v + 1)
                    act.copy(sTh[:, :, :].rearrange("q k n -> q (k n)"), sT_bank[:, :]).then_inc(sTh_ok, 1)

                def hidden(v, f):
                    n = (2 * b + v) * (NF // 2) + f // 2 + 1
                    act.wait_ge(up_ps[f % 2], n)
                    act.wait_ge(hl_ok[f % 2], n)
                    act.activation(hf[f % 4][:, :], up[f % 2], ACT.Gelu, scale=1.0 / WSCALE)\
                        .then_inc(hf_ok[f % 2], 1)

                def hidden_high(v):
                    for p in range(2):
                        act.wait_ge(El_ok[p], (2 * b + 2) * HB + 2)
                    hidden(v, 0)
                    for f in range(NF):
                        if f + 1 < NF:
                            hidden(v, f + 1)
                        act.wait_ge(hf_ok[f % 2], (2 * b + v) * (NF // 2) + f // 2 + 1)
                        act.copy(hh[:, f, :], hf[f % 4][:, :]).then_inc(hh_ok[f % 2], 1)

                def processed_high(v):
                    for q in range(QS):
                        act.wait_ge(dn_ps[q % 2], (2 * b + v) * (QS // 2) + q // 2 + 1)
                        act.copy(Ph[:, v * QS + q, 0:D], down[q % 2]).then_inc(Ph_ok[q % 2], 1)

                def weights(h, p):
                    n = act.snap(b * HB + h + 1)
                    act.wait_ge(pc, 1)
                    act.wait_ge(tp_ps[p], n)
                    act.activation(Ec[p][:, :], L[:, bass.ds(2 * h + p, 1), :].rearrange("q a n -> q (a n)"),
                                   ACT.Exp, bias=nrm[:, bass.ds(2 * h + p, 1)]).then_inc(Ec_ok[p], 1)

                def high(h, p):
                    n = b * HB + h + 1
                    act.wait_ge(tp_ps[p], n + 1)
                    act.copy(Th[p][:, :], tp[p][:, :]).then_inc(Th_ok[p], 1)

                for v in range(2):
                    loops = NT // 4 - 1
                    exps(v, 0, 0)
                    with act.Fori(0, loops) as g:
                        for t in range(4):
                            exps(v, g, t + 1)
                            high_exps(v, g, t)
                    for t in range(4 * loops, NT):
                        if t + 1 < NT:
                            exps(v, 0, t + 1)
                        high_exps(v, 0, t)
                slots_high(0)
                act.wait_ge(A_dve, nb)
                weights(0, 0)
                hidden_high(0)
                slots_high(1)
                processed_high(0)
                hidden_high(1)
                high(0, 0)
                processed_high(1)
                act.activation(table[:, 1:2], zero16[:, 0:1], ACT.Exp)
                weights(0, 1)
                with act.Fori(0, HB - 1) as h:
                    for p in range(2):
                        weights(h + 1, p)
                        high(h + p, 1 - p)
                high(HB - 1, 1)

        @block.tensor
        def _(pe):
            pe.wait_ge(pc, 1)
            pe.wait_ge(sll_ok, 1)
            for e in range(NS):
                if e >= 2:
                    pe.wait_ge(seT_ok, e - 1)
                half16 = lg[e % 2][:, 0:256].bitcast(F16)
                for s, part in enumerate((sp_h, sp_l)):
                    for k in range(KD):
                        at = (s * KD + k) * P
                        last = pe.transpose(half16[:, at:at + P], part[:, e, k * P:(k + 1) * P], ident16[:, :])
                last.then_inc(seT_ps, 1)
            pe.wait_ge(seT_ok, NS)
            pe.wait_ge(set_up, 1)
            for p in range(2):
                pe.sem_inc(B_ps[p], 2)
                pe.sem_inc(tp_ps[p], 1)
            with pe.Fori(0, B) as b:
                nb = pe.snap(b + 1)
                pe.wait_ge(XT_in, 16 * nb)
                turned = pe.snap(pe.to_reg(HB * b + 1))
                pe.wait_ge(pc, 1)
                for p in range(2):
                    pe.wait_ge(Tl_ok[p], turned)
                with pe.Fori(0, HB) as h:
                    m = pe.snap(b * HB + h + 1)
                    for p in range(2):
                        pe.wait_ge(L_ok[p], m)
                        for j in range(2):
                            c = 0
                            for k in range(KD):
                                for sx, ss in parts3:
                                    last = pe.matmul(lg[p][:, j * 512:(j + 1) * 512],
                                                     XT[:, sx * KD + k, bass.ds(h * 2 * P + p * P, P)],
                                                     seT[:, ss, k, j * 512:(j + 1) * 512],
                                                     start=(c == 0), stop=(c == 3 * KD - 1))
                                    c += 1
                        last.then_inc(lg_ps[p], 1)
                pe.wait_ge(cm_ok, (NT + 1) * nb)
                for z in range(2):
                    for e in range(z * QS, (z + 1) * QS):
                        last = pe.transpose(wide[2][:, e * P:(e + 1) * P], cmax[:, e * P:(e + 1) * P], ident[:, :])
                    last.then_inc(cT_ps, 1)
                for p in range(2):
                    pe.wait_ge(o_ok[p], HB * b + 1)
                for z in range(2):
                    pe.wait_ge(mc_ok, 2 * b + z + 1)
                    for e in range(z * QS, (z + 1) * QS):
                        last = pe.transpose(wide[3][:, e * P:(e + 1) * P], mcol[:, e:e + 1].broadcast_to([P, P]),
                                            ident[:, :])
                    last.then_inc(Mb_ps, 1)

                def dispatch(v, g, t):
                    p = t % 2
                    pe.wait_ge(El_ok[p], (2 * b + v) * HB + 2 * g + t // 2 + 3)
                    for q in range(QS):
                        qs = slice(q * P, (q + 1) * P)
                        for e, sx in ((Eh, 0), (Eh, 1), (El, 0)):
                            last = pe.matmul(acc[v][q], e[t % 4][:, qs],
                                             X[:, sx, bass.ds(4 * g + t, 1), 0:XW].rearrange("q a n -> q (a n)"),
                                             start=False, stop=False)
                    last.then_inc(B_ps[p], 1)

                def turn_slots(v):
                    pe.wait_ge(sl_ok, (2 * b + v + 1) * QS)
                    for k in range(KD):
                        for q in range(QS):
                            last = pe.transpose(sT_bank[:, (k * QS + q) * P:(k * QS + q + 1) * P],
                                                sl[:, q, k * P:(k + 1) * P], ident[:, :])
                    last.then_inc(sT_ps, 1)

                sT = (sTh, sTl)
                hT = (hh, hl)

                def hidden(v):
                    s = 2 * b + v
                    pe.wait_ge(sTl_ok, s + 1)
                    for f in range(NF):
                        if v == 1 or f >= 2:
                            pe.wait_ge(hf_ok[f % 2], s * (NF // 2) + f // 2)
                        c = 0
                        for k in range(KD):
                            for sw, ss in parts3:
                                last = pe.matmul(up[f % 2], w1s[:, sw, k, f * P:(f + 1) * P], sT[ss][:, k, :],
                                                 start=(c == 0), stop=(c == 3 * KD - 1))
                                c += 1
                        last.then_inc(up_ps[f % 2], 1)

                def processed(v):
                    s = 2 * b + v
                    for p in range(2):
                        pe.wait_ge(hl_ok[p], (s + 1) * (NF // 2) + 2)
                    for q in range(QS):
                        pe.wait_ge(Pl_ok[q % 2], s * (QS // 2) + q // 2 + 1)
                        c = 0
                        for f in range(NF):
                            for sh, sw in parts3:
                                last = pe.matmul(down[q % 2], hT[sh][:, f, q * P:(q + 1) * P], w2s[:, sw, f, :],
                                                 start=(c == 0), stop=(c == 3 * NF - 1))
                                c += 1
                        last.then_inc(dn_ps[q % 2], 1)

                def turn(h, p):
                    n = b * HB + h + 1
                    pe.wait_ge(Ec_ok[p], n)
                    pe.wait_ge(Tl_ok[p], n)
                    for e in range(NS):
                        last = pe.transpose(tp[p][:, e * P:(e + 1) * P], Ec[p][:, e * P:(e + 1) * P], ident[:, :])
                    last.then_inc(tp_ps[p], 1)

                def combine(h, p):
                    n = b * HB + h + 1
                    pe.wait_ge(Tl_ok[p], n + 1)
                    pe.wait_ge(o_ok[p], n)
                    c = 0
                    for e in range(NS):
                        es = slice(e * P, (e + 1) * P)
                        for a, pp in ((Th, Ph), (Th, Pl), (Tl, Ph)):
                            last = pe.matmul(co[p], a[p][:, es], pp[:, e, 0:XW], start=(c == 0),
                                             stop=(c == 3 * NS - 1))
                            c += 1
                    last.then_inc(co_ps[p], 1)

                arrived = pe.snap(pe.to_reg(32 * NT * nb))
                pe.wait_ge(pc, 1)
                pe.wait_ge(X_in, arrived)
                for v in range(2):
                    if v == 0:
                        for p in range(2):
                            pe.wait_ge(L_ok[p], HB * nb + 1)
                    else:
                        pe.wait_ge(Mb_ok, 2 * nb)
                    for q in range(QS):
                        pe.matmul(acc[v][q], zero16[:, 0:P], zero16[:, :], start=True, stop=False)
                    with pe.Fori(0, NT // 4 - 1) as g:
                        for t in range(4):
                            dispatch(v, g, t)
                    for t in range(NT - 4, NT):
                        if v == 1 and t == NT - 2:
                            turn_slots(0)
                        dispatch(v, 0, t)
                    for q in range(QS):
                        last = pe.matmul(acc[v][q], zero16[:, 0:P], zero16[:, :], start=False, stop=True)
                    last.then_inc(acc_ps, 1)
                hidden(0)
                turn_slots(1)
                processed(0)
                hidden(1)
                turn(0, 0)
                processed(1)
                turn(0, 1)
                cut_to = pe.snap(pe.to_reg(nb * QS + 1))
                pe.wait_ge(pc, 1)
                for p in range(2):
                    pe.wait_ge(Pl_ok[p], cut_to)
                with pe.Fori(0, HB - 1) as h:
                    for p in range(2):
                        combine(h, p)
                        turn(h + 1, p)
                for p in range(2):
                    combine(HB - 1, p)


def build(nc, io, out):
    with ExitStack() as ctx:
        x1_dram = nc.dram_tensor("x1_dram", (B, T, D), F32, kind="Internal").ap()
        X_dram = nc.dram_tensor("X_dram", (2, B, T, D), F16, kind="Internal").ap()
        XT_dram = nc.dram_tensor("XT_dram", (P, 2 * KD, B, T), F16, kind="Internal").ap()
        attention(nc, io, x1_dram, X_dram, XT_dram)
        moe(nc, io, x1_dram, X_dram, XT_dram, out)


_INS = ["L0_attn_x", "L0_attn_Wq", "L0_attn_bq", "L0_attn_Wk", "L0_attn_bk", "L0_attn_Wv", "L0_attn_bv",
        "L0_attn_Wa", "L0_attn_ba", "L0_attn_Wb", "L0_attn_bb", "L0_attn_Wg", "L0_attn_bg", "L0_attn_Wo",
        "L0_attn_bo", "L0_ffn_gamma_x", "L0_ffn_gamma_slot", "L0_ffn_slot_embeds", "L0_ffn_w1", "L0_ffn_w2"]


def kernel(**inputs):
    import numpy as _np
    import concourse.bacc as _bacc
    from concourse import mybir as _mybir
    from concourse.bass_utils import run_bass_kernel_spmd as _run

    nc = _bacc.Bacc("TRN2", target_bir_lowering=False, num_devices=1)
    arrays, io = {}, {}
    for name in _INS + ["const"]:
        a = _np.ascontiguousarray(constants() if name == "const" else inputs[name])
        arrays[f"in_{name}_dram"] = a
        io[name] = nc.dram_tensor(f"in_{name}_dram", a.shape, _mybir.dt.from_np(a.dtype), kind="ExternalInput").ap()
    out = nc.dram_tensor("out_0_dram", (B, T, D), F32, kind="ExternalOutput").ap()
    build(nc, io, out)
    r = _run(nc, [arrays], core_ids=[0])
    return r.results[0]["out_0_dram"]
```

```python
import math
from contextlib import ExitStack

import concourse.bass as bass
import numpy as np
from concourse import mybir

F32 = mybir.dt.float32
F16 = mybir.dt.float16
ALU = mybir.AluOpType
ACT = mybir.ActivationFunctionType
AX = mybir.AxisListType

P = 128
B = 4
T = 2048
D = 256
C = 128
KD = D // P
NCH = T // P
NG = 2
GB = B // NG
NL = 7
KVW = 2 * C + 2
LN_EPS = 1e-5
RMS_GUARD = 1e-24 / D
NORM_EPS2 = 1e-24

E_SLOTS = 1024
HID = 4 * D
NS = E_SLOTS // P
NT = T // P
HS = E_SLOTS // 2
QS = HS // P
NF = HID // P
XW = D + 1
XS = D + 2
WSCALE = 64.0
ESHIFT = 12 * math.log(2)

PARTS3 = ((0, 0), (0, 1), (1, 0))

C_ID, C_MASK = 0, P
CONSTW = P * (1 + NL)


def constants():
    s, t = np.arange(P)[:, None], np.arange(P)[None, :]
    parts = [np.eye(P)]
    for l in range(NL):
        h = 1 << l
        m = (s // (2 * h) == t // (2 * h)) & (s // h % 2 == 0) & (t // h % 2 == 1)
        parts.append(m * (-1.0 if l == 0 else 1.0))
    return np.concatenate([np.asarray(p, np.float32) for p in parts], axis=1)


def attention(nc, io, x1_dram, X_dram, XT_dram, ident_m, ident16, seT, w1s, w2s, XT0):
    held = []
    with ExitStack() as ctx:
        def sb(name, shape, dt=F32):
            return ctx.enter_context(nc.sbuf_tensor(name, shape, dt))

        def per_group(name, shape, dt=F32):
            return [sb(f"{name}{g}", shape, dt) for g in range(NG)]

        def by_parity(name, shape, dt=F32):
            return [per_group(f"{name}_{q}_", shape, dt) for q in range(2)]

        def sem(name):
            held.append(ctx.enter_context(nc.semaphore("a_" + name)))
            return held[-1]

        def sems(name):
            return [sem(f"{name}{g}") for g in range(NG)]

        const = sb("a_const", [P, CONSTW])
        ident = const[:, C_ID:C_ID + P]
        wkv = sb("wkv", [P, KD, KVW])
        wqg = sb("wqg", [P, KD, 2 * C])
        wkv2 = [sb(f"wkv_{n}", [P, KD, KVW], F16) for n in "hl"]
        wqg2 = [sb(f"wqg_{n}", [P, KD, 2 * C], F16) for n in "hl"]
        wo = sb("wo", [P, D])
        bkv = sb("bkv", [P, KVW])
        bq = sb("bq", [P, 1])
        bg = sb("bg", [P, 1])
        bo = sb("bo", [P, D])
        neg_half = sb("a_neg_half", [P, GB])
        ln_eps = sb("a_ln_eps", [P, GB])
        zeros = sb("a_zeros", [P, P])
        table = sb("a_table", [P, 1])

        x = per_group("x", [P, GB, D])
        xres = by_parity("xres", [P, GB, D])
        stats = per_group("stats", [P, GB, 6])
        mv = per_group("mv", [P, GB, 2])
        rstd = per_group("rstd", [P, GB])
        xn = per_group("xn", [P, GB, D])
        xhT = per_group("xhT", [P, KD, GB, P], F16)
        xlT = per_group("xlT", [P, KD, GB, P], F16)
        kvab = by_parity("kvab", [P, GB, KVW])
        qT = by_parity("qT", [P, GB, P])
        qTg = by_parity("qTg", [P, GB, P])
        gateT = by_parity("gateT", [P, GB, P])
        ab = by_parity("ab", [P, GB, 2])
        junk = per_group("junk", [P, GB, C])
        kn2 = per_group("kn2", [P, GB])
        krn = per_group("krn", [P, GB])
        kh = by_parity("kh", [P, GB, C])
        khd = by_parity("khd", [P, GB, C])
        kT = per_group("kT", [P, GB, P])
        kTg = by_parity("kTg", [P, GB, P])
        gam = by_parity("gam", [P, GB, P])
        gbc = by_parity("gbc", [P, GB, P])
        M = per_group("M", [P, GB, P])
        moff = per_group("moff", [P, NL - 1, GB, P])
        Z = by_parity("Z", [P, GB, P])
        ZT = per_group("ZT", [P, GB * P // 2])
        P1T = per_group("P1T", [P, NL - 1, GB * P])
        X0 = per_group("X0", [P, GB, C])
        S = per_group("S", [P, GB, C])
        R = per_group("R", [P, GB, C])
        U = per_group("U", [P, GB, C])
        UT = per_group("UT", [P, GB, P])
        PT = per_group("PT", [P, GB, P])
        OT = per_group("OT", [P, GB, P])
        x1 = per_group("x1", [P, GB, D])
        stats2 = per_group("stats2", [P, GB, 6])
        mv2 = per_group("mv2", [P, GB, 2])
        guard = per_group("guard", [P, GB])
        var2 = per_group("var2", [P, GB])
        rvar = per_group("rvar", [P, GB])
        xf = per_group("xf", [P, GB, D])
        Xh = per_group("Xh", [P, GB, D], F16)
        Xl = per_group("Xl", [P, GB, D], F16)
        XT = per_group("XT", [P, 2, KD, GB, P], F16)
        room = XT0[:, :, :].rearrange("p k t -> p (k t)").bitcast(F32).rearrange("p (a n) -> p a n", a=2)
        slots_in = room[:, 1].rearrange("p (e d) -> p e d", d=D)
        slots_g = sb("slots_g", [P, NS, D])
        sp_h = sb("sp_h", [P, NS, D], F16)
        sp_l = sb("sp_l", [P, NS, D], F16)
        sn2 = sb("sn2", [P, NS])
        srn = sb("srn", [P, NS])
        neg_half_s = sb("neg_half_s", [P, NS])
        gx = sb("gx", [P, D])
        gs = sb("gs", [P, D])
        gxs = sb("gxs", [P, D])
        gx_col = sb("gx_col", [P, KD])
        w1_in = room[:, 0].rearrange("p (k n) -> p k n", k=KD)
        w1_g = slots_g[:, :, :].rearrange("p e d -> p (e d)").rearrange("p (k n) -> p k n", k=KD)
        w2_in = seT[:, :, :, :].rearrange("p s k n -> p (s k n)").bitcast(F32).rearrange("p (f n) -> p f n", f=NF)
        bank = [[ctx.enter_context(nc.psum_tensor(f"a_bank{g}{n}", [P, 512], F32)) for n in range(4)]
                for g in range(NG)]

        def side(ap, l, right):
            return ap.rearrange("p (m two h) -> p m two h", two=2, h=1 << l)[:, :, right, :]

        def packed(ap, l):
            return ap.rearrange("p (m h) -> p m h", h=1 << l)

        def half(g, n, h=0):
            return bank[g][n][:, h * GB * P:(h + 1) * GB * P].rearrange("p (b t) -> p b t", b=GB)

        consts_in, cols_in, pool_consts, dve_consts = (
            sem("consts_in"), sem("cols_in"), sem("pool_consts"), sem("dve_consts"))
        (x_in, xres_ok, stats_ok, mv_ok, rstd_a, rstd_ok, xn_ok, xnT_ps, kv_ps, kv_ok, qg_ps,
         xhT_ok, xlT_ok,
         qg_ok, ab_ok, kn_ok, krn_a, krn_ok, kh_ok, abc_ps, kT_ps, kT_ok, gam_ok, gbc_ok, scaled_ok, khd_ok,
         kk_ps, M_ok, z_half, Z0_ok, moff_ok, ZT_ps, ZT_ok, P1T_ps, P1T_ok, Z_ps, Z_ok, kr_ps, X0_ok, S_ok,
         U_ps, U_ok, R_ps, R_ok, UT_ps, UT_ok, sc_ps, PT_ok, OT_ps, OT_ok, y_ps, x1_ok, x1_out,
         stats2_ok, mv2_ok, guard_ok, var2_ok, rvar_ok, xf_ok, Xh_ok, Xl_ok, XT_ps, XT_ok, X_out) = [
            sems(n) for n in (
                "x_in xres_ok stats_ok mv_ok rstd_a rstd_ok xn_ok xnT_ps kv_ps kv_ok qg_ps "
                "xhT_ok xlT_ok qg_ok ab_ok kn_ok krn_a krn_ok kh_ok abc_ps kT_ps kT_ok gam_ok gbc_ok scaled_ok khd_ok "
                "kk_ps M_ok z_half Z0_ok moff_ok ZT_ps ZT_ok P1T_ps P1T_ok Z_ps Z_ok kr_ps X0_ok S_ok "
                "U_ps U_ok R_ps R_ok UT_ps UT_ok sc_ps PT_ok OT_ps OT_ok y_ps x1_ok x1_out "
                "stats2_ok mv2_ok guard_ok var2_ok rvar_ok xf_ok Xh_ok Xl_ok XT_ps XT_ok X_out").split()]
        (ident_in, XT0_in, mix_in, sq_ok, sn_g, srn_ok, gxs_ok, slg_ok, slh_ok, sll_ok,
         w1g_ok, w1h_ok, w2h_ok, seT_ps, seT_ok) = map(sem, (
             "ident_in XT0_in mix_in sq_ok sn_g srn_ok gxs_ok slg_ok slh_ok sll_ok "
             "w1g_ok w1h_ok w2h_ok seT_ps seT_ok").split())
        N_CONSTS = 13 * 16
        N_MIX = 6 * 16
        work = ExitStack()
        block = work.enter_context(nc.Block())

        def rounds(eng, body):
            with eng.Fori(0, NCH // 2 - 1) as j:
                for q in range(2):
                    body(eng.snap(2 * j + q), q)

        def bcast(v, n):
            return v.rearrange("(a n) -> a n", a=1).broadcast_to([P, n])

        @block.sync
        def _(sp):
            def load(c):
                for g in range(NG):
                    if not isinstance(c, int) or c > 0:
                        sp.wait_ge(xn_ok[g], c)
                        sp.wait_ge(xres_ok[g], c)
                    sp.dma_start(x[g][:, :, :], io["L0_attn_x"][g * GB:(g + 1) * GB, bass.ds(c * P, P), :]
                                 .rearrange("b p d -> p b d")).then_inc(x_in[g], 16)

            load(0)
            sp.dma_start(const[:, C_ID:C_ID + P], io["const"][:, C_ID:C_ID + P]).then_inc(ident_in, 16)
            for dst, src in (
                (wkv[:, :, 0:C], io["L0_attn_Wk"].rearrange("(k p) n -> p k n", p=P)),
                (wkv[:, :, C:2 * C], io["L0_attn_Wv"].rearrange("(k p) n -> p k n", p=P)),
                (wkv[:, :, 2 * C:2 * C + 1], io["L0_attn_Wa"].rearrange("(k p) n -> p k n", p=P)),
                (wkv[:, :, 2 * C + 1:], io["L0_attn_Wb"].rearrange("(k p) n -> p k n", p=P)),
                (const[:, C_MASK:], io["const"][:, C_MASK:]),
                (bo[:, :], bcast(io["L0_attn_bo"], D)),
            ):
                sp.dma_start(dst, src, allow_slow_non_contiguous=True).then_inc(consts_in, 16)

            def store_parts(c):
                n = c + 2
                for g in range(NG):
                    gb = slice(g * GB, (g + 1) * GB)
                    sp.wait_ge(Xh_ok[g], n)
                    sp.dma_start(X_dram[0, gb, bass.ds(c * P, P), :].rearrange("b p d -> p b d"),
                                 Xh[g][:, :, :]).then_inc(X_out[g], 16)
                    sp.wait_ge(Xl_ok[g], n)
                    sp.dma_start(X_dram[1, gb, bass.ds(c * P, P), :].rearrange("b p d -> p b d"),
                                 Xl[g][:, :, :]).then_inc(X_out[g], 16)
                    sp.wait_ge(consts_in, N_CONSTS)
                    sp.wait_ge(XT_ok[g], c + 2)
                    sp.dma_start(XT_dram[:, :, gb, bass.ds(c * P, P)],
                                 XT[g][:, :, :, :, :].rearrange("p s k b t -> p (s k) b t")).then_inc(X_out[g], 16)

            for dst, src in (
                (slots_in, io["L0_ffn_slot_embeds"].rearrange("e p d -> p e d")),
                (gx[:, :], bcast(io["L0_ffn_gamma_x"], D)),
                (gs[:, :], bcast(io["L0_ffn_gamma_slot"], D)),
                (gx_col[:, :], io["L0_ffn_gamma_x"].rearrange("(k p) -> p k", p=P)),
                (w1_in, io["L0_ffn_w1"].rearrange("(k p) n -> p k n", p=P)),
                (w2_in, io["L0_ffn_w2"].rearrange("(f p) n -> p f n", p=P)),
            ):
                sp.dma_start(dst, src, allow_slow_non_contiguous=True).then_inc(mix_in, 16)
            load(1)

            def body(c, q):
                load(c + 2)
                store_parts(c)

            def load_XT0(first, past):
                sp.wait_ge(X_out[0], 48 * past + 48)
                sp.dma_start(XT0[:, :, first * P:past * P], XT_dram[:, :, 0, first * P:past * P]).then_inc(XT0_in, 16)

            rounds(sp, body)
            store_parts(NCH - 2)
            sp.wait_ge(slg_ok, 1)
            load_XT0(0, NCH - 1)
            store_parts(NCH - 1)
            load_XT0(NCH - 1, NCH)
            sp.wait_ge(XT0_in, 32)

        @block.gpsimd
        def _(pool):
            pool.dma_start(bq[:, :], io["L0_attn_bq"].rearrange("(p n) -> p n", n=1),
                           allow_slow_non_contiguous=True).then_inc(cols_in, 16)
            pool.dma_start(bg[:, :], io["L0_attn_bg"].rearrange("(p n) -> p n", n=1),
                           allow_slow_non_contiguous=True).then_inc(cols_in, 16)
            pool.memset(ln_eps[:, :], LN_EPS)
            pool.memset(neg_half_s[:, :], -0.5)
            for g in range(NG):
                pool.memset(P1T[g][:, :, :], 0.0)
            pool.memset(neg_half[:, :], -0.5).then_inc(pool_consts, 1)
            pool.wait_ge(pool_consts, 1)

            def norm(c, q):
                n = c + 1
                for g in range(NG):
                    pool.wait_ge(mv_ok[g], n)
                    pool.tensor_tensor(rstd[g][:, :], mv[g][:, :, 1], ln_eps[:, :], ALU.add).then_inc(rstd_a[g], 1)
                    pool.wait_ge(rstd_a[g], n)
                    pool.tensor_tensor(rstd[g][:, :], rstd[g][:, :], neg_half[:, :], ALU.pow).then_inc(rstd_ok[g], 1)
                if isinstance(c, int):
                    pool.wait_ge(consts_in, N_CONSTS)
                for g in range(NG):
                    pool.wait_ge(x_in[g], 16 * n)
                    if not isinstance(c, int):
                        pool.wait_ge(x1_ok[g], c)
                    pool.tensor_tensor(xres[q][g][:, :, :], x[g][:, :, :],
                                       bo[:, :].rearrange("p (a d) -> p a d", a=1).broadcast_to([P, GB, D]),
                                       ALU.add).then_inc(xres_ok[g], 1)

            def keys(c, q):
                n = c + 1 if isinstance(c, int) else pool.snap(pool.to_reg(c + 1))
                for g in range(NG):
                    pool.wait_ge(pool_consts, 1)
                    pool.wait_ge(kn_ok[g], n)
                    pool.tensor_scalar(krn[g][:, :], kn2[g][:, :], NORM_EPS2, None, ALU.max).then_inc(krn_a[g], 1)
                    pool.wait_ge(krn_a[g], n)
                    pool.tensor_tensor(krn[g][:, :], krn[g][:, :], neg_half[:, :], ALU.pow).then_inc(krn_ok[g], 1)

            def cut(n, l):
                for g in range(NG):
                    pool.wait_ge(M_ok[g], n)
                    ml = const[:, C_MASK + l * P:C_MASK + (l + 1) * P]
                    pool.tensor_tensor(moff[g][:, l - 1], M[g][:, :, :],
                                       ml.rearrange("p (a t) -> p a t", a=1).broadcast_to([P, GB, P]),
                                       ALU.mult).then_inc(moff_ok[g], 1)

            def decayed(c, q):
                n = c + 1
                for g in range(NG):
                    pool.wait_ge(gbc_ok[g], n)
                    pool.wait_ge(kT_ok[g], n)
                    pool.tensor_tensor(kTg[q][g][:, :, :], kT[g][:, :, :], gbc[q][g][:, :, :], ALU.mult)
                    pool.wait_ge(qg_ok[g], n)
                    pool.tensor_tensor(qTg[q][g][:, :, :], qT[q][g][:, :, :], gbc[q][g][:, :, :], ALU.mult)\
                        .then_inc(scaled_ok[g], 1)

            def local(c, q):
                keys(c, q)
                for l in range(1, NL):
                    cut(c + 1, l)
                decayed(c, q)

            def outputs(c, q):
                for g in range(NG):
                    pool.wait_ge(var2_ok[g], c + 1)
                    pool.tensor_tensor(rvar[g][:, :], var2[g][:, :], neg_half[:, :], ALU.pow).then_inc(rvar_ok[g], 1)

            def body(c, q):
                d, r = c + 1, 1 - q
                keys(d, r)
                for l in range(1, NL):
                    cut(c + 2, l)
                norm(c + 2, q)
                outputs(c, q)
                decayed(d, r)

            norm(0, 0)
            local(0, 0)
            norm(1, 1)
            pool.wait_ge(sq_ok, 1)
            pool.tensor_scalar(srn[:, :], sn2[:, :], NORM_EPS2, None, ALU.max).then_inc(sn_g, 1)
            pool.wait_ge(sn_g, 1)
            pool.tensor_tensor(srn[:, :], srn[:, :], neg_half_s[:, :], ALU.pow).then_inc(srn_ok, 1)
            rounds(pool, body)
            local(NCH - 1, 1)
            outputs(NCH - 2, 0)
            outputs(NCH - 1, 1)

        @block.vector
        def _(dve):
            for g in range(NG):
                dve.memset(R[g][:, :, :], 0.0).then_inc(R_ok[g], 1)
                dve.sem_inc(x1_ok[g], 1)
                dve.memset(Xh[g][:, :, :], 0.0).then_inc(Xh_ok[g], 1)
                dve.memset(Xl[g][:, :, :], 0.0).then_inc(Xl_ok[g], 1)
            dve.memset(zeros[:, :], 0.0).then_inc(dve_consts, 1)
            dve.wait_ge(dve_consts, 1)

            def norm(c, q):
                n = dve.snap(dve.to_reg(c + 1)) if not isinstance(c, int) else c + 1
                for g in range(NG):
                    dve.wait_ge(x_in[g], 16 * n)
                    for b in range(GB):
                        last = dve.bn_stats(stats[g][:, b, :], x[g][:, b, :])
                    last.then_inc(stats_ok[g], 1)
                    dve.wait_ge(dve_consts, 1)
                    dve.wait_ge(stats_ok[g], n)
                    for b in range(GB):
                        last = dve.bn_aggr(mv[g][:, b, :], stats[g][:, b, :])
                    last.then_inc(mv_ok[g], 1)

            def norm_end(c, q):
                for g in range(NG):
                    dve.wait_ge(rstd_ok[g], c + 1)
                    for b in range(GB):
                        last = dve.tensor_scalar(xn[g][:, b, :], x[g][:, b, :], mv[g][:, b, 0:1],
                                                 rstd[g][:, b:b + 1], ALU.subtract, ALU.mult)
                    last.then_inc(xn_ok[g], 1)

            def turned_low(c, q):
                for g in range(NG):
                    dve.wait_ge(xhT_ok[g], c + 1)
                    dve.tensor_tensor(xlT[g][:, :, :, :].rearrange("p k b t -> p (k b t)"), bank[g][0][:, :],
                                      xhT[g][:, :, :, :].rearrange("p k b t -> p (k b t)"), ALU.subtract)\
                        .then_inc(xlT_ok[g], 1)

            def biases(c, q):
                for g in range(NG):
                    dve.wait_ge(kv_ps[g], c + 1)
                    for b in range(GB):
                        last = dve.scalar_tensor_tensor(kvab[q][g][:, b, :], bank[g][1 - b][:, 0:KVW], 1.0 / WSCALE,
                                                        bkv[:, :], ALU.mult, ALU.add)
                    last.then_inc(kv_ok[g], 1)

            def keys(c, q):
                for g in range(NG):
                    dve.wait_ge(krn_ok[g], c + 1)
                    for b in range(GB):
                        last = dve.tensor_scalar(kh[q][g][:, b, :], kvab[q][g][:, b, 0:C], krn[g][:, b:b + 1], None,
                                                 ALU.mult)
                    last.then_inc(kh_ok[g], 1)

            def decays(c, q):
                for g in range(NG):
                    dve.wait_ge(abc_ps[g], c + 1)
                    for b in range(GB):
                        last = dve.tensor_tensor_scan(gam[q][g][:, b, :], half(g, 0)[:, b, :], ident, 0.0,
                                                      ALU.mult, ALU.add)
                    last.then_inc(gam_ok[g], 1)
                    for b in range(GB):
                        last = dve.tensor_tensor_scan(gbc[q][g][:, b, :], half(g, 0)[:, b, :], zeros[:, :], 1.0,
                                                      ALU.mult, ALU.add)
                    last.then_inc(gbc_ok[g], 1)

            def decayed(c, q):
                for g in range(NG):
                    dve.wait_ge(gam_ok[g], c + 1)
                    for b in range(GB):
                        last = dve.tensor_scalar(khd[q][g][:, b, :], kh[q][g][:, b, :], gam[q][g][:, b, P - 1:P], None,
                                                 ALU.mult)
                    last.then_inc(khd_ok[g], 1)

            def system(c, q):
                for g in range(NG):
                    dve.wait_ge(kk_ps[g], c + 1)
                    for b in range(GB):
                        last = dve.scalar_tensor_tensor(M[g][:, b, :], half(g, 0)[:, b, :], ab[q][g][:, b, 1:2],
                                                        gam[q][g][:, b, :], ALU.mult, ALU.mult)
                    last.then_inc(M_ok[g], 1)

            def first_doubling(c, q):
                for g in range(NG):
                    dve.wait_ge(M_ok[g], c + 1)
                    m0 = const[:, C_MASK:C_MASK + P].rearrange("p (a t) -> p a t", a=1).broadcast_to([P, GB, P])
                    dve.tensor_tensor(Z[q][g][:, :, :], M[g][:, :, :], m0, ALU.mult).then_inc(z_half[g], 1)
                for g in range(NG):
                    dve.wait_ge(z_half[g], c + 1)
                    dve.tensor_tensor(Z[q][g][:, :, :], Z[q][g][:, :, :],
                                      ident.rearrange("p (a t) -> p a t", a=1).broadcast_to([P, GB, P]),
                                      ALU.add).then_inc(Z0_ok[g], 1)

            def doubling(c, q, l):
                for g in range(NG):
                    dve.wait_ge(Z_ps[g], (NL - 1) * c + l)
                    Zr = side(Z[q][g][:, :, :].rearrange("p b t -> p (b t)"), l, 1)
                    dve.tensor_tensor(Zr, Zr, packed(bank[g][1][:, 0:GB * P // 2], l), ALU.subtract)\
                        .then_inc(Z_ok[g], 1)

            def right_side(c, q):
                for g in range(NG):
                    dve.wait_ge(kr_ps[g], c + 1)
                    dve.tensor_tensor(X0[g][:, :, :], kvab[q][g][:, :, C:2 * C], half(g, 2, 0), ALU.subtract)\
                        .then_inc(X0_ok[g], 1)
                    dve.tensor_copy(S[g][:, :, :], half(g, 2, 1)).then_inc(S_ok[g], 1)

            def next_state(c, q):
                for g in range(NG):
                    dve.wait_ge(R_ps[g], c + 1)
                    for b in range(GB):
                        last = dve.scalar_tensor_tensor(R[g][:, b, :], R[g][:, b, :], gbc[q][g][:, b, P - 1:P],
                                                        half(g, 2)[:, b, :], ALU.mult, ALU.add)
                    last.then_inc(R_ok[g], 1)

            def weights(c, q):
                for g in range(NG):
                    dve.wait_ge(sc_ps[g], c + 1)
                    dve.tensor_tensor(PT[g][:, :, :], half(g, 2), gam[q][g][:, :, :], ALU.mult).then_inc(PT_ok[g], 1)

            def gated(c, q):
                for g in range(NG):
                    dve.wait_ge(OT_ps[g], c + 1)
                    dve.tensor_tensor(OT[g][:, :, :], half(g, 3), gateT[q][g][:, :, :], ALU.mult)\
                        .then_inc(OT_ok[g], 1)

            def residual(c, q):
                for g in range(NG):
                    dve.wait_ge(y_ps[g], c + 1)
                    dve.wait_ge(xres_ok[g], c + 1)
                    dve.wait_ge(x1_out[g], 16 * c + 16)
                    dve.tensor_tensor(x1[g][:, :, :], xres[q][g][:, :, :],
                                      bank[g][2][:, :].rearrange("p (b d) -> p b d", b=GB), ALU.add)\
                        .then_inc(x1_ok[g], 1)

            def statistics(c, q):
                n = dve.snap(dve.to_reg(c + 1)) if not isinstance(c, int) else c + 1
                for g in range(NG):
                    dve.wait_ge(x1_ok[g], n + 1)
                    for b in range(GB):
                        last = dve.bn_stats(stats2[g][:, b, :], x1[g][:, b, :])
                    last.then_inc(stats2_ok[g], 1)
                for g in range(NG):
                    dve.wait_ge(dve_consts, 1)
                    dve.wait_ge(stats2_ok[g], n)
                    for b in range(GB):
                        last = dve.bn_aggr(mv2[g][:, b, :], stats2[g][:, b, :])
                    last.then_inc(mv2_ok[g], 1)
                for g in range(NG):
                    dve.wait_ge(mv2_ok[g], n)
                    dve.tensor_scalar(guard[g][:, :], mv2[g][:, :, 1], RMS_GUARD, RMS_GUARD * LN_EPS,
                                      ALU.mult, ALU.add).then_inc(guard_ok[g], 1)
                for g in range(NG):
                    dve.wait_ge(guard_ok[g], n)
                    dve.tensor_tensor(var2[g][:, :], mv2[g][:, :, 1], guard[g][:, :], ALU.max).then_inc(var2_ok[g], 1)

            def normalised(c, q):
                for g in range(NG):
                    dve.wait_ge(rvar_ok[g], c + 1)
                    for b in range(GB):
                        last = dve.tensor_scalar(xf[g][:, b, :], x1[g][:, b, :], mv2[g][:, b, 0:1],
                                                 rvar[g][:, b:b + 1], ALU.subtract, ALU.mult)
                    last.then_inc(xf_ok[g], 1)

            def low_part(c, q):
                for g in range(NG):
                    dve.wait_ge(Xh_ok[g], c + 2)
                    dve.wait_ge(X_out[g], 48 * c + 48)
                    dve.tensor_tensor(Xl[g][:, :, :], xf[g][:, :, :], Xh[g][:, :, :], ALU.subtract)\
                        .then_inc(Xl_ok[g], 1)

            def mixture_weights(step):
                if step == 1:
                    dve.wait_ge(mix_in, N_MIX)
                    dve.scalar_tensor_tensor(gxs[:, :], gx[:, :], math.sqrt(D), gs[:, :], ALU.mult, ALU.mult)\
                        .then_inc(gxs_ok, 1)
                    for k in range(KD):
                        last = dve.tensor_scalar(w1_g[:, k, :], w1_in[:, k, :], gx_col[:, k:k + 1], WSCALE,
                                                 ALU.mult, ALU.mult)
                    last.then_inc(w1g_ok, 1)
                elif step == 2:
                    dve.tensor_scalar(w2s[:, 0, :, :], w2_in, WSCALE, None, ALU.mult).then_inc(w2h_ok, 1)
                elif step == 3:
                    dve.wait_ge(w1g_ok, 1)
                    dve.tensor_copy(w1s[:, 0, :, :], w1_g).then_inc(w1h_ok, 1)
                elif step == 4:
                    dve.wait_ge(w2h_ok, 1)
                    dve.scalar_tensor_tensor(w2s[:, 1, :, :], w2_in, WSCALE, w2s[:, 0, :, :],
                                             ALU.mult, ALU.subtract)
                elif step == 5:
                    dve.wait_ge(w1h_ok, 1)
                    dve.tensor_tensor(w1s[:, 1, :, :], w1_g, w1s[:, 0, :, :], ALU.subtract)

            def slots_scaled():
                dve.wait_ge(srn_ok, 1)
                dve.wait_ge(gxs_ok, 1)
                for e in range(NS):
                    last = dve.scalar_tensor_tensor(slots_g[:, e, :], slots_in[:, e, :], srn[:, e:e + 1], gxs[:, :],
                                                    ALU.mult, ALU.mult)
                last.then_inc(slg_ok, 1)

            def slots_high():
                dve.wait_ge(slg_ok, 1)
                dve.tensor_copy(sp_h[:, :, :], slots_g[:, :, :]).then_inc(slh_ok, 1)

            def slots_low():
                dve.wait_ge(slh_ok, 1)
                dve.tensor_tensor(sp_l[:, :, :], slots_g[:, :, :], sp_h[:, :, :], ALU.subtract).then_inc(sll_ok, 1)

            def local(c, q):
                turned_low(c, q)
                biases(c, q)
                keys(c, q)
                decays(c, q)
                system(c, q)
                first_doubling(c, q)
                decayed(c, q)
                for l in range(1, NL):
                    doubling(c, q, l)
                    if c == 0:
                        mixture_weights(l)

            def state(c, q):
                right_side(c, q)
                next_state(c, q)
                weights(c, q)
                gated(c, q)
                residual(c, q)
                statistics(c, q)
                normalised(c, q)
                low_part(c, q)

            def both(c, q, norm_too):
                d, r = c + 1, 1 - q
                turned_low(d, r)
                right_side(c, q)
                biases(d, r)
                keys(d, r)
                decays(d, r)
                system(d, r)
                first_doubling(d, r)
                next_state(c, q)
                doubling(d, r, 1)
                decayed(d, r)
                weights(c, q)
                doubling(d, r, 2)
                gated(c, q)
                doubling(d, r, 3)
                if norm_too:
                    norm(c + 2, q)
                else:
                    slots_scaled()
                residual(c, q)
                doubling(d, r, 4)
                statistics(c, q)
                doubling(d, r, 5)
                if norm_too:
                    norm_end(c + 2, q)
                else:
                    slots_high()
                normalised(c, q)
                doubling(d, r, 6)
                low_part(c, q)
                if not norm_too:
                    slots_low()

            norm(0, 0)
            norm_end(0, 0)
            dve.wait_ge(consts_in, N_CONSTS)
            dve.wait_ge(ident_in, 16)
            dve.tensor_copy(ident16[:, :], ident)
            dve.tensor_copy(ident_m[:, :], ident).then_inc(dve_consts, 1)
            for w, w2 in ((wkv, wkv2), (wqg, wqg2)):
                dve.tensor_scalar(w2[0][:, :, :], w[:, :, :], WSCALE, None, ALU.mult).then_inc(dve_consts, 1)
            for n, (w, w2) in enumerate(((wkv, wkv2), (wqg, wqg2))):
                dve.wait_ge(dve_consts, 3 + n)
                dve.scalar_tensor_tensor(w2[1][:, :, :], w[:, :, :], WSCALE, w2[0][:, :, :], ALU.mult, ALU.subtract)\
                    .then_inc(dve_consts, 1)
            local(0, 0)
            norm(1, 1)
            norm_end(1, 1)
            rounds(dve, lambda c, q: both(c, q, True))
            both(NCH - 2, 0, False)
            state(NCH - 1, 1)

        @block.scalar
        def _(act):
            for dst, src in (
                (wqg[:, :, 0:C], io["L0_attn_Wq"].rearrange("(k p) n -> p k n", p=P)),
                (wqg[:, :, C:], io["L0_attn_Wg"].rearrange("(k p) n -> p k n", p=P)),
                (bkv[:, 0:C], bcast(io["L0_attn_bk"], C)),
                (bkv[:, C:2 * C], bcast(io["L0_attn_bv"], C)),
                (bkv[:, 2 * C:2 * C + 1], bcast(io["L0_attn_ba"], 1)),
                (bkv[:, 2 * C + 1:], bcast(io["L0_attn_bb"], 1)),
                (wo[:, :], io["L0_attn_Wo"]),
            ):
                act.dma_start(dst, src, allow_slow_non_contiguous=True).then_inc(consts_in, 16)
            act.wait_ge(cols_in, 32)
            act.wait_ge(pool_consts, 1)
            for g in range(NG):
                act.sem_inc(x1_out[g], 16)
                act.sem_inc(X_out[g], 48)
            act.wait_ge(dve_consts, 1)
            act.activation(table[:, :], zeros[:, 0:1], ACT.Sigmoid)

            def turned_x(c, q):
                for g in range(NG):
                    act.wait_ge(xnT_ps[g], c + 1)
                    act.copy(xhT[g][:, :, :, :].rearrange("p k b t -> p (k b t)"), bank[g][0][:, :])\
                        .then_inc(xhT_ok[g], 1)

            def key_norms(c, q):
                for g in range(NG):
                    act.wait_ge(kv_ok[g], c + 1)
                    for b in range(GB):
                        last = act.activation(junk[g][:, b, :], kvab[q][g][:, b, 0:C], ACT.Square,
                                              accum_out=kn2[g][:, b:b + 1])
                    last.then_inc(kn_ok[g], 1)
                    act.activation(ab[q][g][:, :, :], kvab[q][g][:, :, 2 * C:], ACT.Sigmoid).then_inc(ab_ok[g], 1)

            def queries(c, q):
                for g in range(NG):
                    act.wait_ge(qg_ps[g], c + 1)
                    act.activation(qT[q][g][:, :, :], half(g, 1, 0), ACT.Identity, bias=bq[:, 0:1], scale=1.0 / WSCALE)
                    act.activation(gateT[q][g][:, :, :], half(g, 1, 1), ACT.Sigmoid, bias=bg[:, 0:1],
                                   scale=1.0 / WSCALE)\
                        .then_inc(qg_ok[g], 1)

            def turned_keys(c, q):
                for g in range(NG):
                    act.wait_ge(kT_ps[g], c + 1)
                    act.copy(kT[g][:, :, :], half(g, 1)).then_inc(kT_ok[g], 1)

            def doubling(c, q, l):
                for g in range(NG):
                    act.wait_ge(ZT_ps[g], (NL - 1) * c + l)
                    act.copy(packed(ZT[g][:, :], l), side(bank[g][1][:, 0:GB * P], l, 0)).then_inc(ZT_ok[g], 1)
                for g in range(NG):
                    act.wait_ge(P1T_ps[g], (NL - 1) * c + l)
                    act.copy(side(P1T[g][:, l - 1, :], l, 0), packed(bank[g][0][:, 0:GB * P // 2], l))\
                        .then_inc(P1T_ok[g], 1)

            def updates(c, q):
                for g in range(NG):
                    act.wait_ge(U_ps[g], c + 1)
                    for b in range(GB):
                        last = act.activation(U[g][:, b, :], half(g, 3)[:, b, :], ACT.Identity,
                                              scale=ab[q][g][:, b, 1:2])
                    last.then_inc(U_ok[g], 1)

            def turned_updates(c, q):
                for g in range(NG):
                    act.wait_ge(UT_ps[g], c + 1)
                    act.copy(UT[g][:, :, :], half(g, 3)).then_inc(UT_ok[g], 1)

            def store(c, q):
                for g in range(NG):
                    act.wait_ge(x1_ok[g], c + 2)
                    act.dma_start(x1_dram[g * GB:(g + 1) * GB, bass.ds(c * P, P), :].rearrange("b p d -> p b d"),
                                  x1[g][:, :, :]).then_inc(x1_out[g], 16)

            def high_part(c, q):
                for g in range(NG):
                    act.wait_ge(xf_ok[g], c + 1)
                    act.wait_ge(X_out[g], 48 * c + 48)
                    act.copy(Xh[g][:, :, :], xf[g][:, :, :]).then_inc(Xh_ok[g], 1)

            def turned_parts(c):
                for g in range(NG):
                    act.wait_ge(XT_ps[g], c + 1)
                    act.copy(XT[g][:, :, :, :, :].rearrange("p s k b t -> p (s k b t)"),
                             bank[g][3][:, :].bitcast(F16)).then_inc(XT_ok[g], 1)

            def turned_slots(es):
                for e in es:
                    act.wait_ge(seT_ps, e + 1)
                    act.copy(seT[:, :, :, e * P:(e + 1) * P].rearrange("q s k n -> q (s k) n"),
                             bank[e // 2 % 2][e % 2][:, 0:256].bitcast(F16).rearrange("q (s n) -> q s n", n=P))\
                        .then_inc(seT_ok, 1)

            def both(c, q):
                d, r = c + 1, 1 - q
                turned_x(d, r)
                turned_parts(c)
                key_norms(d, r)
                queries(d, r)
                turned_keys(d, r)
                updates(c, q)
                turned_updates(c, q)
                doubling(d, r, 1)
                for l in range(2, 5):
                    doubling(d, r, l)
                store(c, q)
                doubling(d, r, 5)
                doubling(d, r, 6)
                high_part(c, q)

            turned_x(0, 0)
            key_norms(0, 0)
            queries(0, 0)
            turned_keys(0, 0)
            for l in range(1, NL):
                doubling(0, 0, l)
                if l == 1:
                    act.wait_ge(mix_in, N_MIX)
                if l <= NS // 2:
                    for e in (2 * l - 2, 2 * l - 1):
                        last = act.activation(sp_h[:, e, :], slots_in[:, e, :], ACT.Square,
                                              accum_out=sn2[:, e:e + 1])
            last.then_inc(sq_ok, 1)
            rounds(act, both)
            both(NCH - 2, 0)
            turned_parts(NCH - 1)
            updates(NCH - 1, 1)
            turned_slots((0, 1))
            turned_updates(NCH - 1, 1)
            turned_slots((2, 3))
            turned_slots((4, 5))
            turned_slots((6, 7))
            store(NCH - 1, 1)
            high_part(NCH - 1, 1)
            turned_parts(NCH)
            for g in range(NG):
                act.wait_ge(x1_out[g], 16 * NCH + 16)
                act.wait_ge(X_out[g], 48 * NCH + 48)

        @block.tensor
        def _(pe):
            pe.wait_ge(ident_in, 16)
            pe.wait_ge(dve_consts, 1)
            pe.wait_ge(pool_consts, 1)

            def turn_x(c, q):
                for g in range(NG):
                    pe.wait_ge(xn_ok[g], c + 1)
                    for k in range(KD):
                        for b in range(GB):
                            at = (k * GB + b) * P
                            last = pe.transpose(bank[g][0][:, at:at + P], xn[g][:, b, k * P:(k + 1) * P], ident)
                    last.then_inc(xnT_ps[g], 1)

            def keys_values(c, q):
                for g in range(NG):
                    pe.wait_ge(xhT_ok[g], c + 1)
                    pe.wait_ge(xlT_ok[g], c + 1)
                    if not isinstance(c, int) or c > 0:
                        pe.wait_ge(Z_ok[g], (NL - 1) * c)
                    xT = (xhT[g], xlT[g])
                    for b in range(GB):
                        n = 0
                        for k in range(KD):
                            for sx, sw in PARTS3:
                                last = pe.matmul(bank[g][1 - b][:, 0:KVW], xT[sx][:, k, b, :], wkv2[sw][:, k, :],
                                                 start=(n == 0), stop=(n == 3 * KD - 1))
                                n += 1
                    last.then_inc(kv_ps[g], 1)

            def queries_gates(c, q):
                for g in range(NG):
                    pe.wait_ge(kv_ok[g], c + 1)
                    xT = (xhT[g], xlT[g])
                    for h in range(2):
                        n = 0
                        for k in range(KD):
                            for sx, sw in PARTS3:
                                last = pe.matmul(half(g, 1, h).rearrange("p b t -> p (b t)"),
                                                 wqg2[sw][:, k, h * C:(h + 1) * C],
                                                 xT[sx][:, k].rearrange("p b t -> p (b t)"),
                                                 start=(n == 0), stop=(n == 3 * KD - 1))
                                n += 1
                    last.then_inc(qg_ps[g], 1)

            def spread_alpha(c, q):
                for g in range(NG):
                    pe.wait_ge(ab_ok[g], c + 1)
                    for b in range(GB):
                        last = pe.transpose(half(g, 0)[:, b, :], ab[q][g][:, b, 0:1].broadcast_to([P, P]), ident)
                    last.then_inc(abc_ps[g], 1)

            def turn_keys(c, q):
                for g in range(NG):
                    pe.wait_ge(kh_ok[g], c + 1)
                    pe.wait_ge(qg_ok[g], c + 1)
                    for b in range(GB):
                        last = pe.transpose(half(g, 1)[:, b, :], kh[q][g][:, b, :], ident)
                    last.then_inc(kT_ps[g], 1)

            def system(c, q):
                for g in range(NG):
                    pe.wait_ge(kT_ok[g], c + 1)
                    pe.wait_ge(gbc_ok[g], c + 1)
                    for b in range(GB):
                        last = pe.matmul(half(g, 0)[:, b, :], kT[g][:, b, :], kT[g][:, b, :], start=True, stop=True)
                    last.then_inc(kk_ps[g], 1)

            def doubling(c, q, l, beside=None):
                for g in range(NG):
                    if l == 1:
                        pe.wait_ge(Z0_ok[g], c + 1)
                    else:
                        pe.wait_ge(Z_ok[g], (NL - 1) * c + l - 1)
                    for b in range(GB):
                        last = pe.transpose(half(g, 1)[:, b, :], Z[q][g][:, b, :], ident)
                    last.then_inc(ZT_ps[g], 1)
                if beside:
                    beside[0]()
                for g in range(NG):
                    pe.wait_ge(ZT_ok[g], (NL - 1) * c + l)
                    pe.wait_ge(moff_ok[g], (NL - 1) * c + l)
                    for b in range(GB):
                        bs = slice(b * P // 2, (b + 1) * P // 2)
                        last = pe.matmul(bank[g][0][:, bs], moff[g][:, l - 1, b, :], ZT[g][:, bs],
                                         start=True, stop=True)
                    last.then_inc(P1T_ps[g], 1)
                if beside:
                    beside[1]()
                for g in range(NG):
                    pe.wait_ge(P1T_ok[g], (NL - 1) * c + l)
                    for b in range(GB):
                        last = pe.matmul(packed(bank[g][1][:, b * P // 2:(b + 1) * P // 2], l),
                                         P1T[g][:, l - 1, b * P:(b + 1) * P], side(Z[q][g][:, b, :], l, 1),
                                         start=True, stop=True)
                    last.then_inc(Z_ps[g], 1)

            def recall(c, q):
                for g in range(NG):
                    pe.wait_ge(scaled_ok[g], c + 1)
                    pe.wait_ge(x1_ok[g], c + 1)
                    pe.wait_ge(R_ok[g], c + 1)
                    for b in range(GB):
                        pe.matmul(half(g, 2, 0)[:, b, :], kTg[q][g][:, b, :], R[g][:, b, :], start=True, stop=True)
                    for b in range(GB):
                        last = pe.transpose(half(g, 2, 1)[:, b, :], R[g][:, b, :], ident)
                    last.then_inc(kr_ps[g], 1)

            def updates(c, q):
                for g in range(NG):
                    pe.wait_ge(Z_ok[g], (NL - 1) * c + NL - 1)
                    pe.wait_ge(X0_ok[g], c + 1)
                    pe.wait_ge(XT_ok[g], c + 1)
                    for b in range(GB):
                        last = pe.matmul(half(g, 3)[:, b, :], Z[q][g][:, b, :], X0[g][:, b, :], start=True, stop=True)
                    last.then_inc(U_ps[g], 1)

            def next_state(c, q, groups=range(NG)):
                for g in groups:
                    pe.wait_ge(U_ok[g], c + 1)
                    pe.wait_ge(khd_ok[g], c + 1)
                    pe.wait_ge(S_ok[g], c + 1)
                    for b in range(GB):
                        last = pe.matmul(half(g, 2)[:, b, :], khd[q][g][:, b, :], U[g][:, b, :], start=True, stop=True)
                    last.then_inc(R_ps[g], 1)
                    for b in range(GB):
                        last = pe.transpose(half(g, 3)[:, b, :], U[g][:, b, :], ident)
                    last.then_inc(UT_ps[g], 1)

            def scores(c, q, groups=range(NG)):
                for g in groups:
                    pe.wait_ge(UT_ok[g], c + 1)
                    pe.wait_ge(R_ok[g], c + 2)
                    for b in range(GB):
                        last = pe.matmul(half(g, 2)[:, b, :], UT[g][:, b, :], qT[q][g][:, b, :], start=True, stop=True)
                    last.then_inc(sc_ps[g], 1)

            def heads(c, q, groups=range(NG)):
                for g in groups:
                    pe.wait_ge(PT_ok[g], c + 1)
                    for b in range(GB):
                        pe.matmul(half(g, 3)[:, b, :], S[g][:, b, :], qTg[q][g][:, b, :], start=True, stop=False)
                        last = pe.matmul(half(g, 3)[:, b, :], kh[q][g][:, b, :], PT[g][:, b, :], start=False, stop=True)
                    last.then_inc(OT_ps[g], 1)

            def outputs(c, q, groups=range(NG)):
                for g in groups:
                    pe.wait_ge(OT_ok[g], c + 1)
                    for b in range(GB):
                        last = pe.matmul(bank[g][2][:, b * D:(b + 1) * D], OT[g][:, b, :], wo[:, :],
                                         start=True, stop=True)
                    last.then_inc(y_ps[g], 1)

            def turn_parts(c):
                for g in range(NG):
                    pe.wait_ge(Xh_ok[g], c + 1)
                    pe.wait_ge(Xl_ok[g], c + 1)
                    bank16 = bank[g][3][:, :].bitcast(F16)
                    for s, part in enumerate((Xh, Xl)):
                        for k in range(KD):
                            for b in range(GB):
                                at = ((s * KD + k) * GB + b) * P
                                last = pe.transpose(bank16[:, at:at + P], part[g][:, b, k * P:(k + 1) * P],
                                                    ident16[:, :])
                    last.then_inc(XT_ps[g], 1)

            def turn_slots(es):
                pe.wait_ge(sll_ok, 1)
                pe.wait_ge(dve_consts, 2)
                for e in es:
                    if e >= 4:
                        pe.wait_ge(seT_ok, e - 3)
                    half16 = bank[e // 2 % 2][e % 2][:, 0:256].bitcast(F16)
                    for s, part in enumerate((sp_h, sp_l)):
                        for k in range(KD):
                            at = (s * KD + k) * P
                            last = pe.transpose(half16[:, at:at + P], part[:, e, k * P:(k + 1) * P], ident16[:, :])
                    last.then_inc(seT_ps, 1)

            def both(c, q):
                d, r = c + 1, 1 - q
                turn_x(d, r)
                recall(c, q)
                turn_parts(c)
                keys_values(d, r)
                queries_gates(d, r)
                spread_alpha(d, r)
                turn_keys(d, r)
                updates(c, q)
                system(d, r)
                next_state(c, q)
                beside = (
                    (lambda: None, lambda: scores(c, q, [0])),
                    (lambda: scores(c, q, [1]), lambda: heads(c, q, [0])),
                    (lambda: heads(c, q, [1]), lambda: None),
                    (lambda: outputs(c, q, [0]), lambda: outputs(c, q, [1])),
                    (lambda: None, lambda: None),
                    (lambda: None, lambda: None),
                )
                for l in range(1, NL):
                    doubling(d, r, l, beside[l - 1])

            turn_x(0, 0)
            pe.wait_ge(dve_consts, 6)
            pe.wait_ge(consts_in, N_CONSTS)
            keys_values(0, 0)
            queries_gates(0, 0)
            spread_alpha(0, 0)
            turn_keys(0, 0)
            system(0, 0)
            for l in range(1, NL):
                doubling(0, 0, l)
            rounds(pe, both)
            both(NCH - 2, 0)
            recall(NCH - 1, 1)
            turn_parts(NCH - 1)
            updates(NCH - 1, 1)
            turn_slots((0, 1))
            next_state(NCH - 1, 1)
            turn_slots((2, 3))
            scores(NCH - 1, 1)
            turn_slots((4, 5))
            heads(NCH - 1, 1)
            turn_slots((6, 7))
            outputs(NCH - 1, 1)
            turn_parts(NCH)

        work.close()
        with nc.Block() as clearing:
            @clearing.gpsimd
            def _(pool):
                for s in held[0::5]:
                    pool.sem_clear(s)

            @clearing.vector
            def _(dve):
                for s in held[1::5]:
                    dve.sem_clear(s)

            @clearing.scalar
            def _(act):
                for s in held[2::5]:
                    act.sem_clear(s)

            @clearing.tensor
            def _(pe):
                for s in held[3::5]:
                    pe.sem_clear(s)

            @clearing.sync
            def _(sp):
                for s in held[4::5]:
                    sp.sem_clear(s)


def moe(nc, x1_dram, X_dram, XT_dram, ident, seT, w1s, w2s, XT, out):
    with ExitStack() as ctx:
        def sb(name, shape, dt=F32):
            return ctx.enter_context(nc.sbuf_tensor("m_" + name, shape, dt))

        def two(name, shape, dt=F32):
            return [sb(f"{name}{p}", shape, dt) for p in range(2)]

        def sem(name):
            return ctx.enter_context(nc.semaphore("m_" + name))

        def sems(name):
            return [sem(f"{name}{p}") for p in range(2)]

        zero = sb("zero", [P, 1])
        L = sb("L", [P, NT, E_SLOTS])
        X = sb("X", [P, 2, NT, XS], F16)
        table = sb("table", [P, 2])
        rmax = sb("rmax", [P, 2 * NT])
        rmin = sb("rmin", [P, NT])
        nrm = sb("nrm", [P, NT])
        cmax = sb("cmax", [P, E_SLOTS])
        mcol = sb("mcol", [P, NS])
        Mb = sb("Mb", [P, E_SLOTS])
        eshift = sb("eshift", [P, 1])
        Dm = two("Dm", [P, HS])
        E = [sb(f"E{u}", [P, HS]) for u in range(4)]
        Eh = [sb(f"Eh{u}", [P, HS], F16) for u in range(4)]
        El = [sb(f"El{u}", [P, HS], F16) for u in range(4)]
        rden = sb("rden", [P, QS])
        sl = sb("sl", [P, QS, D])
        sTh = sb("sTh", [P, KD, HS], F16)
        sTl = sb("sTl", [P, KD, HS], F16)
        hf = E
        hh = sb("hh", [P, NF, HS], F16)
        hl = sb("hl", [P, NF, HS], F16)
        Ph = sb("Ph", [P, NS, XS], F16)
        Pl = sb("Pl", [P, NS, XS], F16)
        Ec = two("Ec", [P, E_SLOTS])
        Th = two("Th", [P, E_SLOTS], F16)
        Tl = two("Tl", [P, E_SLOTS], F16)
        cden = two("cden", [P, 1])
        x1t = two("x1t", [P, D])
        o = two("o", [P, D])

        wide = [ctx.enter_context(nc.psum_tensor(f"m_wide{n}", [P, 1024], F32)) for n in range(4)]
        tp = wide[0:2]
        lg = [wide[2 + u // 2][:, 512 * (u % 2):512 * (u % 2) + HS] for u in range(4)]
        cT_bank = wide[0::2]
        Mb_bank = wide[1::2]
        acc = [[wide[2 * v + q // 2][:, 512 * (q % 2):512 * (q % 2) + XW] for q in range(QS)] for v in range(2)]
        sT_bank = wide[0]
        up = [wide[1][:, 512 * p:512 * p + HS] for p in range(2)]
        down = [wide[2][:, 512 * p:512 * p + D] for p in range(2)]
        co = [wide[3][:, 512 * p:512 * p + XW] for p in range(2)]

        pc = sem("pool_consts")
        X_in, XT_in, A_dve, rm_ok, cT_ps, mc_ok, Mb_ps, Mb_ok = map(sem, (
            "X_in XT_in A_dve rm_ok cT_ps mc_ok Mb_ps Mb_ok").split())
        cm_ok = sem("cm_ok")
        rmin_ok = sem("rmin_ok")
        rd_ok, sl_ok, sT_ps, sTh_ok, sTl_ok = map(sem, "rd_ok sl_ok sT_ps sTh_ok sTl_ok".split())
        (lg_ps, L_ok, D_ok, E_ok, Eh_ok, El_ok, B_ps, up_ps, hf_ok, hh_ok, hl_ok, dn_ps, Ph_ok, Pl_ok,
         Ec_ok, tp_ps, Th_ok, Tl_ok, co_ps, cd_ok, o_ok, o_out, x1_in) = [sems(x) for x in (
             "lg_ps L_ok D_ok E_ok Eh_ok El_ok B_ps up_ps hf_ok hh_ok hl_ok dn_ps Ph_ok Pl_ok "
             "Ec_ok tp_ps Th_ok Tl_ok co_ps cd_ok o_ok o_out x1_in").split()]
        HB = NT // 2
        block = ctx.enter_context(nc.Block())

        @block.sync
        def _(sp):
            for p in range(2):
                sp.sem_inc(o_out[p], 16)

            def load_XT(b):
                sp.dma_start(XT[:, :, :], XT_dram[:, :, bass.ds(b, 1), :].rearrange("q k b t -> q k (b t)"))\
                    .then_inc(XT_in, 16)

            def load_X(b):
                sp.wait_ge(pc, 1)
                with sp.Fori(0, NT) as j:
                    for s in range(2):
                        sp.dma_start(X[:, s, bass.ds(j, 1), 0:D].rearrange("q a d -> q (a d)"),
                                     X_dram[s, bass.ds(b, 1), bass.ds(j * P, P), :]
                                     .rearrange("b q d -> (b q) d")).then_inc(X_in, 16)

            def results(b):
                with sp.Fori(0, HB) as h:
                    n = sp.snap(b * HB + h + 1)
                    for p in range(2):
                        sp.wait_ge(o_ok[p], n)
                        sp.dma_start(x1t[p][:, :], x1_dram[bass.ds(b, 1), bass.ds(h * 2 * P + p * P, P), :]
                                     .rearrange("b q d -> (b q) d")).then_inc(x1_in[p], 16)
                    for p in range(2):
                        sp.wait_ge(o_ok[p], n + 1)
                        sp.dma_start(out[bass.ds(b, 1), bass.ds(h * 2 * P + p * P, P), :]
                                     .rearrange("b q d -> (b q) d"), o[p][:, :]).then_inc(o_out[p], 16)

            sp.sem_inc(XT_in, 16)
            load_X(0)
            with sp.Fori(0, B - 1) as b:
                sp.wait_ge(cT_ps, 2 * b + 2)
                load_XT(b + 1)
                done = sp.snap(sp.to_reg((2 * b + 2) * HB + 2))
                sp.wait_ge(pc, 1)
                sp.wait_ge(B_ps[1], done)
                load_X(b + 1)
                results(b)
            results(B - 1)
            for p in range(2):
                sp.wait_ge(o_out[p], 16 * B * HB + 16)

        @block.gpsimd
        def _(pool):
            pool.memset(zero[:, :], 0.0)
            pool.memset(eshift[:, :], ESHIFT)
            for s in range(2):
                pool.memset(X[:, s, :, D:], 1.0 - s)
            pool.memset(Ph[:, :, D:], WSCALE)
            pool.memset(Pl[:, :, D:], 0.0).then_inc(pc, 1)

        @block.vector
        def _(dve):
            for p in range(2):
                dve.sem_inc(El_ok[p], 2)
                dve.sem_inc(hl_ok[p], 2)
                dve.sem_inc(Pl_ok[p], 1)
                dve.sem_inc(Tl_ok[p], 1)
                dve.sem_inc(o_ok[p], 1)

            with dve.Fori(0, B) as b:
                nb = dve.snap(b + 1)
                dve.memset(cmax[:, :], -3.0e38).then_inc(cm_ok, 1)

                def maxima(z, g, t):
                    tile, half_at = 4 * g + t, slice(z * HS, (z + 1) * HS)
                    dve.wait_ge(L_ok[t % 2], (2 * b + z) * HB + 2 * g + t // 2 + 3)
                    dve.wait_ge(cm_ok, 2 * NT * b + nb + z * NT + tile)
                    dve.tensor_tensor(cmax[:, half_at], cmax[:, half_at], L[:, bass.ds(tile, 1), half_at]
                                      .rearrange("q a n -> q (a n)"), ALU.max).then_inc(cm_ok, 1)
                    dve.tensor_reduce(rmax[:, bass.ds(z * NT + tile, 1)], L[:, bass.ds(tile, 1), half_at]
                                      .rearrange("q a n -> q (a n)"), AX.X, ALU.max, negate=True)\
                        .then_inc(rm_ok, 1)

                def column_maxima(z):
                    dve.wait_ge(cT_ps, 2 * b + z + 1)
                    dve.tensor_reduce(mcol[:, z * QS:(z + 1) * QS], cT_bank[z][:, 0:HS]
                                      .rearrange("q (e t) -> q e t", t=P), AX.X, ALU.max).then_inc(mc_ok, 1)

                def shifted(v, g, t):
                    p, s = t % 2, 2 * b + v
                    dve.wait_ge(E_ok[p], s * HB + 2 * g + t // 2 + 1)
                    dve.tensor_tensor(Dm[p][:, :],
                                      L[:, bass.ds(4 * g + t, 1), v * HS:(v + 1) * HS]
                                      .rearrange("q a n -> q (a n)"),
                                      Mb[:, v * HS:(v + 1) * HS], ALU.subtract).then_inc(D_ok[p], 1)

                def low(v, g, t):
                    p, s = t % 2, 2 * b + v
                    dve.wait_ge(Eh_ok[p], s * HB + 2 * g + t // 2 + 1)
                    dve.tensor_tensor(El[t % 4][:, :], E[t % 4][:, :], Eh[t % 4][:, :], ALU.subtract)\
                        .then_inc(El_ok[p], 1)

                def slots_out(v, qs):
                    s = 2 * b + v
                    dve.wait_ge(B_ps[1], (s + 1) * HB + 2)
                    for q in qs:
                        last = dve.reciprocal(rden[:, q:q + 1], acc[v][q][:, D:D + 1])
                    last.then_inc(rd_ok, len(qs))
                    dve.wait_ge(rd_ok, s * QS + qs[-1] + 1)
                    if v == 1:
                        dve.wait_ge(sT_ps, s)
                    for q in qs:
                        last = dve.tensor_scalar(sl[:, q, :], acc[v][q][:, 0:D], rden[:, q:q + 1], None, ALU.mult)
                    last.then_inc(sl_ok, len(qs))

                def slots_low(v):
                    dve.wait_ge(sTh_ok, 2 * b + v + 1)
                    dve.tensor_tensor(sTl[:, :, :].rearrange("q k n -> q (k n)"), sT_bank[:, :],
                                      sTh[:, :, :].rearrange("q k n -> q (k n)"), ALU.subtract).then_inc(sTl_ok, 1)

                def hidden_low(v):
                    for f in range(NF):
                        dve.wait_ge(hh_ok[f % 2], (2 * b + v) * (NF // 2) + f // 2 + 1)
                        dve.tensor_tensor(hl[:, f, :], hf[f % 4][:, :], hh[:, f, :], ALU.subtract)\
                            .then_inc(hl_ok[f % 2], 1)

                def processed_low(v):
                    for q in range(QS):
                        dve.wait_ge(Ph_ok[q % 2], (2 * b + v) * (QS // 2) + q // 2 + 1)
                        dve.tensor_tensor(Pl[:, v * QS + q, 0:D], down[q % 2], Ph[:, v * QS + q, 0:D],
                                          ALU.subtract).then_inc(Pl_ok[q % 2], 1)

                with dve.Fori(0, NT // 4) as g:
                    for t in range(4):
                        maxima(0, g, t)
                for t in range(4):
                    maxima(1, 0, t)
                    if t == 1:
                        column_maxima(0)
                dve.wait_ge(Mb_ok, 2 * b + 1)
                for t in range(2):
                    shifted(0, 0, t)
                with dve.Fori(0, NT // 4 - 2) as g:
                    for t in range(4):
                        maxima(1, g + 1, t)
                for t in range(NT - 4, NT):
                    maxima(1, 0, t)
                    if NT - 4 < t < NT - 1:
                        low(0, 0, t - NT + 3)
                        shifted(0, 0, t - NT + 5)

                for v in range(2):
                    if v == 0:
                        for t in range(2, 4):
                            shifted(0, 0, t + 2)
                            low(0, 0, t)
                    else:
                        dve.wait_ge(Mb_ok, 2 * b + 2)
                        for t in range(2):
                            shifted(1, 0, t)
                    first = 1 - v
                    with dve.Fori(0, 2) as g:
                        for t in range(4):
                            shifted(v, g + first, t + 2)
                            low(v, g + first, t)
                    loops = 2 + first
                    for t in range(4 * loops, NT):
                        if t + 2 < NT:
                            shifted(v, 0, t + 2)
                        low(v, 0, t)
                        if v == 0 and t == 4 * loops:
                            column_maxima(1)
                        if v == 0 and t == NT - 2:
                            dve.wait_ge(rm_ok, 2 * NT * nb)
                            dve.tensor_tensor(rmin[:, :], rmax[:, 0:NT], rmax[:, NT:], ALU.min).then_inc(rmin_ok, 1)
                        if v == 0 and t == NT - 1:
                            dve.wait_ge(rmin_ok, nb)
                            dve.tensor_scalar(nrm[:, :], rmin[:, :], ESHIFT, None, ALU.add).then_inc(A_dve, 1)
                        if v == 1 and t < 4 * loops + QS:
                            slots_out(0, [t - 4 * loops])
                slots_low(0)
                slots_out(1, range(QS))
                hidden_low(0)
                slots_low(1)
                processed_low(0)
                hidden_low(1)

                def low_weights(h, p):
                    n = b * HB + h + 1
                    dve.wait_ge(Th_ok[p], n)
                    dve.tensor_tensor(Tl[p][:, :], tp[p][:, :], Th[p][:, :], ALU.subtract).then_inc(Tl_ok[p], 1)

                def finish(h, p):
                    n = b * HB + h + 1
                    dve.wait_ge(co_ps[p], n)
                    dve.reciprocal(cden[p][:, :], co[p][:, D:D + 1]).then_inc(cd_ok[p], 1)
                    dve.wait_ge(cd_ok[p], n)
                    dve.wait_ge(x1_in[p], 16 * n)
                    dve.wait_ge(o_out[p], 16 * n)
                    dve.scalar_tensor_tensor(o[p][:, :], co[p][:, 0:D], cden[p][:, 0:1], x1t[p][:, :],
                                             ALU.mult, ALU.add).then_inc(o_ok[p], 1)

                low_weights(0, 0)
                processed_low(1)
                low_weights(0, 1)
                with dve.Fori(0, HB - 1) as h:
                    for p in range(2):
                        finish(h, p)
                        low_weights(h + 1, p)
                for p in range(2):
                    finish(HB - 1, p)

        @block.scalar
        def _(act):
            act.wait_ge(pc, 1)
            for p in range(2):
                act.sem_inc(L_ok[p], 2)
                act.sem_inc(E_ok[p], 1)
            with act.Fori(0, B) as b:
                nb = act.snap(b + 1)

                def logits_out(z, g, t):
                    n = act.snap((2 * b + z) * HB + 2 * g + t // 2 + 1)
                    act.wait_ge(pc, 1)
                    act.wait_ge(lg_ps[t % 2], n)
                    act.copy(L[:, bass.ds(4 * g + t, 1), z * HS:(z + 1) * HS].rearrange("q a n -> q (a n)"),
                             lg[t % 4]).then_inc(L_ok[t % 2], 1)

                def maxima_out(z):
                    act.wait_ge(Mb_ps, 2 * b + z + 1)
                    act.copy(Mb[:, z * HS:(z + 1) * HS], Mb_bank[z][:, 0:HS]).then_inc(Mb_ok, 1)

                def exps(v, g, t):
                    p, s = t % 2, 2 * b + v
                    n = s * HB + 2 * g + t // 2 + 1
                    act.wait_ge(D_ok[p], n)
                    act.wait_ge(El_ok[p], n)
                    act.activation(E[t % 4][:, :], Dm[p][:, :], ACT.Exp, bias=eshift[:, 0:1]).then_inc(E_ok[p], 1)

                def high_exps(v, g, t):
                    p, s = t % 2, 2 * b + v
                    n = s * HB + 2 * g + t // 2 + 1
                    act.wait_ge(E_ok[p], n + 1)
                    act.wait_ge(B_ps[p], n)
                    act.copy(Eh[t % 4][:, :], E[t % 4][:, :]).then_inc(Eh_ok[p], 1)

                def slots_high(v):
                    act.wait_ge(sT_ps, 2 * b + v + 1)
                    act.copy(sTh[:, :, :].rearrange("q k n -> q (k n)"), sT_bank[:, :]).then_inc(sTh_ok, 1)

                def hidden(v, f):
                    n = (2 * b + v) * (NF // 2) + f // 2 + 1
                    act.wait_ge(up_ps[f % 2], n)
                    act.wait_ge(hl_ok[f % 2], n)
                    act.activation(hf[f % 4][:, :], up[f % 2], ACT.Gelu, scale=1.0 / WSCALE)\
                        .then_inc(hf_ok[f % 2], 1)

                def hidden_high(v):
                    for p in range(2):
                        act.wait_ge(El_ok[p], (2 * b + 2) * HB + 2)
                    hidden(v, 0)
                    for f in range(NF):
                        if f + 1 < NF:
                            hidden(v, f + 1)
                        act.wait_ge(hf_ok[f % 2], (2 * b + v) * (NF // 2) + f // 2 + 1)
                        act.copy(hh[:, f, :], hf[f % 4][:, :]).then_inc(hh_ok[f % 2], 1)

                def processed_high(v):
                    for q in range(QS):
                        act.wait_ge(dn_ps[q % 2], (2 * b + v) * (QS // 2) + q // 2 + 1)
                        act.copy(Ph[:, v * QS + q, 0:D], down[q % 2]).then_inc(Ph_ok[q % 2], 1)

                def weights(h, p):
                    n = act.snap(b * HB + h + 1)
                    act.wait_ge(pc, 1)
                    act.wait_ge(tp_ps[p], n)
                    act.activation(Ec[p][:, :], L[:, bass.ds(2 * h + p, 1), :].rearrange("q a n -> q (a n)"),
                                   ACT.Exp, bias=nrm[:, bass.ds(2 * h + p, 1)]).then_inc(Ec_ok[p], 1)

                def high(h, p):
                    n = b * HB + h + 1
                    act.wait_ge(tp_ps[p], n + 1)
                    act.copy(Th[p][:, :], tp[p][:, :]).then_inc(Th_ok[p], 1)

                with act.Fori(0, NT // 4) as g:
                    for t in range(4):
                        logits_out(0, g, t)
                for t in range(4):
                    logits_out(1, 0, t)
                act.activation(table[:, 0:1], zero[:, :], ACT.Exp)
                maxima_out(0)
                with act.Fori(0, NT // 4 - 2) as g:
                    for t in range(4):
                        logits_out(1, g + 1, t)
                for t in range(NT - 4, NT):
                    logits_out(1, 0, t)
                    if t < NT - 2:
                        exps(0, 0, t - NT + 4)
                    if NT - 4 < t < NT - 1:
                        high_exps(0, 0, t - NT + 3)

                for v in range(2):
                    if v == 0:
                        exps(0, 0, 2)
                        for t in range(2, 4):
                            exps(0, 0, t + 1)
                            high_exps(0, 0, t)
                    else:
                        maxima_out(1)
                        exps(1, 0, 0)
                    first = 1 - v
                    loops = NT // 4 - 1 - first
                    with act.Fori(0, loops) as g:
                        for t in range(4):
                            exps(v, g + first, t + 1)
                            high_exps(v, g + first, t)
                    for t in range(NT - 4, NT):
                        if t + 1 < NT:
                            exps(v, 0, t + 1)
                        high_exps(v, 0, t)
                slots_high(0)
                act.wait_ge(A_dve, nb)
                weights(0, 0)
                hidden_high(0)
                slots_high(1)
                processed_high(0)
                hidden_high(1)
                high(0, 0)
                act.activation(table[:, 1:2], zero[:, :], ACT.Exp)
                weights(0, 1)
                processed_high(1)
                with act.Fori(0, HB - 1) as h:
                    for p in range(2):
                        weights(h + 1, p)
                        high(h + p, 1 - p)
                high(HB - 1, 1)

        @block.tensor
        def _(pe):
            pe.wait_ge(pc, 1)
            for p in range(2):
                pe.sem_inc(B_ps[p], 2)
                pe.sem_inc(tp_ps[p], 1)
            with pe.Fori(0, B) as b:
                nb = pe.snap(b + 1)
                pe.wait_ge(XT_in, 16 * nb)

                def logits(z, g, t):
                    pe.wait_ge(L_ok[t % 2], (2 * b + z) * HB + 2 * g + t // 2 + 1)
                    c = 0
                    for k in range(KD):
                        for sx, ss in PARTS3:
                            last = pe.matmul(lg[t % 4], XT[:, sx * KD + k, bass.ds((4 * g + t) * P, P)],
                                             seT[:, ss, k, z * HS:(z + 1) * HS],
                                             start=(c == 0), stop=(c == 3 * KD - 1))
                            c += 1
                    last.then_inc(lg_ps[t % 2], 1)

                def turn_maxima(z):
                    pe.wait_ge(cm_ok, 2 * NT * b + nb + (z + 1) * NT)
                    for e in range(QS):
                        at = z * HS + e * P
                        last = pe.transpose(cT_bank[z][:, e * P:(e + 1) * P], cmax[:, at:at + P], ident[:, :])
                    last.then_inc(cT_ps, 1)

                def spread_maxima(z):
                    pe.wait_ge(mc_ok, 2 * b + z + 1)
                    for e in range(QS):
                        last = pe.transpose(Mb_bank[z][:, e * P:(e + 1) * P],
                                            mcol[:, z * QS + e:z * QS + e + 1].broadcast_to([P, P]), ident[:, :])
                    last.then_inc(Mb_ps, 1)

                for t in range(4):
                    if t == 2:
                        for p in range(2):
                            pe.wait_ge(o_ok[p], HB * b + 1)
                    logits(0, 0, t)
                with pe.Fori(0, NT // 4 - 1) as g:
                    for t in range(4):
                        logits(0, g + 1, t)
                for t in range(4):
                    logits(1, 0, t)
                    if t == 1:
                        for p in range(2):
                            pe.wait_ge(Tl_ok[p], HB * b + 1)
                        turn_maxima(0)
                spread_maxima(0)
                with pe.Fori(0, NT // 4 - 1) as g:
                    for t in range(4):
                        logits(1, g + 1, t)

                def dispatch(v, g, t, first=False):
                    p = t % 2
                    pe.wait_ge(El_ok[p], (2 * b + v) * HB + 2 * g + t // 2 + 3)
                    for q in range(QS):
                        qs = slice(q * P, (q + 1) * P)
                        for e, sx in ((Eh, 0), (Eh, 1), (El, 0)):
                            last = pe.matmul(acc[v][q], e[t % 4][:, qs],
                                             X[:, sx, bass.ds(4 * g + t, 1), 0:XW].rearrange("q a n -> q (a n)"),
                                             start=first and e is Eh and sx == 0,
                                             stop=t == NT - 1 and e is El)
                    last.then_inc(B_ps[p], 1)

                def turn_slots(v):
                    pe.wait_ge(sl_ok, (2 * b + v + 1) * QS)
                    for k in range(KD):
                        for q in range(QS):
                            last = pe.transpose(sT_bank[:, (k * QS + q) * P:(k * QS + q + 1) * P],
                                                sl[:, q, k * P:(k + 1) * P], ident[:, :])
                    last.then_inc(sT_ps, 1)

                sT = (sTh, sTl)
                hT = (hh, hl)

                def hidden(v):
                    s = 2 * b + v
                    pe.wait_ge(sTl_ok, s + 1)
                    for f in range(NF):
                        if v == 1 or f >= 2:
                            pe.wait_ge(hf_ok[f % 2], s * (NF // 2) + f // 2)
                        c = 0
                        for k in range(KD):
                            for sw, ss in PARTS3:
                                last = pe.matmul(up[f % 2], w1s[:, sw, k, f * P:(f + 1) * P], sT[ss][:, k, :],
                                                 start=(c == 0), stop=(c == 3 * KD - 1))
                                c += 1
                        last.then_inc(up_ps[f % 2], 1)

                def processed(v):
                    s = 2 * b + v
                    for q in range(QS):
                        pe.wait_ge(Pl_ok[q % 2], s * (QS // 2) + q // 2 + 1)
                        c = 0
                        for f in range(NF):
                            if q == 0:
                                pe.wait_ge(hl_ok[f % 2], s * (NF // 2) + f // 2 + 3)
                            for sh, sw in PARTS3:
                                last = pe.matmul(down[q % 2], hT[sh][:, f, q * P:(q + 1) * P], w2s[:, sw, f, :],
                                                 start=(c == 0), stop=(c == 3 * NF - 1))
                                c += 1
                        last.then_inc(dn_ps[q % 2], 1)

                def turn(h, p):
                    n = b * HB + h + 1
                    pe.wait_ge(Ec_ok[p], n)
                    pe.wait_ge(Tl_ok[p], n)
                    for e in range(NS):
                        last = pe.transpose(tp[p][:, e * P:(e + 1) * P], Ec[p][:, e * P:(e + 1) * P], ident[:, :])
                    last.then_inc(tp_ps[p], 1)

                def combine(h, p):
                    n = b * HB + h + 1
                    pe.wait_ge(Tl_ok[p], n + 1)
                    pe.wait_ge(o_ok[p], n)
                    c = 0
                    for e in range(NS):
                        es = slice(e * P, (e + 1) * P)
                        for a, pp in ((Th, Ph), (Th, Pl), (Tl, Ph)):
                            last = pe.matmul(co[p], a[p][:, es], pp[:, e, 0:XW], start=(c == 0),
                                             stop=(c == 3 * NS - 1))
                            c += 1
                    last.then_inc(co_ps[p], 1)

                arrived = pe.snap(pe.to_reg(32 * NT * nb))
                pe.wait_ge(pc, 1)
                pe.wait_ge(X_in, arrived)
                pe.wait_ge(Mb_ok, 2 * b + 1)
                for t in range(4):
                    dispatch(0, 0, t, first=t == 0)
                turn_maxima(1)
                with pe.Fori(0, NT // 4 - 2) as g:
                    for t in range(4):
                        dispatch(0, g + 1, t)
                for t in range(NT - 4, NT):
                    dispatch(0, 0, t)
                    if t == NT - 4:
                        spread_maxima(1)
                pe.wait_ge(Mb_ok, 2 * b + 2)
                for t in range(4):
                    dispatch(1, 0, t, first=t == 0)
                with pe.Fori(0, NT // 4 - 2) as g:
                    for t in range(4):
                        dispatch(1, g + 1, t)
                for t in range(NT - 4, NT):
                    if t == NT - 2:
                        turn_slots(0)
                    dispatch(1, 0, t)
                hidden(0)
                turn_slots(1)
                processed(0)
                hidden(1)
                turn(0, 0)
                processed(1)
                turn(0, 1)
                cut_to = pe.snap(pe.to_reg(nb * QS + 1))
                pe.wait_ge(pc, 1)
                for p in range(2):
                    pe.wait_ge(Pl_ok[p], cut_to)
                with pe.Fori(0, HB - 1) as h:
                    for p in range(2):
                        combine(h, p)
                        turn(h + 1, p)
                for p in range(2):
                    combine(HB - 1, p)


def build(nc, io, out):
    with ExitStack() as ctx:
        x1_dram = nc.dram_tensor("x1_dram", (B, T, D), F32, kind="Internal").ap()
        X_dram = nc.dram_tensor("X_dram", (2, B, T, D), F16, kind="Internal").ap()
        XT_dram = nc.dram_tensor("XT_dram", (P, 2 * KD, B, T), F16, kind="Internal").ap()

        def sb(name, shape, dt=F32):
            return ctx.enter_context(nc.sbuf_tensor(name, shape, dt))

        ident = sb("ident", [P, P])
        ident16 = sb("ident16", [P, P], F16)
        seT = sb("seT", [P, 2, KD, E_SLOTS], F16)
        w1s = sb("w1s", [P, 2, KD, HID], F16)
        w2s = sb("w2s", [P, 2, NF, D], F16)
        XT = sb("XT", [P, 2 * KD, T], F16)
        attention(nc, io, x1_dram, X_dram, XT_dram, ident, ident16, seT, w1s, w2s, XT)
        moe(nc, x1_dram, X_dram, XT_dram, ident, seT, w1s, w2s, XT, out)


_INS = ["L0_attn_x", "L0_attn_Wq", "L0_attn_bq", "L0_attn_Wk", "L0_attn_bk", "L0_attn_Wv", "L0_attn_bv",
        "L0_attn_Wa", "L0_attn_ba", "L0_attn_Wb", "L0_attn_bb", "L0_attn_Wg", "L0_attn_bg", "L0_attn_Wo",
        "L0_attn_bo", "L0_ffn_gamma_x", "L0_ffn_gamma_slot", "L0_ffn_slot_embeds", "L0_ffn_w1", "L0_ffn_w2"]


def kernel(**inputs):
    import numpy as _np
    import concourse.bacc as _bacc
    from concourse import mybir as _mybir
    from concourse.bass_utils import run_bass_kernel_spmd as _run

    nc = _bacc.Bacc("TRN2", target_bir_lowering=False, num_devices=1)
    arrays, io = {}, {}
    for name in _INS + ["const"]:
        a = _np.ascontiguousarray(constants() if name == "const" else inputs[name])
        arrays[f"in_{name}_dram"] = a
        io[name] = nc.dram_tensor(f"in_{name}_dram", a.shape, _mybir.dt.from_np(a.dtype), kind="ExternalInput").ap()
    out = nc.dram_tensor("out_0_dram", (B, T, D), F32, kind="ExternalOutput").ap()
    build(nc, io, out)
    r = _run(nc, [arrays], core_ids=[0])
    return r.results[0]["out_0_dram"]
```
